# Optimizing a Trainium2 kernel written in Bass

```python
import numpy as np
import jax
import jax.numpy as jnp

def _softmax(x, axis=-1):
    return jax.nn.softmax(x, axis=axis)
def _gelu(x):
    return jax.nn.gelu(x, approximate=True)
def _silu(x):
    return jax.nn.silu(x)
def _sigmoid(x):
    return jax.nn.sigmoid(x)
def _layernorm(x, axis=-1, eps=1e-5):
    m = jnp.mean(x, axis=axis, keepdims=True)
    v = jnp.var(x, axis=axis, keepdims=True)
    return (x - m) / jnp.sqrt(v + eps)
def _scatter_add(tgt, idx, src, axis=0):
    return tgt.at[idx].add(src)
def _segment_sum(src, seg, n):
    return jax.ops.segment_sum(src, seg, n)

kernel_name = 'mk_conv_attn_hybrid_d2_conv_nhwc256_4ee73b'

def setup_inputs(seed: int = 0):
    np.random.seed(seed)
    _w = jnp.asarray
    def _rec_inputs():
        import jax
        import jax.numpy as jnp
        _gk = jax.random.key(seed)
        x = -0.0005207 + 1.001 * jax.random.normal(jax.random.fold_in(_gk, 1), (2, 64, 64, 256), jnp.float32)
        return x
    x = _rec_inputs()
    def _L0_conv_setup():
        import jax, jax.numpy as jnp
        import numpy as np
        KSIZE = 7
        HEAD_DIM = 64
        EPS = 1e-06

        def rmsnorm(x, w):
            return x * jax.lax.rsqrt(jnp.mean(x * x, axis=-1, keepdims=True) + EPS) * w

        def rope2d(x):
            B, H, W, C = x.shape
            half = C // 2
            q = half // 2
            inv = 1.0 / 10000.0 ** (jnp.arange(q, dtype=jnp.float32) / q)
            th_y = jnp.arange(H, dtype=jnp.float32)[:, None] * inv
            th_x = jnp.arange(W, dtype=jnp.float32)[:, None] * inv

            def rot(v, th):
                c, s = (jnp.cos(th), jnp.sin(th))
                a, b = (v[..., 0], v[..., 1])
                return jnp.stack([a * c - b * s, a * s + b * c], axis=-1)
            xy = rot(x[..., :half].reshape(B, H, W, q, 2), th_y[None, :, None, :])
            xx = rot(x[..., half:].reshape(B, H, W, q, 2), th_x[None, None, :, :])
            return jnp.concatenate([xy.reshape(B, H, W, half), xx.reshape(B, H, W, half)], axis=-1)

        def neighborhood_attn(x, w_qkv, w_proj, b_proj, k=KSIZE, hd=HEAD_DIM):
            B, H, W, C = x.shape
            nh = C // hd
            qkv = x @ w_qkv
            qv, kv, vv = jnp.split(qkv, 3, axis=-1)
            qh = qv.reshape(B, H, W, nh, hd)
            kh = kv.reshape(B, H, W, nh, hd)
            vh = vv.reshape(B, H, W, nh, hd)
            idx_h = jnp.clip(jnp.arange(H) - k // 2, 0, H - k)[:, None] + jnp.arange(k)
            idx_w = jnp.clip(jnp.arange(W) - k // 2, 0, W - k)[:, None] + jnp.arange(k)

            def gather(t):
                g = t[:, idx_h]
                g = g[:, :, :, idx_w]
                return g.transpose(0, 1, 3, 5, 2, 4, 6).reshape(B, H, W, nh, k * k, hd)
            kn = gather(kh)
            vn = gather(vh)
            scale = 1.0 / np.sqrt(hd).astype(np.float32)
            logits = jnp.einsum('bxynd,bxynkd->bxynk', qh, kn) * scale
            attn = jax.nn.softmax(logits, axis=-1)
            out = jnp.einsum('bxynk,bxynkd->bxynd', attn, vn).reshape(B, H, W, C)
            return out @ w_proj + b_proj

        def geglu(x, ff1_w, ff1_b, ff2_w, ff2_b):
            h = x @ ff1_w + ff1_b
            gate, value = jnp.split(h, 2, axis=-1)
            return jax.nn.gelu(gate, approximate=False) * value @ ff2_w + ff2_b
        key = jax.random.key(seed)
        B, H, W, C = (2, 64, 64, 256)
        ks = jax.random.split(key, 8)
        g = lambda k, shape, sc: jax.random.normal(k, shape, jnp.float32) * sc
        return {'x': g(ks[0], (B, H, W, C), 1.0), 'norm1_w': jnp.ones((C,), jnp.float32), 'norm2_w': jnp.ones((C,), jnp.float32), 'w_qkv': g(ks[1], (C, 3 * C), 0.02), 'w_proj': g(ks[2], (C, C), 0.02), 'b_proj': g(ks[3], (C,), 0.02), 'ff1_w': g(ks[4], (C, 2 * C), 0.02), 'ff1_b': g(ks[5], (2 * C,), 0.02), 'ff2_w': g(ks[6], (C, C), 0.02), 'ff2_b': g(ks[7], (C,), 0.02)}
    _L0_conv_all = _L0_conv_setup()
    _L0_conv_in = {k: v for k, v in _L0_conv_all.items() if k in ('norm1_w', 'norm2_w', 'w_qkv', 'w_proj', 'b_proj', 'ff1_w', 'ff1_b', 'ff2_w', 'ff2_b', )}
    del _L0_conv_all

    def _L1_attn_setup():
        import jax, jax.numpy as jnp
        import numpy as np
        NUM_HEADS = 4
        LN_EPS = 1e-05

        def positional_encoding(length, d_model):
            pos = jnp.arange(length, dtype=jnp.float32)[:, None]
            div = jnp.exp(jnp.arange(0, d_model, 2, dtype=jnp.float32) * (-np.log(10000.0) / d_model))
            pe = jnp.zeros((length, d_model), dtype=jnp.float32)
            pe = pe.at[:, 0::2].set(jnp.sin(pos * div))
            pe = pe.at[:, 1::2].set(jnp.cos(pos * div))
            return pe

        def rel_shift(pos_score):
            B, H, S, _ = pos_score.shape
            padded = jnp.pad(pos_score, ((0, 0), (0, 0), (0, 0), (1, 0)))
            padded = padded.reshape(B, H, S + 1, S)
            return padded[:, :, 1:].reshape(B, H, S, S)
        key = jax.random.key(seed)
        ks = jax.random.split(key, 8)
        B, S, D, H = (8, 2048, 256, NUM_HEADS)
        dh = D // H
        s = 0.02
        return {'inputs': jax.random.normal(ks[0], (B, S, D), dtype=jnp.float32), 'ln_gamma': jnp.ones((D,), jnp.float32), 'ln_beta': jnp.zeros((D,), jnp.float32), 'Wq': jax.random.normal(ks[1], (D, D), jnp.float32) * s, 'bq': jnp.zeros((D,), jnp.float32), 'Wk': jax.random.normal(ks[2], (D, D), jnp.float32) * s, 'bk': jnp.zeros((D,), jnp.float32), 'Wv': jax.random.normal(ks[3], (D, D), jnp.float32) * s, 'bv': jnp.zeros((D,), jnp.float32), 'Wpos': jax.random.normal(ks[4], (D, D), jnp.float32) * s, 'u_bias': jax.random.normal(ks[5], (H, dh), jnp.float32) * s, 'v_bias': jax.random.normal(ks[6], (H, dh), jnp.float32) * s, 'Wout': jax.random.normal(ks[7], (D, D), jnp.float32) * s, 'bout': jnp.zeros((D,), jnp.float32)}
    _L1_attn_all = _L1_attn_setup()
    _L1_attn_in = {k: v for k, v in _L1_attn_all.items() if k in ('ln_gamma', 'ln_beta', 'Wq', 'bq', 'Wk', 'bk', 'Wv', 'bv', 'Wpos', 'u_bias', 'v_bias', 'Wout', 'bout', )}
    del _L1_attn_all

    def _L1_ffn_setup():
        import jax, jax.numpy as jnp
        import numpy as np
        B, S, D = (8, 4096, 256)
        H = 4 * D
        CAPACITY = 0.5
        key = jax.random.key(seed)
        ks = jax.random.split(key, 6)
        x = jax.random.normal(ks[0], (B, S, D), dtype=jnp.float32)
        attention_mask = jnp.zeros((B, 1, 1, S), dtype=jnp.float32)
        wr = jax.random.normal(ks[1], (D, 1), dtype=jnp.float32) * 0.02
        br = jnp.zeros((1,), dtype=jnp.float32)
        w1 = jax.random.normal(ks[2], (D, H), dtype=jnp.float32) * 0.02
        b1 = jnp.zeros((H,), dtype=jnp.float32)
        w2 = jax.random.normal(ks[3], (H, D), dtype=jnp.float32) * 0.02
        b2 = jnp.zeros((D,), dtype=jnp.float32)
        return {'x': x, 'attention_mask': attention_mask, 'wr': wr, 'br': br, 'w1': w1, 'b1': b1, 'w2': w2, 'b2': b2}
    _L1_ffn_all = _L1_ffn_setup()
    _L1_ffn_in = {k: v for k, v in _L1_ffn_all.items() if k in ('attention_mask', 'wr', 'br', 'w1', 'b1', 'w2', 'b2', )}
    del _L1_ffn_all

    return {
        "x": x,
        "L0_conv_norm1_w": _L0_conv_in["norm1_w"],
        "L0_conv_norm2_w": _L0_conv_in["norm2_w"],
        "L0_conv_w_qkv": _L0_conv_in["w_qkv"],
        "L0_conv_w_proj": _L0_conv_in["w_proj"],
        "L0_conv_b_proj": _L0_conv_in["b_proj"],
        "L0_conv_ff1_w": _L0_conv_in["ff1_w"],
        "L0_conv_ff1_b": _L0_conv_in["ff1_b"],
        "L0_conv_ff2_w": _L0_conv_in["ff2_w"],
        "L0_conv_ff2_b": _L0_conv_in["ff2_b"],
        "L1_attn_ln_gamma": _L1_attn_in["ln_gamma"],
        "L1_attn_ln_beta": _L1_attn_in["ln_beta"],
        "L1_attn_Wq": _L1_attn_in["Wq"],
        "L1_attn_bq": _L1_attn_in["bq"],
        "L1_attn_Wk": _L1_attn_in["Wk"],
        "L1_attn_bk": _L1_attn_in["bk"],
        "L1_attn_Wv": _L1_attn_in["Wv"],
        "L1_attn_bv": _L1_attn_in["bv"],
        "L1_attn_Wpos": _L1_attn_in["Wpos"],
        "L1_attn_u_bias": _L1_attn_in["u_bias"],
        "L1_attn_v_bias": _L1_attn_in["v_bias"],
        "L1_attn_Wout": _L1_attn_in["Wout"],
        "L1_attn_bout": _L1_attn_in["bout"],
        "L1_ffn_attention_mask": _L1_ffn_in["attention_mask"],
        "L1_ffn_wr": _L1_ffn_in["wr"],
        "L1_ffn_br": _L1_ffn_in["br"],
        "L1_ffn_w1": _L1_ffn_in["w1"],
        "L1_ffn_b1": _L1_ffn_in["b1"],
        "L1_ffn_w2": _L1_ffn_in["w2"],
        "L1_ffn_b2": _L1_ffn_in["b2"],
    }

def reference(x, L0_conv_norm1_w, L0_conv_norm2_w, L0_conv_w_qkv, L0_conv_w_proj, L0_conv_b_proj, L0_conv_ff1_w, L0_conv_ff1_b, L0_conv_ff2_w, L0_conv_ff2_b, L1_attn_ln_gamma, L1_attn_ln_beta, L1_attn_Wq, L1_attn_bq, L1_attn_Wk, L1_attn_bk, L1_attn_Wv, L1_attn_bv, L1_attn_Wpos, L1_attn_u_bias, L1_attn_v_bias, L1_attn_Wout, L1_attn_bout, L1_ffn_attention_mask, L1_ffn_wr, L1_ffn_br, L1_ffn_w1, L1_ffn_b1, L1_ffn_w2, L1_ffn_b2):
    import jax
    import jax.numpy as jnp
    def _L0_conv_ref(x, norm1_w, norm2_w, w_qkv, w_proj, b_proj, ff1_w, ff1_b, ff2_w, ff2_b):
        import jax, jax.numpy as jnp
        import numpy as np
        KSIZE = 7
        HEAD_DIM = 64
        EPS = 1e-06

        def rmsnorm(x, w):
            return x * jax.lax.rsqrt(jnp.mean(x * x, axis=-1, keepdims=True) + EPS) * w

        def rope2d(x):
            B, H, W, C = x.shape
            half = C // 2
            q = half // 2
            inv = 1.0 / 10000.0 ** (jnp.arange(q, dtype=jnp.float32) / q)
            th_y = jnp.arange(H, dtype=jnp.float32)[:, None] * inv
            th_x = jnp.arange(W, dtype=jnp.float32)[:, None] * inv

            def rot(v, th):
                c, s = (jnp.cos(th), jnp.sin(th))
                a, b = (v[..., 0], v[..., 1])
                return jnp.stack([a * c - b * s, a * s + b * c], axis=-1)
            xy = rot(x[..., :half].reshape(B, H, W, q, 2), th_y[None, :, None, :])
            xx = rot(x[..., half:].reshape(B, H, W, q, 2), th_x[None, None, :, :])
            return jnp.concatenate([xy.reshape(B, H, W, half), xx.reshape(B, H, W, half)], axis=-1)

        def neighborhood_attn(x, w_qkv, w_proj, b_proj, k=KSIZE, hd=HEAD_DIM):
            B, H, W, C = x.shape
            nh = C // hd
            qkv = x @ w_qkv
            qv, kv, vv = jnp.split(qkv, 3, axis=-1)
            qh = qv.reshape(B, H, W, nh, hd)
            kh = kv.reshape(B, H, W, nh, hd)
            vh = vv.reshape(B, H, W, nh, hd)
            idx_h = jnp.clip(jnp.arange(H) - k // 2, 0, H - k)[:, None] + jnp.arange(k)
            idx_w = jnp.clip(jnp.arange(W) - k // 2, 0, W - k)[:, None] + jnp.arange(k)

            def gather(t):
                g = t[:, idx_h]
                g = g[:, :, :, idx_w]
                return g.transpose(0, 1, 3, 5, 2, 4, 6).reshape(B, H, W, nh, k * k, hd)
            kn = gather(kh)
            vn = gather(vh)
            scale = 1.0 / np.sqrt(hd).astype(np.float32)
            logits = jnp.einsum('bxynd,bxynkd->bxynk', qh, kn) * scale
            attn = jax.nn.softmax(logits, axis=-1)
            out = jnp.einsum('bxynk,bxynkd->bxynd', attn, vn).reshape(B, H, W, C)
            return out @ w_proj + b_proj

        def geglu(x, ff1_w, ff1_b, ff2_w, ff2_b):
            h = x @ ff1_w + ff1_b
            gate, value = jnp.split(h, 2, axis=-1)
            return jax.nn.gelu(gate, approximate=False) * value @ ff2_w + ff2_b
        h = rope2d(rmsnorm(x, norm1_w))
        x = x + neighborhood_attn(h, w_qkv, w_proj, b_proj)
        x = x + geglu(rmsnorm(x, norm2_w), ff1_w, ff1_b, ff2_w, ff2_b)
        return x

    def _L1_attn_ref(inputs, ln_gamma, ln_beta, Wq, bq, Wk, bk, Wv, bv, Wpos, u_bias, v_bias, Wout, bout):
        import jax, jax.numpy as jnp
        import numpy as np
        NUM_HEADS = 4
        LN_EPS = 1e-05

        def positional_encoding(length, d_model):
            pos = jnp.arange(length, dtype=jnp.float32)[:, None]
            div = jnp.exp(jnp.arange(0, d_model, 2, dtype=jnp.float32) * (-np.log(10000.0) / d_model))
            pe = jnp.zeros((length, d_model), dtype=jnp.float32)
            pe = pe.at[:, 0::2].set(jnp.sin(pos * div))
            pe = pe.at[:, 1::2].set(jnp.cos(pos * div))
            return pe

        def rel_shift(pos_score):
            B, H, S, _ = pos_score.shape
            padded = jnp.pad(pos_score, ((0, 0), (0, 0), (0, 0), (1, 0)))
            padded = padded.reshape(B, H, S + 1, S)
            return padded[:, :, 1:].reshape(B, H, S, S)
        B, S, D = inputs.shape
        H = NUM_HEADS
        dh = D // H
        mu = jnp.mean(inputs, axis=-1, keepdims=True)
        var = jnp.mean(jnp.square(inputs - mu), axis=-1, keepdims=True)
        x = (inputs - mu) / jnp.sqrt(var + LN_EPS) * ln_gamma + ln_beta
        pe = positional_encoding(S, D)
        q = (x @ Wq + bq).reshape(B, S, H, dh)
        k = (x @ Wk + bk).reshape(B, S, H, dh)
        v = (x @ Wv + bv).reshape(B, S, H, dh)
        p = (pe @ Wpos).reshape(S, H, dh)
        content_score = jnp.einsum('bshd,bthd->bhst', q + u_bias, k)
        pos_score = jnp.einsum('bshd,thd->bhst', q + v_bias, p)
        pos_score = rel_shift(pos_score)
        score = (content_score + pos_score) / np.sqrt(D).astype(np.float32)
        attn = jax.nn.softmax(score, axis=-1)
        ctx = jnp.einsum('bhst,bthd->bshd', attn, v).reshape(B, S, D)
        return ctx @ Wout + bout

    def _L1_ffn_ref(x, attention_mask, wr, br, w1, b1, w2, b2):
        import jax, jax.numpy as jnp
        import numpy as np
        B, S, D = (8, 4096, 256)
        H = 4 * D
        CAPACITY = 0.5
        b, s, d = x.shape
        weights = (jnp.einsum('bsd,do->bso', x, wr) + br)[..., 0]
        k = max(1, int(CAPACITY * s))
        kk = k - 1 if k > 1 else 1
        _, idx = jax.lax.top_k(weights, k)
        sel_idx = idx[:, :kk]
        sel = jnp.take_along_axis(x, sel_idx[:, :, None], axis=1)
        h = jax.nn.gelu(jnp.einsum('bkd,dh->bkh', sel, w1) + b1)
        y = jnp.einsum('bkh,hd->bkd', h, w2) + b2
        w_sel = jnp.take_along_axis(weights, sel_idx, axis=1)
        y = y * w_sel[..., None]
        batch_idx = jnp.arange(b)[:, None]
        processed = jnp.zeros_like(x).at[batch_idx, sel_idx].set(y)
        return processed + x

    def _gn(v, G=32, eps=1e-5):
        B_, H_, W_, C_ = v.shape
        g = v.reshape(B_, H_, W_, G, C_ // G)
        m = jnp.mean(g, axis=(1, 2, 4), keepdims=True)
        s = jnp.var(g, axis=(1, 2, 4), keepdims=True)
        return ((g - m) / jnp.sqrt(s + eps)).reshape(v.shape)

    def _ln_c(v, eps=1e-6):
        m = jnp.mean(v, axis=-1, keepdims=True)
        s = jnp.var(v, axis=-1, keepdims=True)
        return (v - m) / jnp.sqrt(s + eps)

    def _ln_t(v, eps=1e-5):
        m = jnp.mean(v, axis=-1, keepdims=True)
        s = jnp.var(v, axis=-1, keepdims=True)
        return (v - m) / jnp.sqrt(s + eps)

    def _to_tokens(v):
        B_, H_, W_, C_ = v.shape
        return v.reshape(B_, H_ * W_, C_)
    def _from_tokens(t, like):
        return t.reshape(like.shape)

    x = _L0_conv_ref(x, L0_conv_norm1_w, L0_conv_norm2_w, L0_conv_w_qkv, L0_conv_w_proj, L0_conv_b_proj, L0_conv_ff1_w, L0_conv_ff1_b, L0_conv_ff2_w, L0_conv_ff2_b)
    t = _to_tokens(x)
    t = t + _L1_attn_ref(_ln_t(t), L1_attn_ln_gamma, L1_attn_ln_beta, L1_attn_Wq, L1_attn_bq, L1_attn_Wk, L1_attn_bk, L1_attn_Wv, L1_attn_bv, L1_attn_Wpos, L1_attn_u_bias, L1_attn_v_bias, L1_attn_Wout, L1_attn_bout)
    t = t + _L1_ffn_ref(_ln_t(t), L1_ffn_attention_mask, L1_ffn_wr, L1_ffn_br, L1_ffn_w1, L1_ffn_b1, L1_ffn_w2, L1_ffn_b2)
    x = _from_tokens(t, x)
    return x


_drawn_inputs = setup_inputs


def setup_inputs(seed=0):
    import zlib

    import numpy as np

    out = dict(_drawn_inputs(seed))
    spreads = {'L0_conv_norm1_w': (1.0, 0.6),
     'L0_conv_norm2_w': (1.0, 0.6),
     'L1_attn_ln_gamma': (1.0, 0.6),
     'L1_attn_ln_beta': (0.0, 0.777),
     'L1_attn_bq': (0.0, 0.8),
     'L1_attn_bk': (0.0, 2.0),
     'L1_attn_bv': (0.0, 0.326),
     'L1_attn_bout': (0.0, 0.1),
     'L1_ffn_b1': (0.0, 0.8),
     'L1_ffn_b2': (0.0, 0.67)}
    factors = {'L0_conv_w_qkv': 3.741,
     'L0_conv_w_proj': 3.763,
     'L0_conv_b_proj': 3.098,
     'L0_conv_ff1_w': 2.864,
     'L0_conv_ff1_b': 8.0,
     'L0_conv_ff2_w': 2.866,
     'L0_conv_ff2_b': 2.805,
     'L1_attn_Wq': 8.0,
     'L1_attn_Wk': 8.0,
     'L1_attn_Wv': 5.003,
     'L1_attn_Wpos': 8.0,
     'L1_attn_u_bias': 8.0,
     'L1_attn_v_bias': 27.085,
     'L1_ffn_wr': 3.945,
     'L1_ffn_w1': 4.658,
     'L1_ffn_w2': 4.348}
    for name, (base, spread) in spreads.items():
        noise = np.random.default_rng([zlib.crc32(name.encode()), seed]).standard_normal(out[name].shape)
        drawn = base * np.exp(spread * noise) if base else spread * noise
        out[name] = jnp.asarray(drawn.astype(out[name].dtype))
    for name, factor in factors.items():
        out[name] = (out[name] * factor).astype(out[name].dtype)
    return out
```

```python
import numpy as np
import math
import concourse.bass as bass
from concourse import mybir
from contextlib import ExitStack

P = 128
F32 = mybir.dt.float32
F16 = mybir.dt.float16
U32 = mybir.dt.uint32
ALU = mybir.AluOpType
ACT = mybir.ActivationFunctionType
AX_X = mybir.AxisListType.X
ds = bass.ds

PRIME = 2


def made(n, per=1):
    return (n + 1 + PRIME) * per


def made_before(n, back, per=1):
    return (n + 1 + PRIME - back) * per


Q_SCALE = 32.0
B_SCALE = 8.0
PE_SCALE = 128.0
V_SCALE = 32.0
SCORE_SCALE = Q_SCALE * Q_SCALE
assert SCORE_SCALE == B_SCALE * PE_SCALE
P_SCALE = 1024.0


TOK = 512
SUB = TOK // P
C = 256
NH = 4
HD = C // NH


class Mem:

    def __init__(self, nc, ctx, tag):
        self.nc, self.ctx, self.tag = nc, ctx, tag

    def sb(self, name, shape, dt=F32):
        return self.ctx.enter_context(self.nc.sbuf_tensor(f"{self.tag}_{name}", shape, dt))

    def psum(self, name, shape):
        return self.ctx.enter_context(self.nc.psum_tensor(f"{self.tag}_{name}", shape, F32))

    def sem(self, name):
        return self.ctx.enter_context(self.nc.semaphore(f"{self.tag}_{name}"))


def bounded(value, most):
    return value if isinstance(value, int) else value.with_bounds(min_val=0, max_val=most)


def rows(dram, first, n=SUB):
    return dram[ds(first, n * P), :].rearrange("(k p) c -> p k c", p=P)


def spread(vec, n=P):
    return vec.rearrange("(o c) -> o c", o=1).to_broadcast([n, vec.shape[0]])


def columns(vec):
    return vec.rearrange("(k p) -> p k", p=P)


def over_rows(tile):
    return tile[:].rearrange("p (o c) -> p o c", o=1).to_broadcast([P, SUB, tile.shape[1]])


def qkv_phase(nc, n_tok, seq, x, norm_w, w_qkv, rope, identity, qk_t, v_out):
    steps = n_tok // TOK
    with ExitStack() as ctx:
        m = Mem(nc, ctx, "qkv")
        w_sb = m.sb("w", [P, 2, 3 * C])
        nw = m.sb("nw", [P, C])
        ident = m.sb("id", [P, P])
        x_sb = m.sb("x", [P, 2, SUB, C])
        rope_sb = m.sb("rope", [P, 2, 2, SUB, P])
        junk = m.sb("junk", [P, SUB, C])
        ss = m.sb("ss", [P, 2, SUB])
        ms = m.sb("ms", [P, 2, SUB])
        sd = m.sb("sd", [P, 2, SUB])
        rs = m.sb("rs", [P, 2, SUB])
        xn = m.sb("xn", [P, SUB, C])
        t_v = m.sb("t_v", [P, 2, SUB, P])
        t_p = m.sb("t_p", [P, 2, SUB, P])
        h_sb = m.sb("h", [P, 2, SUB, C])
        ht = m.sb("ht", [P, 2, 2, TOK])
        qk_o = m.sb("qk_o", [P, 2, 4, TOK])
        v_o = m.sb("v_o", [P, 2, SUB, C])
        t_ps = m.psum("t_ps", [P, 2, TOK])
        qk_ps = m.psum("qk_ps", [P, 4, TOK])
        v_ps = m.psum("v_ps", [P, SUB, C])

        const_in = m.sem("const_in")
        x_in = [m.sem(f"x_in{p}") for p in range(2)]
        stored = [m.sem(f"stored{p}") for p in range(2)]
        squared = m.sem("squared")
        meaned = m.sem("meaned")
        rooted = m.sem("rooted")
        inverted = m.sem("inverted")
        normed = m.sem("normed")
        halves = m.sem("halves")
        even_done = m.sem("even_done")
        pool_step = m.sem("pool_step")
        odd_done = m.sem("odd_done")
        turned = m.sem("turned")
        ht_a = m.sem("ht_a")
        ht_b = m.sem("ht_b")
        multiplied = m.sem("multiplied")
        qk_read = m.sem("qk_read")
        v_read = m.sem("v_read")
        block = ctx.enter_context(nc.Block())

        @block.sync
        def _(sp):
            sp.dma_start(w_sb[:], w_qkv.rearrange("(k p) n -> p k n", p=P)).then_inc(const_in, 16)
            sp.dma_start(nw[:], spread(norm_w)).then_inc(const_in, 16)
            sp.dma_start(ident[:], identity).then_inc(const_in, 16)
            for s in stored:
                sp.sem_inc(s, 32)

            def load(t, par):
                sp.wait_ge(even_done, made_before(t, 2))
                sp.wait_ge(odd_done, made_before(t, 2))
                sp.dma_start(x_sb[:, par], rows(x, t * TOK)).then_inc(x_in[par], 16)
                pos = (t % (seq // TOK)) * TOK
                for a in range(2):
                    sp.dma_start(rope_sb[:, par, a], rows(rope[a], pos)).then_inc(x_in[par], 16)

            def store(t, par):
                sp.wait_ge(v_read, made(t))
                sp.wait_ge(qk_read, made(t))
                sp.dma_start(rows(v_out, t * TOK), v_o[:, par]).then_inc(stored[par], 16)
                sp.dma_start(qk_t.rearrange("(m p) t -> p m t", p=P)[:, :, ds(t * TOK, TOK)],
                             qk_o[:, par]).then_inc(stored[par], 16)

            load(0, 0)
            with sp.Fori(0, steps // 2 - 1) as i:
                load(2 * i + 1, 1)
                store(2 * i, 0)
                load(2 * i + 2, 0)
                store(2 * i + 1, 1)
            load(steps - 1, 1)
            store(steps - 2, 0)
            store(steps - 1, 1)
            for s in stored:
                sp.wait_ge(s, 32 * (steps // 2 + 1))

        @block.scalar
        def _(act):
            for s in (squared, rooted, ht_a, qk_read):
                act.sem_inc(s, PRIME)

            def norm(t, i, par):
                act.wait_ge(x_in[par], 48 * (i + 1))
                for k in range(SUB):
                    sq = nc.scalar.activation(junk[:, k], x_sb[:, par, k], ACT.Square, accum_out=ss[:, par, k:k + 1])
                sq.then_inc(squared, 1)
                act.wait_ge(meaned, made(t))
                nc.scalar.activation(sd[:, par], ms[:, par], ACT.Sqrt).then_inc(rooted, 1)

            def step(t, i, par):
                norm(t, i, par)
                act.wait_ge(turned, made(t))
                nc.scalar.activation(ht[:, par, 0], t_ps[:, 0], ACT.Copy).then_inc(ht_a, 1)
                act.wait_ge(multiplied, made(t))
                act.wait_ge(stored[par], 32 * (i + 1))
                nc.scalar.activation(qk_o[:, par], qk_ps[:], ACT.Copy).then_inc(qk_read, 1)

            with act.Fori(0, steps // 2) as i:
                step(2 * i, i, 0)
                step(2 * i + 1, i, 1)

        @block.vector
        def _(dve):
            for s in (meaned, inverted, normed, halves, even_done, ht_b, v_read):
                dve.sem_inc(s, PRIME)
            dve.wait_ge(const_in, 48)

            def step(t, i, par):
                dve.wait_ge(squared, made(t))
                nc.vector.tensor_scalar(ms[:, par], ss[:, par], 1.0 / C, 1e-6, ALU.mult, ALU.add).then_inc(meaned, 1)
                dve.wait_ge(rooted, made(t))
                nc.vector.reciprocal(rs[:, par], sd[:, par]).then_inc(inverted, 1)
                dve.wait_ge(inverted, made(t))
                dve.wait_ge(x_in[par], 48 * (i + 1))
                dve.wait_ge(odd_done, made_before(t, 1))
                for k in range(SUB):
                    st = nc.vector.scalar_tensor_tensor(out=xn[:, k], in0=x_sb[:, par, k], scalar=rs[:, par, k:k + 1],
                                                        in1=nw[:], op0=ALU.mult, op1=ALU.mult)
                st.then_inc(normed, 1)
                dve.wait_ge(normed, made(t))
                ev, od = xn[:, :, 0::2], xn[:, :, 1::2]
                nc.vector.tensor_tensor(t_v[:, 0], ev, rope_sb[:, par, 0], ALU.mult)
                nc.vector.tensor_tensor(t_v[:, 1], od, rope_sb[:, par, 1], ALU.mult).then_inc(halves, 1)
                dve.wait_ge(halves, made(t))
                dve.wait_ge(turned, made_before(t, 2))
                nc.vector.tensor_tensor(h_sb[:, par, :, 0::2], t_v[:, 0], t_v[:, 1],
                                        ALU.subtract).then_inc(even_done, 1)
                dve.wait_ge(turned, made(t))
                nc.vector.tensor_copy(ht[:, par, 1], t_ps[:, 1]).then_inc(ht_b, 1)
                dve.wait_ge(multiplied, made(t))
                dve.wait_ge(stored[par], 32 * (i + 1))
                nc.vector.tensor_copy(v_o[:, par], v_ps[:]).then_inc(v_read, 1)

            with dve.Fori(0, steps // 2) as i:
                step(2 * i, i, 0)
                step(2 * i + 1, i, 1)

        @block.gpsimd
        def _(pool):
            for s in (pool_step, odd_done):
                pool.sem_inc(s, PRIME)

            def step(t, par):
                pool.wait_ge(normed, made(t))
                ev, od = xn[:, :, 0::2], xn[:, :, 1::2]
                nc.gpsimd.tensor_tensor(t_p[:, 0], ev, rope_sb[:, par, 1], ALU.mult)
                nc.gpsimd.tensor_tensor(t_p[:, 1], od, rope_sb[:, par, 0], ALU.mult).then_inc(pool_step, 1)
                pool.wait_ge(pool_step, made(t))
                pool.wait_ge(turned, made_before(t, 2))
                nc.gpsimd.tensor_tensor(h_sb[:, par, :, 1::2], t_p[:, 0], t_p[:, 1], ALU.add).then_inc(odd_done, 1)

            with pool.Fori(0, steps // 2) as i:
                step(2 * i, 0)
                step(2 * i + 1, 1)

        @block.tensor
        def _(pe):
            pe.sem_inc(turned, PRIME)
            pe.sem_inc(multiplied, PRIME)
            pe.wait_ge(const_in, 48)

            def step(t, par):
                pe.wait_ge(even_done, made(t))
                pe.wait_ge(odd_done, made(t))
                pe.wait_ge(ht_a, made_before(t, 1))
                pe.wait_ge(ht_b, made_before(t, 1))
                for k in range(SUB):
                    for c in range(2):
                        tr = nc.tensor.transpose(t_ps[:, c, k * P:(k + 1) * P], h_sb[:, par, k, c * P:(c + 1) * P],
                                                 ident[:])
                tr.then_inc(turned, 1)
                pe.wait_ge(ht_a, made(t))
                pe.wait_ge(ht_b, made(t))
                pe.wait_ge(qk_read, made_before(t, 1))
                for o in range(4):
                    for c in range(2):
                        nc.tensor.matmul(qk_ps[:, o], w_sb[:, c, o * P:(o + 1) * P], ht[:, par, c],
                                         start=(c == 0), stop=(c == 1))
                pe.wait_ge(v_read, made_before(t, 1))
                for k in range(SUB):
                    for c in range(2):
                        mm = nc.tensor.matmul(v_ps[:, k], ht[:, par, c, k * P:(k + 1) * P], w_sb[:, c, 2 * C:3 * C],
                                              start=(c == 0), stop=(c == 1))
                mm.then_inc(multiplied, 1)

            with pe.Fori(0, steps // 2) as i:
                step(2 * i, 0)
                step(2 * i + 1, 1)


def window_phase(nc, batches, rows_, cols, qk_t, v, masks, identity, ctx_out):
    KS = 7
    pairs = rows_ // 2
    units = batches * pairs
    span = 8
    assert cols == 64 and span * cols == 512
    last = rows_ - span
    hi_y = pairs - 2
    UB = 4
    with ExitStack() as ctx:
        m = Mem(nc, ctx, "win")
        mask_sb = m.sb("mask", [P, 3 * 512])
        ident = m.sb("id", [P, P])
        q_sb = m.sb("q", [HD, UB, NH, P])
        k_sb = m.sb("k", [HD, UB, NH, 512])
        v_sb = m.sb("v", [P, UB, SUB, C])
        s_sb = m.sb("s", [P, 2, 2, 512])
        mx = m.sb("mx", [P, 2, 2])
        nm = m.sb("nm", [P, 2, 2])
        p_sb = m.sb("p", [P, 2, 2, 512])
        sm = m.sb("sm", [P, 2, 2])
        rs = m.sb("rs", [P, 2, 2])
        pt = m.sb("pt", [P, 2, 2, 512])
        o_sb = m.sb("o", [P, 2, NH, HD])
        s_ps = m.psum("s_ps", [P, 4, 512])
        t_ps = m.psum("t_ps", [P, 2, 512])
        o_ps = m.psum("o_ps", [P, 2, 512])

        const_in = m.sem("const_in")
        qkv_in = [m.sem(f"qkv_in{p}") for p in range(UB)]
        stored = [m.sem(f"stored{p}") for p in range(2)]
        scored = m.sem("scored")
        masked = m.sem("masked")
        maxed = m.sem("maxed")
        negated = m.sem("negated")
        exped = m.sem("exped")
        turned = m.sem("turned")
        pt_a = m.sem("pt_a")
        pt_b = m.sem("pt_b")
        weighed = m.sem("weighed")
        inverted = m.sem("inverted")
        out_made = m.sem("out_made")
        block = ctx.enter_context(nc.Block())

        @block.sync
        def _(sp):
            sp.dma_start(mask_sb[:], masks).then_inc(const_in, 16)
            sp.dma_start(ident[:], identity).then_inc(const_in, 16)
            for s in stored:
                sp.sem_inc(s, 16)

            def load(u, buf, first=False):
                b, y = u // pairs, u % pairs
                inner = (y >= 2) * (y < hi_y)
                top = (2 * y - KS // 2) * inner + last * (y >= hi_y)
                tok = b * (rows_ * cols) + y * P
                key = bounded(b * (rows_ * cols) + top * cols, batches * rows_ * cols - 512)
                if not first:
                    sp.wait_ge(weighed, made(2 * (u - UB) + 1))
                qk = qk_t.rearrange("(a h d) t -> a d h t", a=2, h=NH)
                sp.dma_start(q_sb[:, buf], qk[0][:, :, ds(tok, P)]).then_inc(qkv_in[buf], 16)
                sp.dma_start(k_sb[:, buf], qk[1][:, :, ds(key, 512)]).then_inc(qkv_in[buf], 16)
                sp.dma_start(v_sb[:, buf], rows(v, key)).then_inc(qkv_in[buf], 16)

            def store(u, par):
                sp.wait_ge(out_made, made(2 * u + 1))
                sp.dma_start(ctx_out[ds(u * P, P), :], o_sb[:, par].rearrange("p h d -> p (h d)")
                             ).then_inc(stored[par], 16)

            for u in range(UB):
                load(u, u, first=True)
            with sp.Fori(0, units // UB - 1) as i:
                for a in range(UB):
                    store(UB * i + a, a % 2)
                    load(UB * (i + 1) + a, a)
            for u in range(units - UB, units):
                store(u, u % 2)
            for s in stored:
                sp.wait_ge(s, 16 * (units // 2 + 1))

        def pipeline(eng, scores, turn, weigh, turn_first=False):
            for n in range(2):
                scores(n, 0, n)
            turn(0, 0)

            def item(i, j, left=2 * UB):
                n = 2 * UB * i + j
                if turn_first and left > 1:
                    turn(n + 1, j + 1)
                if left > 2:
                    scores(n + 2, i + (j + 2) // (2 * UB), (j + 2) % (2 * UB))
                weigh(n, i, j)
                if left > 1 and not turn_first:
                    turn(n + 1, j + 1)

            with eng.Fori(0, units // UB - 1) as i:
                for j in range(2 * UB):
                    item(i, j)
            for j in range(2 * UB):
                item(units // UB - 1, j, left=2 * UB - j)

        @block.tensor
        def _(pe):
            for s in (scored, turned, weighed):
                pe.sem_inc(s, PRIME)
            pe.wait_ge(const_in, 32)

            def scores(n, i, j):
                if j % 2 == 0:
                    pe.wait_ge(qkv_in[j // 2], 48 * (i + 1))
                pe.wait_ge(masked, made_before(n, 2))
                for a in range(2):
                    h = 2 * (j % 2) + a
                    mm = nc.tensor.matmul(s_ps[:, h], q_sb[:, j // 2, h], k_sb[:, j // 2, h], start=True, stop=True)
                mm.then_inc(scored, 1)

            def turn(n, j):
                pe.wait_ge(exped, made(n))
                pe.wait_ge(pt_a, made_before(n, 1))
                pe.wait_ge(pt_b, made_before(n, 1))
                for a in range(2):
                    for c in range(4):
                        tr = nc.tensor.transpose(t_ps[:, a, c * P:(c + 1) * P],
                                                 p_sb[:, j % 2, a, c * P:(c + 1) * P], ident[:])
                tr.then_inc(turned, 1)

            def weigh(n, i, j):
                pe.wait_ge(pt_a, made(n))
                pe.wait_ge(pt_b, made(n))
                pe.wait_ge(out_made, made_before(n, 2))
                for a in range(2):
                    h = 2 * (j % 2) + a
                    for c in range(4):
                        mm = nc.tensor.matmul(o_ps[:, j % 2, a * HD:(a + 1) * HD], pt[:, j % 2, a, c * P:(c + 1) * P],
                                              v_sb[:, j // 2, c, h * HD:(h + 1) * HD], start=(c == 0), stop=(c == 3))
                mm.then_inc(weighed, 1)

            pipeline(pe, scores, turn, weigh)

        @block.vector
        def _(dve):
            for s in (masked, maxed, negated, pt_a, inverted, out_made):
                dve.sem_inc(s, PRIME)
            dve.wait_ge(const_in, 32)

            def find_max(n, i, j):
                y = (n // 2) % pairs
                kind = (y >= 2) + (y >= hi_y) if not isinstance(y, int) else int(y >= 2) + int(y >= hi_y)
                dve.wait_ge(scored, made(n))
                dve.wait_ge(exped, made_before(n, 2))
                mk = mask_sb[:, ds(kind * 512, 512)]
                for a in range(2):
                    op = nc.vector.tensor_tensor(s_sb[:, j % 2, a], s_ps[:, 2 * (j % 2) + a], mk, ALU.add)
                op.then_inc(masked, 1)
                dve.wait_ge(masked, made(n))
                nc.vector.tensor_reduce(mx[:, j % 2], s_sb[:, j % 2], AX_X, ALU.max).then_inc(maxed, 1)
                dve.wait_ge(maxed, made(n))
                nc.vector.tensor_scalar(nm[:, j % 2], mx[:, j % 2], -(HD ** -0.5), None, ALU.mult).then_inc(negated, 1)

            def copy_turned(n, j):
                dve.wait_ge(turned, made(n))
                dve.wait_ge(weighed, made_before(n, 2))
                nc.vector.tensor_copy(pt[:, j % 2, 0], t_ps[:, 0]).then_inc(pt_a, 1)

            def finish(n, i, j):
                dve.wait_ge(exped, made(n))
                nc.vector.reciprocal(rs[:, j % 2], sm[:, j % 2]).then_inc(inverted, 1)
                dve.wait_ge(inverted, made(n))
                dve.wait_ge(weighed, made(n))
                if j % 2 == 0:
                    dve.wait_ge(stored[j // 2 % 2], 16 * (UB // 2 * i + j // 4 + 1))
                nc.vector.tensor_tensor(o_sb[:, j // 2 % 2, 2 * (j % 2):2 * (j % 2) + 2],
                                        o_ps[:, j % 2, 0:2 * HD].rearrange("p (h d) -> p h d", h=2),
                                        rs[:, j % 2].rearrange("p (h o) -> p h o", o=1).to_broadcast([P, 2, HD]),
                                        ALU.mult).then_inc(out_made, 1)

            pipeline(dve, find_max, copy_turned, finish)

        @block.scalar
        def _(act):
            act.sem_inc(exped, PRIME)
            act.sem_inc(pt_b, PRIME)

            def exponentials(n, i, j):
                act.wait_ge(negated, made(n))
                act.wait_ge(turned, made_before(n, 2))
                act.wait_ge(inverted, made_before(n, 2))
                for a in range(2):
                    ex = nc.scalar.activation(p_sb[:, j % 2, a], s_sb[:, j % 2, a], ACT.Exp, bias=nm[:, j % 2, a:a + 1],
                                              scale=HD ** -0.5, accum_out=sm[:, j % 2, a:a + 1])
                ex.then_inc(exped, 1)

            def copy_turned(n, j):
                act.wait_ge(turned, made(n))
                act.wait_ge(weighed, made_before(n, 2))
                nc.scalar.activation(pt[:, j % 2, 1], t_ps[:, 1], ACT.Copy).then_inc(pt_b, 1)

            def nothing(n, i, j):
                pass

            pipeline(act, exponentials, copy_turned, nothing, turn_first=True)


def layer0_mlp_phase(nc, n_tok, x, ctx_in, w_proj, b_proj, norm_w, ff1_w, ff1_b, ff2_w, ff2_b, identity, x_out):
    steps = n_tok // TOK
    with ExitStack() as ctx:
        m = Mem(nc, ctx, "mlp")
        wp = m.sb("wp", [P, 2, C])
        w1 = m.sb("w1", [P, 2, 2 * C])
        w2 = m.sb("w2", [P, 2, C])
        nw = m.sb("nw", [P, C])
        bp = m.sb("bp", [P, C])
        b2 = m.sb("b2", [P, C])
        b1 = m.sb("b1", [P, 4])
        ident = m.sb("id", [P, P])
        c_sb = m.sb("c", [P, 2, SUB, C])
        x_sb = m.sb("x", [P, 2, SUB, C])
        xb = m.sb("xb", [P, SUB, C])
        x1 = m.sb("x1", [P, 2, SUB, C])
        x1b = m.sb("x1b", [P, 2, SUB, C])
        junk = m.sb("junk", [P, SUB, C])
        ss = m.sb("ss", [P, SUB])
        ms = m.sb("ms", [P, SUB])
        sd = m.sb("sd", [P, SUB])
        rs = m.sb("rs", [P, SUB])
        xn = m.sb("xn", [P, SUB, C])
        ct = m.sb("ct", [P, 2, TOK])
        nt = m.sb("nt", [P, 2, TOK])
        gate = m.sb("gate", [P, 2, TOK])
        ut = m.sb("ut", [P, 2, TOK])
        x2 = m.sb("x2", [P, 2, SUB, C])
        t_ps = m.psum("t_ps", [P, 2, TOK])
        f_ps = m.psum("f_ps", [P, 4, TOK])
        p_ps = m.psum("p_ps", [P, SUB, C])

        const_in = m.sem("const_in")
        rows_in = [m.sem(f"rows_in{p}") for p in range(2)]
        stored = [m.sem(f"stored{p}") for p in range(2)]
        ctx_turned = m.sem("ctx_turned")
        ct_a, ct_b = m.sem("ct_a"), m.sem("ct_b")
        projected = m.sem("projected")
        xb_made = m.sem("xb_made")
        x1_made = m.sem("x1_made")
        x1b_made = m.sem("x1b_made")
        squared, meaned, rooted, inverted = m.sem("squared"), m.sem("meaned"), m.sem("rooted"), m.sem("inverted")
        normed = m.sem("normed")
        rows_turned = m.sem("rows_turned")
        nt_a, nt_b = m.sem("nt_a"), m.sem("nt_b")
        widened = m.sem("widened")
        gated = m.sem("gated")
        u_made = m.sem("u_made")
        narrowed = m.sem("narrowed")
        x2_made = m.sem("x2_made")
        block = ctx.enter_context(nc.Block())

        @block.sync
        def _(sp):
            sp.dma_start(wp[:], w_proj.rearrange("(k p) n -> p k n", p=P)).then_inc(const_in, 16)
            sp.dma_start(w1[:], ff1_w.rearrange("(k p) n -> p k n", p=P)).then_inc(const_in, 16)
            sp.dma_start(w2[:], ff2_w.rearrange("(k p) n -> p k n", p=P)).then_inc(const_in, 16)
            sp.dma_start(nw[:], spread(norm_w)).then_inc(const_in, 16)
            sp.dma_start(bp[:], spread(b_proj)).then_inc(const_in, 16)
            sp.dma_start(b2[:], spread(ff2_b)).then_inc(const_in, 16)
            sp.dma_start(b1[:], columns(ff1_b), allow_slow_non_contiguous=True).then_inc(const_in, 16)
            sp.dma_start(ident[:], identity).then_inc(const_in, 16)
            for s in stored:
                sp.sem_inc(s, 16)

            def load(t, par):
                sp.wait_ge(ctx_turned, made_before(t, 2))
                sp.wait_ge(xb_made, made_before(t, 2))
                sp.dma_start(c_sb[:, par], rows(ctx_in, t * TOK)).then_inc(rows_in[par], 16)
                sp.dma_start(x_sb[:, par], rows(x, t * TOK)).then_inc(rows_in[par], 16)

            def store(t, par):
                sp.wait_ge(x2_made, made(t))
                sp.dma_start(rows(x_out, t * TOK), x2[:, par]).then_inc(stored[par], 16)

            load(0, 0)
            load(1, 1)
            with sp.Fori(0, steps // 2 - 1) as i:
                load(2 * i + 2, 0)
                store(2 * i, 0)
                load(2 * i + 3, 1)
                store(2 * i + 1, 1)
            store(steps - 2, 0)
            store(steps - 1, 1)
            for s in stored:
                sp.wait_ge(s, 16 * (steps // 2 + 1))

        @block.tensor
        def _(pe):
            for s in (ctx_turned, projected, rows_turned, widened, narrowed):
                pe.sem_inc(s, PRIME)
            pe.wait_ge(const_in, 128)

            def project(t, i, par):
                pe.wait_ge(rows_in[par], 32 * (i + 1))
                pe.wait_ge(nt_a, made_before(t, 1))
                pe.wait_ge(nt_b, made_before(t, 1))
                for k in range(SUB):
                    for c in range(2):
                        tr = nc.tensor.transpose(t_ps[:, c, k * P:(k + 1) * P], c_sb[:, par, k, c * P:(c + 1) * P],
                                                 ident[:])
                tr.then_inc(ctx_turned, 1)
                pe.wait_ge(ct_a, made(t))
                pe.wait_ge(ct_b, made(t))
                pe.wait_ge(x2_made, made_before(t, 2))
                for k in range(SUB):
                    for c in range(2):
                        mm = nc.tensor.matmul(p_ps[:, k], ct[:, c, k * P:(k + 1) * P], wp[:, c],
                                              start=(c == 0), stop=(c == 1))
                mm.then_inc(projected, 1)

            def widen(t):
                pe.wait_ge(normed, made(t))
                for k in range(SUB):
                    for c in range(2):
                        tr = nc.tensor.transpose(t_ps[:, c, k * P:(k + 1) * P], xn[:, k, c * P:(c + 1) * P], ident[:])
                tr.then_inc(rows_turned, 1)
                pe.wait_ge(nt_a, made(t))
                pe.wait_ge(nt_b, made(t))
                pe.wait_ge(u_made, made_before(t, 1))
                for o in range(4):
                    for c in range(2):
                        mm = nc.tensor.matmul(f_ps[:, o], w1[:, c, o * P:(o + 1) * P], nt[:, c],
                                              start=(c == 0), stop=(c == 1))
                mm.then_inc(widened, 1)

            def narrow(t):
                pe.wait_ge(u_made, made(t))
                for k in range(SUB):
                    for c in range(2):
                        mm = nc.tensor.matmul(p_ps[:, k], ut[:, c, k * P:(k + 1) * P], w2[:, c],
                                              start=(c == 0), stop=(c == 1))
                mm.then_inc(narrowed, 1)

            def step(t, i, par, ahead=True):
                widen(t)
                if ahead:
                    project(t + 1, i + par, 1 - par)
                    pe.wait_ge(x1_made, made(t + 1))
                narrow(t)

            project(0, 0, 0)
            with pe.Fori(0, steps // 2 - 1) as i:
                step(2 * i, i, 0)
                step(2 * i + 1, i, 1)
            step(steps - 2, steps // 2 - 1, 0)
            step(steps - 1, steps // 2 - 1, 1, ahead=False)

        @block.gpsimd
        def _(pool):
            pool.sem_inc(xb_made, PRIME)
            pool.sem_inc(x1b_made, PRIME)
            pool.wait_ge(const_in, 128)

            def step(t, i, par):
                pool.wait_ge(rows_in[par], 32 * (i + 1))
                pool.wait_ge(x1_made, made_before(t, 1))
                nc.gpsimd.tensor_tensor(xb[:], x_sb[:, par], over_rows(bp), ALU.add).then_inc(xb_made, 1)
                pool.wait_ge(x1_made, made(t))
                pool.wait_ge(x2_made, made_before(t, 2))
                nc.gpsimd.tensor_tensor(x1b[:, par], x1[:, par], over_rows(b2), ALU.add).then_inc(x1b_made, 1)

            with pool.Fori(0, steps // 2) as i:
                step(2 * i, i, 0)
                step(2 * i + 1, i, 1)

        @block.scalar
        def _(act):
            for s in (ct_a, squared, rooted, nt_a, gated):
                act.sem_inc(s, PRIME)
            act.wait_ge(const_in, 128)

            def first_half(t, par):
                act.wait_ge(ctx_turned, made(t))
                act.wait_ge(projected, made_before(t, 1))
                nc.scalar.activation(ct[:, 0], t_ps[:, 0], ACT.Copy).then_inc(ct_a, 1)
                act.wait_ge(x1_made, made(t))
                act.wait_ge(meaned, made_before(t, 1))
                for k in range(SUB):
                    sq = nc.scalar.activation(junk[:, k], x1[:, par, k], ACT.Square, accum_out=ss[:, k:k + 1])
                sq.then_inc(squared, 1)
                act.wait_ge(meaned, made(t))
                act.wait_ge(inverted, made_before(t, 1))
                nc.scalar.activation(sd[:], ms[:], ACT.Sqrt).then_inc(rooted, 1)

            def step(t, par, ahead=True):
                act.wait_ge(rows_turned, made(t))
                act.wait_ge(widened, made_before(t, 1))
                nc.scalar.activation(nt[:, 0], t_ps[:, 0], ACT.Copy).then_inc(nt_a, 1)
                act.wait_ge(widened, made(t))
                act.wait_ge(u_made, made_before(t, 1))
                for c in range(2):
                    ge = nc.scalar.activation(gate[:, c], f_ps[:, c], ACT.Gelu, bias=b1[:, c:c + 1])
                ge.then_inc(gated, 1)
                if ahead:
                    first_half(t + 1, 1 - par)

            first_half(0, 0)
            with act.Fori(0, steps // 2 - 1) as i:
                step(2 * i, 0)
                step(2 * i + 1, 1)
            step(steps - 2, 0)
            step(steps - 1, 1, ahead=False)

        @block.vector
        def _(dve):
            for s in (ct_b, x1_made, meaned, inverted, normed, nt_b, u_made, x2_made):
                dve.sem_inc(s, PRIME)
            dve.wait_ge(const_in, 128)

            def first_half(t, par):
                dve.wait_ge(ctx_turned, made(t))
                dve.wait_ge(projected, made_before(t, 1))
                nc.vector.tensor_copy(ct[:, 1], t_ps[:, 1]).then_inc(ct_b, 1)
                dve.wait_ge(projected, made(t))
                dve.wait_ge(xb_made, made(t))
                dve.wait_ge(x1b_made, made_before(t, 2))
                nc.vector.tensor_tensor(x1[:, par], p_ps[:], xb[:], ALU.add).then_inc(x1_made, 1)
                dve.wait_ge(squared, made(t))
                nc.vector.tensor_scalar(ms[:], ss[:], 1.0 / C, 1e-6, ALU.mult, ALU.add).then_inc(meaned, 1)
                dve.wait_ge(rooted, made(t))
                nc.vector.reciprocal(rs[:], sd[:]).then_inc(inverted, 1)
                dve.wait_ge(inverted, made(t))
                dve.wait_ge(rows_turned, made_before(t, 1))
                for k in range(SUB):
                    st = nc.vector.scalar_tensor_tensor(out=xn[:, k], in0=x1[:, par, k], scalar=rs[:, k:k + 1],
                                                        in1=nw[:], op0=ALU.mult, op1=ALU.mult)
                st.then_inc(normed, 1)

            def step(t, i, par, ahead=True):
                dve.wait_ge(rows_turned, made(t))
                dve.wait_ge(widened, made_before(t, 1))
                nc.vector.tensor_copy(nt[:, 1], t_ps[:, 1]).then_inc(nt_b, 1)
                dve.wait_ge(gated, made(t))
                dve.wait_ge(narrowed, made_before(t, 1))
                for c in range(2):
                    st = nc.vector.scalar_tensor_tensor(out=ut[:, c], in0=f_ps[:, 2 + c], scalar=b1[:, 2 + c:3 + c],
                                                        in1=gate[:, c], op0=ALU.add, op1=ALU.mult)
                st.then_inc(u_made, 1)
                if ahead:
                    first_half(t + 1, 1 - par)
                dve.wait_ge(narrowed, made(t))
                dve.wait_ge(x1b_made, made(t))
                dve.wait_ge(stored[par], 16 * (i + 1))
                nc.vector.tensor_tensor(x2[:, par], p_ps[:], x1b[:, par], ALU.add).then_inc(x2_made, 1)

            first_half(0, 0)
            with dve.Fori(0, steps // 2 - 1) as i:
                step(2 * i, i, 0)
                step(2 * i + 1, i, 1)
            step(steps - 2, steps // 2 - 1, 0)
            step(steps - 1, steps // 2 - 1, 1, ahead=False)


def tables_phase(nc, batches, seq, x, gamma, beta, wq, bq, wk, bk, wv, bv, wpos_t, u_bias, v_bias, turn_tab,
                 identity, q_tab, q_past, k_tab, v_tab):
    per_b = seq // TOK
    steps = batches * per_b
    with ExitStack() as ctx:
        m = Mem(nc, ctx, "tab")
        wq_sb = m.sb("wq", [P, 2, NH, 2, HD])
        wk_sb = m.sb("wk", [P, 2, NH, 2, HD])
        wv_sb = m.sb("wv", [P, 2, C])
        wp_sb = m.sb("wp", [HD, NH, 2, P])
        turn = m.sb("turn", [P, 2, seq])
        ga = m.sb("ga", [P, C])
        be = m.sb("be", [P, C])
        bvb = m.sb("bvb", [P, C])
        bvs = m.sb("bvs", [P, C])
        bq_sb = m.sb("bq", [P, NH])
        bk_sb = m.sb("bk", [P, NH])
        ub = m.sb("ub", [P, NH])
        vb = m.sb("vb", [P, NH])
        bqu = m.sb("bqu", [P, NH])
        bqus = m.sb("bqus", [P, NH])
        bqv = m.sb("bqv", [P, NH])
        bks = m.sb("bks", [P, NH])
        ident = m.sb("id", [P, P])
        x_sb = m.sb("x", [P, 2, SUB, C])
        spare = m.sb("spare", [P, 1])
        st1, st2 = m.sb("st1", [P, SUB, 6]), m.sb("st2", [P, SUB, 6])
        mv1, mv2 = m.sb("mv1", [P, SUB, 2]), m.sb("mv2", [P, SUB, 2])
        ve1, ve2 = m.sb("ve1", [P, SUB]), m.sb("ve2", [P, SUB])
        sd1, sd2 = m.sb("sd1", [P, SUB]), m.sb("sd2", [P, SUB])
        rs1, rs2 = m.sb("rs1", [P, SUB]), m.sb("rs2", [P, SUB])
        xn = m.sb("xn", [P, SUB, C])
        xm = m.sb("xm", [P, SUB, C])
        xg = m.sb("xg", [P, SUB, C])
        xa = m.sb("xa", [P, SUB, C])
        ht = m.sb("ht", [P, 2, TOK])
        qs = m.sb("qs", [P, 2, TOK])
        ks = m.sb("ks", [P, 2, TOK])
        qv = m.sb("qv", [HD, 2, TOK])
        prod = m.sb("prod", [P, 4, TOK])
        bs = m.sb("bs", [P, 2, TOK])
        qh = m.sb("qh", [P, TOK], F16)
        past = m.sb("past", [P, NH, 2])
        qt_o = m.sb("qt_o", [P, 2, 5, TOK], F16)
        kt_o = m.sb("kt_o", [P, 2, 2, TOK], F16)
        vs = m.sb("vs", [P, SUB, C])
        vt_o = m.sb("vt_o", [P, NH, SUB, 2, HD], F16)
        past_o = m.sb("past_o", [P, NH, 2, 2], F16)
        t_ps = m.psum("t_ps", [P, 2, TOK])
        q_ps = m.psum("q_ps", [P, TOK])
        k_ps = m.psum("k_ps", [P, TOK])
        a_ps = m.psum("a_ps", [P, 2, TOK])
        v_ps = m.psum("v_ps", [P, SUB, C])

        const_in = m.sem("const_in")
        bias_made = m.sem("bias_made")
        x_in = [m.sem(f"x_in{p}") for p in range(2)]
        qk_stored = [m.sem(f"qk_stored{p}") for p in range(2)]
        v_stored, past_stored = m.sem("v_stored"), m.sem("past_stored")
        stats1, mean1, eps1, root1, inv1, norm1 = (m.sem(n) for n in (
            "stats1", "mean1", "eps1", "root1", "inv1", "norm1"))
        stats2, mean2, eps2, root2, inv2, norm2 = (m.sem(n) for n in (
            "stats2", "mean2", "eps2", "root2", "inv2", "norm2"))
        gained, shifted = m.sem("gained"), m.sem("shifted")
        rows_turned, ht_a, ht_b = m.sem("rows_turned"), m.sem("ht_a"), m.sem("ht_b")
        queried, keyed, rotated, valued = m.sem("queried"), m.sem("keyed"), m.sem("rotated"), m.sem("valued")
        qs_made, qv_made, ks_made = m.sem("qs_made"), m.sem("qv_made"), m.sem("ks_made")
        products, bs_made = m.sem("products"), m.sem("bs_made")
        b_hi, c_hi, k_hi, v_hi = m.sem("b_hi"), m.sem("c_hi"), m.sem("k_hi"), m.sem("v_hi")
        b_lo, c_lo, k_lo, v_lo = m.sem("b_lo"), m.sem("c_lo"), m.sem("k_lo"), m.sem("v_lo")
        v_scaled, past_made, past_hi, past_lo = (m.sem(n) for n in ("v_scaled", "past_made", "past_hi", "past_lo"))
        block = ctx.enter_context(nc.Block())
        N_CONST = 22 * 16

        @block.sync
        def _(sp):
            for dst, w in ((wq_sb, wq), (wk_sb, wk)):
                for a in range(2):
                    for c in range(2):
                        sp.dma_start(dst[:, c, :, a, :], w[c * P:(c + 1) * P, :].rearrange("p (h d) -> p h d", h=NH)
                                     ).then_inc(const_in, 16)
            sp.dma_start(wv_sb[:], wv.rearrange("(k p) n -> p k n", p=P)).then_inc(const_in, 16)
            sp.dma_start(wp_sb[:], wpos_t).then_inc(const_in, 16)
            sp.dma_start(turn[:], turn_tab).then_inc(const_in, 16)
            sp.dma_start(ga[:], spread(gamma)).then_inc(const_in, 16)
            sp.dma_start(be[:], spread(beta)).then_inc(const_in, 16)
            sp.dma_start(bvb[:], spread(bv)).then_inc(const_in, 16)
            sp.dma_start(ident[:], identity).then_inc(const_in, 16)
            for dst, vec in ((bq_sb, bq.rearrange("(h d) -> d h", h=NH)), (bk_sb, bk.rearrange("(h d) -> d h", h=NH)),
                             (ub, u_bias.rearrange("h d -> d h")), (vb, v_bias.rearrange("h d -> d h"))):
                for a in range(2 if dst is not vb else 1):
                    sp.dma_start(dst[a * HD:(a + 1) * HD, :], vec, allow_slow_non_contiguous=True
                                 ).then_inc(const_in, 16)
            for s in qk_stored:
                sp.sem_inc(s, 48)
            sp.sem_inc(v_stored, 64)
            sp.sem_inc(past_stored, 16)

            def load(t, par):
                sp.wait_ge(norm1, made_before(t, 2))
                sp.dma_start(x_sb[:, par], rows(x, t * TOK)).then_inc(x_in[par], 16)

            def store(t):
                b, k = t // per_b, t % per_b
                for h in range(NH):
                    n = NH * t + h
                    hp = h % 2
                    q_dst = q_tab[ds(b * NH + h, 1)].rearrange("o p n c -> p (o n) c")
                    sp.wait_ge(b_lo, made(n))
                    sp.wait_ge(c_lo, made(n))
                    sp.dma_start(q_dst[:, :, ds(k * TOK + 1, TOK)], qt_o[:, hp]).then_inc(qk_stored[hp], 16)
                    sp.dma_start(q_dst[:, :, 0:1], qt_o[:, hp, :, TOK - 1:TOK], allow_slow_non_contiguous=True
                                 ).then_inc(qk_stored[hp], 16)
                    sp.wait_ge(k_lo, made(n))
                    sp.dma_start(k_tab[ds(b * NH + h, 1)].rearrange("o p a s -> p (o a) s")[:, :, ds(k * TOK, TOK)],
                                 kt_o[:, hp]).then_inc(qk_stored[hp], 16)
                sp.wait_ge(v_lo, made(t))
                for h in range(NH):
                    sp.dma_start(v_tab[ds(b * NH + h, 1)].rearrange("o p t d -> p (o t) d")[:, ds(k * SUB, SUB), :],
                                 vt_o[:, h].rearrange("p k a d -> p k (a d)")).then_inc(v_stored, 16)
                sp.wait_ge(past_lo, made(t))
                sp.dma_start(q_past[ds(b * NH, NH)].rearrange("h p n o -> p h (n o)"),
                             past_o[:].rearrange("p h a n -> p h (a n)")).then_inc(past_stored, 16)

            load(0, 0)
            load(1, 1)
            with sp.Fori(0, steps // 2 - 1) as i:
                load(2 * i + 2, 0)
                store(2 * i)
                load(2 * i + 3, 1)
                store(2 * i + 1)
            store(steps - 2)
            store(steps - 1)
            for s in qk_stored:
                sp.wait_ge(s, 48 * (2 * steps + 1))
            sp.wait_ge(v_stored, 64 * (steps + 1))
            sp.wait_ge(past_stored, 16 * (steps + 1))

        @block.tensor
        def _(pe):
            for s in (rows_turned, queried, keyed, rotated, valued):
                pe.sem_inc(s, PRIME)
            pe.wait_ge(const_in, N_CONST)

            def query(n, h):
                pe.wait_ge(qv_made, made_before(n, 1))
                for c in range(2):
                    mm = nc.tensor.matmul(q_ps[:], wq_sb[:, c, h].rearrange("p a d -> p (a d)"), ht[:, c],
                                          start=(c == 0), stop=(c == 1))
                mm.then_inc(queried, 1)

            def key(n, h):
                pe.wait_ge(ks_made, made_before(n, 1))
                for c in range(2):
                    mm = nc.tensor.matmul(k_ps[:], wk_sb[:, c, h].rearrange("p a d -> p (a d)"), ht[:, c],
                                          start=(c == 0), stop=(c == 1))
                mm.then_inc(keyed, 1)

            def position(n, h):
                pe.wait_ge(qv_made, made(n))
                pe.wait_ge(products, made_before(n, 1))
                for a in range(2):
                    mm = nc.tensor.matmul(a_ps[:, a], wp_sb[:, h, a], qv[:, h % 2], start=True, stop=True)
                mm.then_inc(rotated, 1)

            def step(t):
                pe.wait_ge(shifted, made(t))
                for k in range(SUB):
                    for c in range(2):
                        tr = nc.tensor.transpose(t_ps[:, c, k * P:(k + 1) * P], xa[:, k, c * P:(c + 1) * P], ident[:])
                tr.then_inc(rows_turned, 1)
                pe.wait_ge(ht_a, made(t))
                pe.wait_ge(ht_b, made(t))
                query(NH * t, 0)
                key(NH * t, 0)
                pe.wait_ge(v_scaled, made_before(t, 1))
                for h in range(NH):
                    n = NH * t + h
                    for c in range(2):
                        mm = nc.tensor.matmul(v_ps[:, h], ht[:, c, h * P:(h + 1) * P], wv_sb[:, c],
                                              start=(c == 0), stop=(c == 1))
                    if h < NH - 1:
                        query(n + 1, h + 1)
                        key(n + 1, h + 1)
                    else:
                        mm.then_inc(valued, 1)
                    position(n, h)

            with pe.Fori(0, steps // 2) as i:
                step(2 * i)
                step(2 * i + 1)

        @block.scalar
        def _(act):
            for s in (root1, root2, ht_a, qs_made, qv_made, ks_made, v_hi):
                act.sem_inc(s, PRIME)
            act.wait_ge(bias_made, 4)

            def roots(t, which):
                eps, inv, root, ve, sd = ((eps1, inv1, root1, ve1, sd1), (eps2, inv2, root2, ve2, sd2))[which]
                act.wait_ge(eps, made(t))
                act.wait_ge(inv, made_before(t, 1))
                nc.scalar.activation(sd[:], ve[:], ACT.Sqrt).then_inc(root, 1)

            def head(n, h):
                hp = h % 2
                act.wait_ge(queried, made(n))
                act.wait_ge(c_lo, made_before(n, 2))
                nc.scalar.activation(qs[:, hp], q_ps[:], ACT.Identity, bias=bqus[:, h:h + 1], scale=Q_SCALE
                                     ).then_inc(qs_made, 1)
                act.wait_ge(rotated, made_before(n, 2))
                nc.scalar.activation(qv[:, hp], q_ps[0:HD], ACT.Identity, bias=bqv[0:HD, h:h + 1]
                                     ).then_inc(qv_made, 1)
                act.wait_ge(keyed, made(n))
                act.wait_ge(k_lo, made_before(n, 2))
                nc.scalar.activation(ks[:, hp], k_ps[:], ACT.Identity, bias=bks[:, h:h + 1], scale=Q_SCALE
                                     ).then_inc(ks_made, 1)

            def step(t, ahead=True):
                act.wait_ge(rows_turned, made(t))
                act.wait_ge(valued, made_before(t, 1))
                act.wait_ge(keyed, NH * t + PRIME)
                nc.scalar.activation(ht[:, 0], t_ps[:, 0], ACT.Copy).then_inc(ht_a, 1)
                for h in range(NH):
                    head(NH * t + h, h)
                    if ahead and h in (1, 2):
                        roots(t + 1, h - 1)
                act.wait_ge(v_scaled, made(t))
                act.wait_ge(v_stored, 64 * (t + 1))
                nc.scalar.activation(vt_o[:, :, :, 0, :], vs[:].rearrange("p k (h d) -> p h k d", h=NH), ACT.Copy
                                     ).then_inc(v_hi, 1)

            roots(0, 0)
            roots(0, 1)
            with act.Fori(0, steps // 2 - 1) as i:
                step(2 * i)
                step(2 * i + 1)
            step(steps - 2)
            step(steps - 1, ahead=False)

        @block.vector
        def _(dve):
            for s in (stats1, mean1, eps1, inv1, norm1, stats2, mean2, eps2, inv2, norm2, ht_b, products, b_hi, c_hi,
                      c_lo, k_hi, v_scaled, past_made, past_hi, past_lo):
                dve.sem_inc(s, PRIME)
            dve.wait_ge(const_in, N_CONST)
            nc.vector.tensor_tensor(bqu[:], bq_sb[:], ub[:], ALU.add).then_inc(bias_made, 1)
            nc.vector.tensor_tensor(bqv[0:HD], bq_sb[0:HD], vb[0:HD], ALU.add)
            nc.vector.tensor_scalar(bvs[:], bvb[:], V_SCALE, None, ALU.mult).then_inc(bias_made, 1)
            nc.vector.tensor_scalar(bks[:], bk_sb[:], Q_SCALE, None, ALU.mult).then_inc(bias_made, 1)
            dve.wait_ge(bias_made, 3)
            nc.vector.tensor_scalar(bqus[:], bqu[:], Q_SCALE, None, ALU.mult).then_inc(bias_made, 1)

            def moments(t, src, st, mv, ve, stats, mean, eps):
                for k in range(SUB):
                    op = nc.vector.bn_stats(st[:, k], src[:, k])
                op.then_inc(stats, 1)
                dve.wait_ge(stats, made(t))
                nc.vector.tensor_copy(spare[:], st[:, 0, 0:1])
                for k in range(SUB):
                    op = nc.vector.bn_aggr(mv[:, k], st[:, k])
                op.then_inc(mean, 1)
                dve.wait_ge(mean, made(t))
                nc.vector.tensor_scalar(ve[:], mv[:, :, 1], 1e-5, None, ALU.add).then_inc(eps, 1)

            def centre(t, dst, src, mv, sd, rs, root, inv, norm):
                dve.wait_ge(root, made(t))
                nc.vector.reciprocal(rs[:], sd[:]).then_inc(inv, 1)
                dve.wait_ge(inv, made(t))
                for k in range(SUB):
                    op = nc.vector.tensor_scalar(dst[:, k], src[:, k], mv[:, k, 0:1], rs[:, k:k + 1],
                                                 ALU.subtract, ALU.mult)
                op.then_inc(norm, 1)

            def norm_a(t, i, par):
                dve.wait_ge(x_in[par], 16 * (i + 1))
                moments(t, x_sb[:, par], st1, mv1, ve1, stats1, mean1, eps1)

            def norm_b(t, par):
                centre(t, xn, x_sb[:, par], mv1, sd1, rs1, root1, inv1, norm1)
                dve.wait_ge(norm1, made(t))
                moments(t, xn, st2, mv2, ve2, stats2, mean2, eps2)

            def norm_c(t):
                dve.wait_ge(gained, made_before(t, 1))
                centre(t, xm, xn, mv2, sd2, rs2, root2, inv2, norm2)

            def head(t, n, h):
                hp = h % 2
                col = (t % per_b) * TOK
                cos, sin = turn[:, 0, ds(col, TOK)], turn[:, 1, ds(col, TOK)]
                dve.wait_ge(qk_stored[hp], 48 * (n // 2 + 1))
                dve.wait_ge(qs_made, made(n))
                dve.wait_ge(c_lo, made_before(n, 1))
                nc.vector.tensor_copy(qt_o[0:HD, hp, 4], qs[0:HD, hp])
                nc.vector.tensor_copy(qh[HD:P], qs[HD:P, hp]).then_inc(c_hi, 1)
                dve.wait_ge(c_hi, made(n))
                nc.vector.tensor_tensor(qt_o[HD:P, hp, 4], qs[HD:P, hp], qh[HD:P], ALU.subtract).then_inc(c_lo, 1)
                dve.wait_ge(ks_made, made(n))
                nc.vector.tensor_copy(kt_o[:, hp, 0], ks[:, hp]).then_inc(k_hi, 1)
                dve.wait_ge(rotated, made(n))
                dve.wait_ge(bs_made, made_before(n, 1))
                dve.wait_ge(past_lo, made_before(t, 1))
                nc.vector.tensor_scalar(past[:, h], a_ps[:, :, TOK - 1], B_SCALE, None, ALU.mult
                                        ).then_inc(past_made, 1)
                nc.vector.tensor_tensor(prod[:, 0], a_ps[:, 0], cos, ALU.mult)
                nc.vector.tensor_tensor(prod[:, 1], a_ps[:, 1], sin, ALU.mult)
                nc.vector.tensor_tensor(prod[:, 2], a_ps[:, 1], cos, ALU.mult)
                nc.vector.tensor_tensor(prod[:, 3], a_ps[:, 0], sin, ALU.mult).then_inc(products, 1)
                dve.wait_ge(bs_made, made(n))
                nc.vector.tensor_copy(qt_o[:, hp, 0:4:2], bs[:]).then_inc(b_hi, 1)

            def step(t, i, par, ahead=True):
                dve.wait_ge(rows_turned, made(t))
                dve.wait_ge(valued, made_before(t, 1))
                dve.wait_ge(keyed, NH * t + PRIME)
                nc.vector.tensor_copy(ht[:, 1], t_ps[:, 1]).then_inc(ht_b, 1)
                for h in range(NH):
                    head(t, NH * t + h, h)
                    if ahead and h == 0:
                        norm_a(t + 1, i + par, 1 - par)
                    if ahead and h == 1:
                        norm_b(t + 1, 1 - par)
                    if ahead and h == 2:
                        norm_c(t + 1)
                dve.wait_ge(valued, made(t))
                dve.wait_ge(v_lo, made_before(t, 1))
                nc.vector.scalar_tensor_tensor(out=vs[:], in0=v_ps[:], scalar=V_SCALE, in1=over_rows(bvs),
                                               op0=ALU.mult, op1=ALU.add).then_inc(v_scaled, 1)
                dve.wait_ge(past_made, NH * (t + 1) + PRIME)
                dve.wait_ge(past_stored, 16 * (t + 1))
                nc.vector.tensor_copy(past_o[:, :, :, 0], past[:]).then_inc(past_hi, 1)
                dve.wait_ge(past_hi, made(t))
                nc.vector.tensor_tensor(past_o[:, :, :, 1], past[:], past_o[:, :, :, 0], ALU.subtract
                                        ).then_inc(past_lo, 1)

            norm_a(0, 0, 0)
            norm_b(0, 0)
            norm_c(0)
            with dve.Fori(0, steps // 2 - 1) as i:
                step(2 * i, i, 0)
                step(2 * i + 1, i, 1)
            step(steps - 2, steps // 2 - 1, 0)
            step(steps - 1, steps // 2 - 1, 1, ahead=False)

        @block.gpsimd
        def _(pool):
            for s in (gained, shifted, bs_made, b_lo, k_lo, v_lo):
                pool.sem_inc(s, PRIME)
            pool.wait_ge(const_in, N_CONST)

            def affine(t):
                pool.wait_ge(norm2, made(t))
                nc.gpsimd.tensor_tensor(xg[:], xm[:], over_rows(ga), ALU.mult).then_inc(gained, 1)
                pool.wait_ge(gained, made(t))
                pool.wait_ge(rows_turned, made_before(t, 1))
                nc.gpsimd.tensor_tensor(xa[:], xg[:], over_rows(be), ALU.add).then_inc(shifted, 1)

            def head(n, h):
                hp = h % 2
                pool.wait_ge(k_hi, made(n))
                nc.gpsimd.tensor_tensor(kt_o[:, hp, 1], ks[:, hp], kt_o[:, hp, 0], ALU.subtract).then_inc(k_lo, 1)
                pool.wait_ge(products, made(n))
                pool.wait_ge(b_hi, made_before(n, 1))
                pool.wait_ge(b_lo, made_before(n, 1))
                nc.gpsimd.tensor_tensor(bs[:, 0], prod[:, 0], prod[:, 1], ALU.add)
                nc.gpsimd.tensor_tensor(bs[:, 1], prod[:, 2], prod[:, 3], ALU.subtract).then_inc(bs_made, 1)
                pool.wait_ge(b_hi, made(n))
                nc.gpsimd.tensor_tensor(qt_o[:, hp, 1:4:2], bs[:], qt_o[:, hp, 0:4:2], ALU.subtract).then_inc(b_lo, 1)

            def step(t, ahead=True):
                for h in range(NH):
                    head(NH * t + h, h)
                if ahead:
                    affine(t + 1)
                pool.wait_ge(v_hi, made(t))
                nc.gpsimd.tensor_tensor(vt_o[:, :, :, 1, :], vs[:].rearrange("p k (h d) -> p h k d", h=NH),
                                        vt_o[:, :, :, 0, :], ALU.subtract).then_inc(v_lo, 1)

            affine(0)
            with pool.Fori(0, steps // 2 - 1) as i:
                step(2 * i)
                step(2 * i + 1)
            step(steps - 2)
            step(steps - 1, ahead=False)


def ffn_phase(nc, batches, seq, x, ctx_in, w_out, b_out, wr, br, ff1_w, ff1_b, ff2_w, ff2_b, identity, prefix, out):
    per_b = seq // TOK
    steps = batches * per_b
    tiles = batches * seq // P
    bt = seq // P
    keep = seq // 2 - 1
    F = ff1_w.shape[1]
    MF = F // P
    CH = MF // 2
    with ExitStack() as ctx:
        m = Mem(nc, ctx, "ffn")
        z0 = m.sb("z0", [P, tiles * C])
        z1 = m.sb("z1", [P, tiles * C])
        wo = m.sb("wo", [P, 2, C])
        w1 = m.sb("w1", [P, 2, F])
        w2 = m.sb("w2", [P, MF, C])
        bo = m.sb("bo", [P, C])
        b1 = m.sb("b1", [P, MF])
        b2 = m.sb("b2", [P, C])
        wrb = m.sb("wrb", [P, C])
        brb = m.sb("brb", [P, 1])
        ident = m.sb("id", [P, P])
        pre = m.sb("pre", [P, 2 * P])
        c_sb = m.sb("c", [P, SUB, C])
        x_sb = m.sb("x", [P, SUB, C])
        xb = m.sb("xb", [P, SUB, C])
        t1 = m.sb("t1", [P, SUB, C])
        xf = m.sb("xf", [P, SUB, C])
        junk = m.sb("junk", [P, SUB, C])
        st = m.sb("st", [P, SUB, 6])
        mv = m.sb("mv", [P, SUB, 2])
        ve, sd, rs = m.sb("ve", [P, SUB]), m.sb("sd", [P, SUB]), m.sb("rs", [P, SUB])
        w_row = m.sb("w_row", [P, SUB])
        spare = m.sb("spare", [P, 1])
        w_all = m.sb("w_all", [P, tiles])
        ct = m.sb("ct", [P, 2, TOK])
        nt = m.sb("nt", [P, 2, TOK])
        gt = m.sb("gt", [P, MF, TOK])
        t_ps = m.psum("t_ps", [P, 2, TOK])
        f_ps = m.psum("f_ps", [P, 4, TOK])
        p_ps = m.psum("p_ps", [P, SUB, C])

        const_in, rows_in, wrapped = m.sem("const_in"), m.sem("rows_in"), m.sem("wrapped")
        ctx_turned, ct_a, ct_b, projected = m.sem("ctx_turned"), m.sem("ct_a"), m.sem("ct_b"), m.sem("projected")
        xb_made, t1_made, stats, mean = m.sem("xb_made"), m.sem("t1_made"), m.sem("stats"), m.sem("mean")
        eps, root, inv, normed = m.sem("eps"), m.sem("root"), m.sem("inv"), m.sem("normed")
        z0_made, routed, weighted = m.sem("z0_made"), m.sem("routed"), m.sem("weighted")
        rows_turned, nt_a, nt_b = m.sem("rows_turned"), m.sem("nt_a"), m.sem("nt_b")
        widened, gated, narrowed, z1_made = m.sem("widened"), m.sem("gated"), m.sem("narrowed"), m.sem("z1_made")
        step_done, counted, chosen, stored = m.sem("sel_step"), m.sem("counted"), m.sem("chosen"), m.sem("stored")
        out_made = m.sem("out_made")

        ke = m.sb("ke", [P, batches, bt], U32)
        fl = m.sb("fl", [P, batches, bt], U32)
        hb = m.sb("hb", [P, batches, bt], U32)
        lb = m.sb("lb", [P, batches, bt], U32)
        hi = m.sb("hi", [P, batches, bt])
        lo = m.sb("lo", [P, batches, bt])
        cmp_ = m.sb("cmp", [P, batches, bt])
        over = m.sb("over", [P, batches, bt])
        tie = m.sb("tie", [P, batches, bt])
        low_key = m.sb("low_key", [P, batches, bt])
        pad = bt
        scan = m.sb("scan", [P, 2, batches, pad + bt])
        cur = m.sb("cur", [P, 2, batches])
        cand = m.sb("cand", [P, batches])
        bit = m.sb("bit", [P, 2])
        cnt = m.sb("cnt", [P, batches])
        inc = m.sb("inc", [P, batches])
        want = m.sb("want", [P, 3, batches])
        fac = m.sb("fac", [P, tiles])
        block = ctx.enter_context(nc.Block())
        N_CONST = 11 * 16

        @block.sync
        def _(sp):
            for dst, src in ((wo[:], w_out.rearrange("(k p) n -> p k n", p=P)),
                             (w1[:], ff1_w.rearrange("(k p) n -> p k n", p=P)),
                             (w2[:], ff2_w.rearrange("(k p) n -> p k n", p=P)), (bo[:], spread(b_out)),
                             (b2[:], spread(ff2_b)), (wrb[:], spread(wr)), (brb[:], spread(br)),
                             (ident[:], identity), (pre[:], prefix)):
                sp.dma_start(dst, src).then_inc(const_in, 16)
            sp.dma_start(b1[:], columns(ff1_b), allow_slow_non_contiguous=True).then_inc(const_in, 16)
            sp.dma_start(ctx_in[:, seq, :], ctx_in[:, 0, :]).then_inc(const_in, 16)
            sp.wait_ge(const_in, N_CONST)

            def load(t):
                sp.wait_ge(ctx_turned, made_before(t, 1))
                sp.wait_ge(xb_made, made_before(t, 1))
                first = (t // per_b) * (seq + 1) + (t % per_b) * TOK + 1
                sp.dma_start(c_sb[:], rows(ctx_in.rearrange("b r c -> (b r) c"), first)).then_inc(rows_in, 16)
                sp.dma_start(x_sb[:], rows(x, t * TOK)).then_inc(rows_in, 16)

            with sp.Fori(0, steps) as t:
                load(t)
            with sp.Fori(0, steps) as t:
                sp.wait_ge(out_made, t + 1)
                sp.dma_start(rows(out, t * TOK), z0[:, ds(t * (SUB * C), SUB * C)].rearrange(
                    "p (k c) -> p k c", k=SUB)).then_inc(stored, 16)
            sp.wait_ge(stored, 16 * steps)

        @block.tensor
        def _(pe):
            for s in (ctx_turned, projected, rows_turned, narrowed):
                pe.sem_inc(s, PRIME)
            pe.sem_inc(widened, 2 * CH)
            pe.wait_ge(const_in, N_CONST)

            def project(t):
                pe.wait_ge(rows_in, 32 * (t + 1))
                pe.wait_ge(nt_a, made_before(t, 1))
                pe.wait_ge(nt_b, made_before(t, 1))
                for k in range(SUB):
                    for c in range(2):
                        tr = nc.tensor.transpose(t_ps[:, c, k * P:(k + 1) * P], c_sb[:, k, c * P:(c + 1) * P], ident[:])
                tr.then_inc(ctx_turned, 1)
                pe.wait_ge(ct_a, made(t))
                pe.wait_ge(ct_b, made(t))
                pe.wait_ge(z1_made, made_before(t, 2))
                for k in range(SUB):
                    for c in range(2):
                        mm = nc.tensor.matmul(p_ps[:, k], ct[:, c, k * P:(k + 1) * P], wo[:, c],
                                              start=(c == 0), stop=(c == 1))
                mm.then_inc(projected, 1)

            def widen(t):
                pe.wait_ge(normed, made(t))
                for k in range(SUB):
                    for c in range(2):
                        tr = nc.tensor.transpose(t_ps[:, c, k * P:(k + 1) * P], xf[:, k, c * P:(c + 1) * P], ident[:])
                tr.then_inc(rows_turned, 1)
                pe.wait_ge(nt_a, made(t))
                pe.wait_ge(nt_b, made(t))
                for q in range(CH):
                    pe.wait_ge(gated, CH * t + q - 1 + 2 * CH)
                    for o in range(2):
                        for c in range(2):
                            mm = nc.tensor.matmul(f_ps[:, 2 * (q % 2) + o], w1[:, c, (2 * q + o) * P:(2 * q + o + 1) * P],
                                                  nt[:, c], start=(c == 0), stop=(c == 1))
                    mm.then_inc(widened, 1)

            def narrow(t):
                pe.wait_ge(gated, CH * (t + 1) + 2 * CH)
                for k in range(SUB):
                    for c in range(MF):
                        mm = nc.tensor.matmul(p_ps[:, k], gt[:, c, k * P:(k + 1) * P], w2[:, c],
                                              start=(c == 0), stop=(c == MF - 1))
                mm.then_inc(narrowed, 1)

            def step(t, ahead=True):
                widen(t)
                if ahead:
                    project(t + 1)
                    pe.wait_ge(t1_made, made(t + 1))
                narrow(t)

            project(0)
            with pe.Fori(0, steps - 1) as t:
                step(t)
            step(steps - 1, ahead=False)

            ones = pre[:, P:2 * P]
            with pe.Fori(0, 33) as n:
                pe.wait_ge(counted, n + 1)
                nc.tensor.matmul(t_ps[:, 0, 0:batches], ones, cnt[:], start=True, stop=True).then_inc(chosen, 1)
            pe.wait_ge(counted, 34)
            nc.tensor.matmul(t_ps[:, 0, 0:batches], ones, cnt[:], start=True, stop=True).then_inc(chosen, 1)
            tie_rows = tie[:].rearrange("p b t -> p (b t)")
            nc.tensor.matmul(t_ps[:, 1, 0:tiles], pre[:, 0:P], tie_rows, start=True, stop=True)
            nc.tensor.matmul(p_ps[:, 0, 0:tiles], ones, tie_rows, start=True, stop=True).then_inc(chosen, 1)

        @block.gpsimd
        def _(pool):
            for s in (xb_made, z0_made):
                pool.sem_inc(s, PRIME)
            pool.wait_ge(const_in, N_CONST)
            with pool.Fori(0, steps) as t:
                pool.wait_ge(rows_in, 32 * (t + 1))
                pool.wait_ge(t1_made, made_before(t, 1))
                nc.gpsimd.tensor_tensor(xb[:], x_sb[:], over_rows(bo), ALU.add).then_inc(xb_made, 1)
                pool.wait_ge(normed, made(t))
                nc.gpsimd.tensor_tensor(z0[:, ds(t * (SUB * C), SUB * C)].rearrange("p (k c) -> p k c", k=SUB),
                                        t1[:], xf[:], ALU.add).then_inc(z0_made, 1)

        @block.scalar
        def _(act):
            for s in (ct_a, root, nt_a):
                act.sem_inc(s, PRIME)
            act.sem_inc(gated, 2 * CH)
            act.wait_ge(const_in, N_CONST)

            def first_half(t):
                act.wait_ge(ctx_turned, made(t))
                act.wait_ge(projected, made_before(t, 1))
                nc.scalar.activation(ct[:, 0], t_ps[:, 0], ACT.Copy).then_inc(ct_a, 1)
                act.wait_ge(eps, made(t))
                act.wait_ge(inv, made_before(t, 1))
                nc.scalar.activation(sd[:], ve[:], ACT.Sqrt).then_inc(root, 1)

            def step(t, ahead=True):
                act.wait_ge(rows_turned, made(t))
                act.wait_ge(widened, CH * t + 2 * CH)
                nc.scalar.activation(nt[:, 0], t_ps[:, 0], ACT.Copy).then_inc(nt_a, 1)
                act.wait_ge(narrowed, made_before(t, 1))
                for q in range(CH):
                    act.wait_ge(widened, CH * t + q + 1 + 2 * CH)
                    for o in range(2):
                        ge = nc.scalar.activation(gt[:, 2 * q + o], f_ps[:, 2 * (q % 2) + o], ACT.Gelu_apprx_tanh,
                                                  bias=b1[:, 2 * q + o:2 * q + o + 1])
                    ge.then_inc(gated, 1)
                if ahead:
                    first_half(t + 1)

            first_half(0)
            with act.Fori(0, steps - 1) as t:
                step(t)
            step(steps - 1, ahead=False)

        @block.vector
        def _(dve):
            for s in (ct_b, t1_made, stats, mean, eps, inv, normed, routed, weighted, nt_b, z1_made):
                dve.sem_inc(s, PRIME)
            dve.wait_ge(const_in, N_CONST)

            def first_half(t):
                dve.wait_ge(ctx_turned, made(t))
                dve.wait_ge(projected, made_before(t, 1))
                nc.vector.tensor_copy(ct[:, 1], t_ps[:, 1]).then_inc(ct_b, 1)
                dve.wait_ge(projected, made(t))
                dve.wait_ge(xb_made, made(t))
                dve.wait_ge(z0_made, made_before(t, 1))
                nc.vector.tensor_tensor(t1[:], p_ps[:], xb[:], ALU.add).then_inc(t1_made, 1)
                dve.wait_ge(t1_made, made(t))
                for k in range(SUB):
                    op = nc.vector.bn_stats(st[:, k], t1[:, k])
                op.then_inc(stats, 1)
                dve.wait_ge(stats, made(t))
                nc.vector.tensor_copy(spare[:], st[:, 0, 0:1])
                for k in range(SUB):
                    op = nc.vector.bn_aggr(mv[:, k], st[:, k])
                op.then_inc(mean, 1)
                dve.wait_ge(mean, made(t))
                nc.vector.tensor_scalar(ve[:], mv[:, :, 1], 1e-5, None, ALU.add).then_inc(eps, 1)
                dve.wait_ge(root, made(t))
                nc.vector.reciprocal(rs[:], sd[:]).then_inc(inv, 1)
                dve.wait_ge(inv, made(t))
                dve.wait_ge(rows_turned, made_before(t, 1))
                for k in range(SUB):
                    op = nc.vector.tensor_scalar(xf[:, k], t1[:, k], mv[:, k, 0:1], rs[:, k:k + 1],
                                                 ALU.subtract, ALU.mult)
                op.then_inc(normed, 1)
                dve.wait_ge(normed, made(t))
                for k in range(SUB):
                    op = nc.vector.tensor_tensor_reduce(out=junk[:, k], in0=xf[:, k], in1=wrb[:], scale=1.0, scalar=0.0,
                                                        op0=ALU.mult, op1=ALU.add, accum_out=w_row[:, k:k + 1])
                op.then_inc(routed, 1)
                dve.wait_ge(routed, made(t))
                nc.vector.tensor_scalar(w_all[:, ds(t * SUB, SUB)], w_row[:], brb[:, 0:1], None, ALU.add
                                        ).then_inc(weighted, 1)

            def step(t, ahead=True):
                dve.wait_ge(rows_turned, made(t))
                dve.wait_ge(widened, CH * t + 2 * CH)
                nc.vector.tensor_copy(nt[:, 1], t_ps[:, 1]).then_inc(nt_b, 1)
                if ahead:
                    first_half(t + 1)
                dve.wait_ge(narrowed, made(t))
                nc.vector.tensor_tensor(z1[:, ds(t * (SUB * C), SUB * C)].rearrange("p (k c) -> p k c", k=SUB),
                                        p_ps[:], over_rows(b2), ALU.add).then_inc(z1_made, 1)

            first_half(0)
            with dve.Fori(0, steps - 1) as t:
                step(t)
            step(steps - 1, ahead=False)

            done = [0]

            def chained(ins):
                done[0] += 1
                ins.then_inc(step_done, 1)
                dve.wait_ge(step_done, done[0])

            dve.wait_ge(weighted, made(steps - 1))
            wv = w_all[:].rearrange("p (b t) -> p b t", b=batches)
            chained(nc.vector.tensor_scalar(fl[:].bitcast(mybir.dt.int32), wv.bitcast(mybir.dt.int32), 31, -2 ** 31,
                                            ALU.arith_shift_right, ALU.bitwise_or))
            chained(nc.vector.tensor_tensor(ke[:], wv.bitcast(U32), fl[:], ALU.bitwise_xor))
            nc.vector.tensor_scalar(hb[:], ke[:], 16, None, ALU.logical_shift_right)
            chained(nc.vector.tensor_scalar(lb[:], ke[:], 65535, None, ALU.bitwise_and))
            nc.vector.tensor_copy(hi[:], hb[:])
            nc.vector.tensor_copy(lo[:], lb[:])
            nc.vector.memset(want[:, 0], float(keep))
            nc.vector.memset(bit[:], 32768.0)
            nc.vector.memset(scan[:], 0.0)
            chained(nc.vector.memset(cur[:], 0.0))

            def count(key, op, least, base=None):
                for b in range(batches):
                    ins = nc.vector.tensor_scalar(cmp_[:, b], key[:, b], least[:, b:b + 1], 0.0, op, ALU.add,
                                                  accum_out=cnt[:, b:b + 1])
                ins.then_inc(counted, 1)

            first_loop = done[0]

            def largest(key, half, first):
                start = done[0]
                with dve.Fori(0, 16) as n:
                    base = start + 3 * n
                    nc.vector.tensor_scalar(cand[:], cur[:, half], bit[:, half:half + 1], None, ALU.add
                                            ).then_inc(step_done, 1)
                    dve.wait_ge(step_done, base + 1)
                    count(key, ALU.is_ge, cand)
                    dve.wait_ge(chosen, first + n + 1)
                    nc.vector.tensor_tensor(inc[:], t_ps[:, 0, 0:batches], want[:, half], ALU.is_ge
                                            ).then_inc(step_done, 1)
                    dve.wait_ge(step_done, base + 2)
                    nc.vector.scalar_tensor_tensor(out=cur[:, half], in0=inc[:], scalar=bit[:, half:half + 1],
                                                   in1=cur[:, half], op0=ALU.mult, op1=ALU.add)
                    nc.vector.tensor_scalar(bit[:, half:half + 1], bit[:, half:half + 1], 0.5, None, ALU.mult
                                            ).then_inc(step_done, 1)
                    dve.wait_ge(step_done, base + 3)
                done[0] += 48

            largest(hi, 0, 0)
            count(hi, ALU.is_gt, cur[:, 0])
            for b in range(batches):
                nc.vector.tensor_scalar(over[:, b], hi[:, b], cur[:, 0, b:b + 1], None, ALU.is_gt)
                op = nc.vector.tensor_scalar(tie[:, b], hi[:, b], cur[:, 0, b:b + 1], None, ALU.is_equal)
            chained(op)
            chained(nc.vector.scalar_tensor_tensor(out=low_key[:], in0=lo[:], scalar=1.0, in1=tie[:],
                                                   op0=ALU.add, op1=ALU.mult))
            chained(nc.vector.tensor_scalar(low_key[:], low_key[:], -1.0, None, ALU.add))
            dve.wait_ge(chosen, 17)
            chained(nc.vector.tensor_tensor(want[:, 1], want[:, 0], t_ps[:, 0, 0:batches], ALU.subtract))
            largest(low_key, 1, 17)
            for b in range(batches):
                nc.vector.tensor_scalar(tie[:, b], low_key[:, b], cur[:, 1, b:b + 1], None, ALU.is_equal)
            count(low_key, ALU.is_gt, cur[:, 1])
            dve.wait_ge(counted, 34)
            chained(nc.vector.tensor_tensor(over[:], over[:], cmp_[:], ALU.add))
            dve.wait_ge(chosen, 35)
            chained(nc.vector.tensor_tensor(want[:, 2], want[:, 1], t_ps[:, 0, 0:batches], ALU.subtract))
            tot = p_ps[:, 0, 0:tiles].rearrange("p (b t) -> p b t", b=batches)
            chained(nc.vector.tensor_copy(scan[:, 0, :, pad:], tot))
            side, d = 0, 1
            while d < bt:
                chained(nc.vector.tensor_tensor(scan[:, 1 - side, :, pad:], scan[:, side, :, pad:],
                                                scan[:, side, :, pad - d:pad + bt - d], ALU.add))
                side, d = 1 - side, 2 * d
            rank = low_key
            chained(nc.vector.tensor_tensor(rank[:], scan[:, side, :, pad:], tot, ALU.subtract))
            chained(nc.vector.tensor_tensor(rank[:], rank[:], t_ps[:, 1, 0:tiles].rearrange(
                "p (b t) -> p b t", b=batches), ALU.add))
            for b in range(batches):
                op = nc.vector.tensor_scalar(cmp_[:, b], rank[:, b], want[:, 2, b:b + 1], None, ALU.is_le)
            chained(op)
            chained(nc.vector.tensor_tensor(tie[:], tie[:], cmp_[:], ALU.mult))
            chained(nc.vector.tensor_tensor(over[:], over[:], tie[:], ALU.add))
            chained(nc.vector.tensor_tensor(fac[:].rearrange("p (b t) -> p b t", b=batches), over[:], wv, ALU.mult))
            dve.wait_ge(z0_made, made(steps - 1))
            dve.wait_ge(z1_made, made(steps - 1))
            with dve.Fori(0, steps) as t:
                for k in range(SUB):
                    tile = ds(t * (SUB * C) + k * C, C)
                    op = nc.vector.scalar_tensor_tensor(out=z0[:, tile], in0=z1[:, tile],
                                                        scalar=fac[:, ds(t * SUB + k, 1)], in1=z0[:, tile],
                                                        op0=ALU.mult, op1=ALU.add)
                op.then_inc(out_made, 1)


def flash_phase(nc, seq, heads, q_tab, q_past, k_tab, v_tab, pe_tab, diag_masks, identity, ctx_out):
    tiles = seq // P
    blocks = seq // 512
    spi = seq // 1024
    n_tiles = heads * tiles
    dim = 256
    sc = 1.0 / (math.sqrt(dim) * SCORE_SCALE)

    with ExitStack() as ctx:
        def sb(name, shape, dt):
            return ctx.enter_context(nc.sbuf_tensor(name, shape, dt))

        def psum(name, shape):
            return ctx.enter_context(nc.psum_tensor(name, shape, F32))

        def sem(name):
            return ctx.enter_context(nc.semaphore(name))

        pe_sb = sb("pe_sb", [P, 2, 2, 2 * seq], F16)
        k_sb = sb("k_sb", [P, 2 * 2 * seq], F16)
        v_sb = sb("v_sb", [P, 2 * tiles * P], F16)
        q_sb = sb("q_sb", [P, 2, 9 * P], F16)
        mask_sb = sb("mask_sb", [P, 2 * 256], F32)
        id_sb = sb("fid_sb", [P, P], F32)
        p_sb = sb("p_sb", [P, 2, 1024], F32)
        hi_sb = sb("hi_sb", [P, 2, 8, P], F16)
        lo_sb = sb("lo_sb", [P, 2, 8, P], F16)
        dmask = sb("dmask", [P, 256], F32)
        dsum = sb("dsum", [P, P], F32)
        NS = 2 * spi
        blk_max = sb("blk_max", [P, NS], F32)
        run_max = sb("run_max", [P, NS], F32)
        max_step = sb("max_step", [P, NS], F32)
        neg_max = sb("neg_max", [P, NS], F32)
        corr = sb("corr", [P, NS], F32)
        row_sum = sb("row_sum", [P, NS], F32)
        tot = sb("tot", [P, NS], F32)
        o_acc = sb("o_acc", [P, NS, P], F32)
        o_sum = sb("o_sum", [P, 64], F32)
        r_tot = sb("r_tot", [P, 1], F32)
        o_out = sb("o_out", [P, 2, 64], F32)

        s_ps = psum("s_ps", [P, 2, 1024])
        t_ps = psum("t_ps", [P, 8, P])
        o_ps = psum("o_ps", [P, 512])
        d_ps = psum("d_ps", [P, 512])

        const_in = sem("f_const_in")
        q_in = [sem(f"f_q_in{p}") for p in range(2)]
        kv_in = sem("f_kv_in")
        scored = sem("f_scored")
        exped = sem("f_exped")
        turned = sem("f_turned")
        hi_made = sem("f_hi_made")
        lo_made = sem("f_lo_made")
        pv_made = sem("f_pv_made")
        maxed = sem("f_maxed")
        o_added = sem("f_o_added")
        diag_read = sem("f_diag_read")
        ctx_made = sem("f_ctx_made")
        stored = sem("f_stored")
        out_free = sem("f_out_free")
        dve_step = sem("f_dve_step")
        fin_step = sem("f_fin_step")

        def head_of(g):
            return g // tiles

        def over_tiles(eng, query_tile):
            with eng.Fori(0, n_tiles // 4 - 1) as q4:
                for r in range(4):
                    query_tile(4 * q4 + r, r)
            for r in range(4):
                query_tile(n_tiles - 4 + r, r, last=r == 3)

        block = ctx.enter_context(nc.Block())

        @block.sync
        def _(sp):
            sp.dma_start(pe_sb[:], pe_tab).then_inc(const_in, 16)
            sp.dma_start(mask_sb[:], diag_masks).then_inc(const_in, 16)
            sp.dma_start(id_sb[:], identity).then_inc(const_in, 16)

            def load_kv(h):
                par = h % 2
                sp.dma_start(k_sb[:, ds(par * (2 * seq), 2 * seq)],
                             k_tab[ds(h, 1)].rearrange("o p a s -> p (o a s)")).then_inc(kv_in, 16)
                sp.dma_start(v_sb[:, ds(par * (tiles * P), tiles * P)],
                             v_tab[ds(h, 1)].rearrange("o p t d -> p (o t d)")).then_inc(kv_in, 16)

            def load_q(g, par, first=False):
                sp.wait_ge(scored, spi * g + PRIME)
                h, i = g // tiles, g % tiles
                q = q_sb[:, par, :].rearrange("p (n c) -> p n c", c=P)
                src = q_tab[ds(h, 1)].rearrange("o p n c -> p (o n) c")
                if first:
                    sp.dma_start(q[:, 0:4, 1:P], src[:, 0:4, 2:P + 1]).then_inc(q_in[par], 16)
                    sp.dma_start(q[:, 0:4, 0:1], q_past[ds(h, 1)].rearrange("o p n c -> p (o n) c"),
                                 allow_slow_non_contiguous=True).then_inc(q_in[par], 16)
                    sp.dma_start(q[:, 4:9, :], src[:, :, 0:P]).then_inc(q_in[par], 16)
                else:
                    sp.dma_start(q[:, 0:4, :], src[:, 0:4, ds(i * P + 1, P)]).then_inc(q_in[par], 16)
                    sp.dma_start(q[:, 4:8, :], src[:, 0:4, ds(i * P, P)]).then_inc(q_in[par], 16)
                    sp.dma_start(q[:, 8:9, :], src[:, 4:5, ds(i * P, P)]).then_inc(q_in[par], 16)

            load_kv(0)
            with sp.Fori(0, heads - 1) as h:
                g0 = h * tiles
                load_q(g0, 0, first=True)
                load_q(g0 + 1, 1)
                load_q(g0 + 2, 0)
                load_q(g0 + 3, 1)
                sp.wait_ge(pv_made, spi * g0 + PRIME)
                sp.wait_ge(kv_in, 32 * (h + 1))
                load_kv(h + 1)
                with sp.Fori(2, tiles // 2) as i2:
                    load_q(g0 + 2 * i2, 0)
                    load_q(g0 + 2 * i2 + 1, 1)
            load_q((heads - 1) * tiles, 0, first=True)
            load_q((heads - 1) * tiles + 1, 1)
            with sp.Fori(1, tiles // 2) as i2:
                load_q((heads - 1) * tiles + 2 * i2, 0)
                load_q((heads - 1) * tiles + 2 * i2 + 1, 1)

        @block.tensor
        def _(pe):
            pe.sem_inc(scored, PRIME + spi)
            pe.sem_inc(turned, PRIME)
            pe.sem_inc(pv_made, PRIME)
            pe.wait_ge(const_in, 48)

            def scores(g, r, s, half):
                h = head_of(g)
                par = r % 2
                i4 = (g % tiles) // 4
                kb = (h % 2) * (2 * seq)
                j = 2 * s + half
                out = s_ps[:, s % 2, half * 512:(half + 1) * 512]
                q = q_sb[:, par, :]
                content = q[:, 8 * P:9 * P]

                def part(sel, n):
                    if isinstance(sel, int):
                        return q[:, sel * 512 + n * P:sel * 512 + (n + 1) * P]
                    return q_sb[:, par, ds(sel * 512 + n * P, P)]

                def position(to, sel, first, n_keys, start=False):
                    for a in range(2):
                        for n, b in ((0, 0), (1, 0), (0, 1)):
                            mm = nc.tensor.matmul(to, part(sel, 2 * a + n), pe_sb[:, a, b, ds(first, n_keys)],
                                                  start=start and a + n + b == 0, stop=a == 1 and b == 1,
                                                  skip_group_check=True)
                    return mm

                if s == 0 and half == 0:
                    pe.wait_ge(q_in[par], 48 * (g // 2 + 1))
                    pe.wait_ge(kv_in, 32 * (h + 1))
                    col = i4 * 512
                    for a in range(2):
                        nc.tensor.matmul(out, content, k_sb[:, ds(kb + a * seq + col, 512)],
                                         start=(a == 0), stop=(a == 1), skip_group_check=True)
                    if r < 3:
                        position(out[:, (r + 1) * P:512], 0, col + (r + 1) * P, (3 - r) * P)
                    if r > 0:
                        position(out[:, 0:r * P], 1, col + seq, r * P)
                    pe.wait_ge(diag_read, made_before(g, 1))
                    for sel in (1, 0):
                        position(d_ps[:, (1 - sel) * P:(2 - sel) * P], sel, col + r * P + sel * seq, P, start=True)
                    return None
                col = ((i4 + j) % blocks) * 512
                past = (i4 + j) >= blocks
                for a in range(2):
                    nc.tensor.matmul(out, content, k_sb[:, ds(kb + a * seq + col, 512)],
                                     start=(a == 0), stop=False, skip_group_check=True)
                mm = position(out, past, (i4 + j) * 512, 512)
                return mm

            def turn(n, s):
                pe.wait_ge(exped, made(n))
                pe.wait_ge(lo_made, made_before(n, 1))
                for k in range(8):
                    tr = nc.tensor.transpose(t_ps[:, k, :], p_sb[:, s % 2, k * P:(k + 1) * P], id_sb[:])
                tr.then_inc(turned, 1)

            def weigh(g, n, s):
                h = head_of(g)
                i4 = (g % tiles) // 4
                vb = (h % 2) * (tiles * P)
                pe.wait_ge(hi_made, made(n))
                pe.wait_ge(o_added, made_before(n, 1))

                def tile_of(k):
                    return ((i4 + 2 * s + k // 4) % blocks) * 4 + k % 4

                for k in range(8):
                    nc.tensor.matmul(o_ps[:, 0:P], hi_sb[:, s % 2, k, :], v_sb[:, ds(vb + tile_of(k) * P, P)],
                                     start=(k == 0), stop=False, skip_group_check=True)
                pe.wait_ge(lo_made, made(n))
                for k in range(8):
                    mm = nc.tensor.matmul(o_ps[:, 0:64], lo_sb[:, s % 2, k, :], v_sb[:, ds(vb + tile_of(k) * P, 64)],
                                          start=False, stop=(k == 7), skip_group_check=True)
                mm.then_inc(pv_made, 1)

            def query_tile(g, r, last=False):
                for s in range(spi):
                    n = spi * g + s
                    turn(n, s)
                    ahead, s2 = (s + 2) // spi, (s + 2) % spi
                    if not (last and ahead):
                        scores(g + ahead, (r + ahead) % 4, s2, 0)
                        scores(g + ahead, (r + ahead) % 4, s2, 1).then_inc(scored, 1)
                    weigh(g, n, s)

            for s in range(2):
                scores(s // spi, s // spi, s % spi, 0)
                scores(s // spi, s // spi, s % spi, 1).then_inc(scored, 1)
            over_tiles(pe, query_tile)

        @block.vector
        def _(dve):
            for s_ in (lo_made, maxed, o_added, diag_read, ctx_made):
                dve.sem_inc(s_, PRIME)
            dve.wait_ge(const_in, 48)

            def row_max(g, r, s):
                par = r % 2
                n = spi * g + s
                x = par * spi + s
                base = CHAIN * g
                dve.wait_ge(scored, n + 1 + PRIME + spi)
                if s == 0:
                    variant = (g % tiles) < 1
                    nc.vector.tensor_tensor(dmask[:], d_ps[:, 0:256], mask_sb[:, ds(variant * 256, 256)],
                                            ALU.mult).then_inc(diag_read, 1)
                    dve.wait_ge(diag_read, made(g))
                    nc.vector.tensor_tensor(dsum[:], dmask[:, 0:P], dmask[:, P:2 * P],
                                            ALU.add).then_inc(dve_step, 1)
                    dve.wait_ge(dve_step, base + 1)
                    nc.vector.tensor_tensor(s_ps[:, 0, r * P:(r + 1) * P], s_ps[:, 0, r * P:(r + 1) * P], dsum[:],
                                            ALU.add).then_inc(dve_step, 1)
                    dve.wait_ge(dve_step, base + 2)
                    nc.vector.tensor_reduce(run_max[:, x:x + 1], s_ps[:, s % 2, :], AX_X, ALU.max).then_inc(dve_step, 1)
                    dve.wait_ge(dve_step, base + 3)
                else:
                    nc.vector.tensor_reduce(blk_max[:, x:x + 1], s_ps[:, s % 2, :], AX_X, ALU.max).then_inc(dve_step, 1)
                    dve.wait_ge(dve_step, base + 3 + 2 * s - 1)
                    nc.vector.tensor_tensor(run_max[:, x:x + 1], blk_max[:, x:x + 1], run_max[:, x - 1:x],
                                            ALU.max).then_inc(dve_step, 1)
                    dve.wait_ge(dve_step, base + 3 + 2 * s)
                if s:
                    nc.vector.tensor_tensor(max_step[:, x:x + 1], run_max[:, x - 1:x], run_max[:, x:x + 1],
                                            ALU.subtract)
                nc.vector.tensor_scalar(neg_max[:, x:x + 1], run_max[:, x:x + 1], -sc, math.log(P_SCALE),
                                        ALU.mult, ALU.add).then_inc(maxed, 1)

            CHAIN = 3 + 2 * (spi - 1)

            def low_part(n, s):
                dve.wait_ge(hi_made, made(n))
                dve.wait_ge(pv_made, made_before(n, 2))
                nc.vector.tensor_tensor(lo_sb[:, s % 2, :, :], t_ps[:], hi_sb[:, s % 2, :, :],
                                        ALU.subtract).then_inc(lo_made, 1)

            def add_output(g, par, s):
                n = spi * g + s
                x = par * spi + s
                dve.wait_ge(exped, made(n))
                dve.wait_ge(pv_made, made(n))
                if s:
                    dve.wait_ge(o_added, made_before(n, 1))
                    nc.vector.scalar_tensor_tensor(out=tot[:, x:x + 1], in0=tot[:, x - 1:x], scalar=corr[:, x:x + 1],
                                                   in1=row_sum[:, x:x + 1], op0=ALU.mult, op1=ALU.add)
                    nc.vector.scalar_tensor_tensor(out=o_acc[:, x, :], in0=o_acc[:, x - 1, :], scalar=corr[:, x:x + 1],
                                                   in1=o_ps[:, 0:P], op0=ALU.mult, op1=ALU.add).then_inc(o_added, 1)
                else:
                    nc.vector.tensor_copy(tot[:, x:x + 1], row_sum[:, x:x + 1])
                    nc.vector.tensor_copy(o_acc[:, x, :], o_ps[:, 0:P]).then_inc(o_added, 1)

            def finish(g, par):
                x = par * spi + spi - 1
                dve.wait_ge(o_added, made(spi * g + spi - 1))
                nc.vector.reciprocal(r_tot[:], tot[:, x:x + 1]).then_inc(fin_step, 1)
                nc.vector.tensor_tensor(o_sum[:], o_acc[:, x, 0:64], o_acc[:, x, 64:128], ALU.add).then_inc(fin_step, 1)
                dve.wait_ge(fin_step, 2 * g + 2)
                dve.wait_ge(out_free, made_before(g, 2))
                nc.vector.tensor_scalar(o_out[:, par, :], o_sum[:], r_tot[:, 0:1], 1.0 / V_SCALE,
                                        ALU.mult, ALU.mult).then_inc(ctx_made, 1)

            def query_tile(g, r, last=False):
                par = r % 2
                for s in range(spi):
                    ahead, s2 = (s + 1) // spi, (s + 1) % spi
                    if not (last and ahead):
                        row_max(g + ahead, (r + ahead) % 4, s2)
                    low_part(spi * g + s, s)
                    add_output(g, par, s)
                finish(g, par)

            row_max(0, 0, 0)
            over_tiles(dve, query_tile)

        @block.scalar
        def _(act):
            act.sem_inc(exped, PRIME)
            act.sem_inc(hi_made, PRIME)

            def exponentials(g, par, s):
                n = spi * g + s
                x = par * spi + s
                act.wait_ge(maxed, made(n))
                act.wait_ge(turned, made_before(n, 2))
                if s:
                    nc.scalar.activation(corr[:, x:x + 1], max_step[:, x:x + 1], ACT.Exp, scale=sc)
                nc.scalar.activation(p_sb[:, s % 2, :], s_ps[:, s % 2, :], ACT.Exp, bias=neg_max[:, x:x + 1],
                                     scale=sc, accum_out=row_sum[:, x:x + 1]).then_inc(exped, 1)

            def high_part(n, s):
                act.wait_ge(turned, made(n))
                act.wait_ge(pv_made, made_before(n, 2))
                nc.scalar.activation(hi_sb[:, s % 2, :, :], t_ps[:], ACT.Copy).then_inc(hi_made, 1)

            def query_tile(g, r, last=False):
                for s in range(spi):
                    high_part(spi * g + s, s)
                    ahead, s2 = (s + 1) // spi, (s + 1) % spi
                    if not (last and ahead):
                        exponentials(g + ahead, (r + ahead) % 2, s2)

            exponentials(0, 0, 0)
            over_tiles(act, query_tile)

        @block.gpsimd
        def _(pool):
            pool.sem_inc(out_free, PRIME)
            with pool.Fori(0, n_tiles // 2) as g2:
                for par in range(2):
                    g = 2 * g2 + par
                    pool.wait_ge(ctx_made, made(g))
                    pool.dma_start(ctx_out(g), o_out[:, par, :]).then_inc(stored, 16)
                    pool.wait_ge(stored, 16 * (g + 1))
                    pool.sem_inc(out_free, 1)


def two_layers(nc, x, norm1_w, norm2_w, w_qkv, w_proj, b_proj, l0_ff1_w, l0_ff1_b, l0_ff2_w, l0_ff2_b, gamma, beta,
               wq, bq, wk, bk, wv, bv, wpos_t, u_bias, v_bias, w_out, b_out, wr, br, ff1_w, ff1_b, ff2_w, ff2_b,
               rope, win_mask, turn_tab, pe_tab, diag_mask, identity, prefix, out):
    batches, height, width, c = x.shape
    seq = height * width
    n = batches * seq
    heads = batches * NH
    tiles = seq // P

    def scratch(name, shape, dt=F32):
        return nc.dram_tensor(name, shape, dt).ap()

    x = x.rearrange("b h w c -> (b h w) c")
    out = out.rearrange("b h w c -> (b h w) c")
    qk_t = scratch("qk_t", (2 * c, n))
    v_rows = scratch("v_rows", (n, c))
    ctx0 = scratch("ctx0", (n, c))
    x1 = scratch("x1", (n, c))
    q_tab = scratch("q_tab", (heads, P, 5, 1 + seq), F16)
    q_past = scratch("q_past", (heads, P, 4, 1), F16)
    k_tab = scratch("k_tab", (heads, P, 2, seq), F16)
    v_tab = scratch("v_tab", (heads, P, tiles, P), F16)
    ctx1 = scratch("ctx1", (batches, 1 + seq, c))
    ctx1_rows = ctx1.rearrange("b r c -> (b r) c")

    def ctx_out(g):
        b, h, i = g // (NH * tiles), (g // tiles) % NH, g % tiles
        return ctx1_rows[ds(b * (seq + 1) + i * P, P), ds(h * HD, HD)]

    qkv_phase(nc, n, seq, x, norm1_w, w_qkv, rope, identity, qk_t, v_rows)
    window_phase(nc, batches, height, width, qk_t, v_rows, win_mask, identity, ctx0)
    layer0_mlp_phase(nc, n, x, ctx0, w_proj, b_proj, norm2_w, l0_ff1_w, l0_ff1_b, l0_ff2_w, l0_ff2_b, identity, x1)
    tables_phase(nc, batches, seq, x1, gamma, beta, wq, bq, wk, bk, wv, bv, wpos_t, u_bias, v_bias, turn_tab,
                 identity, q_tab, q_past, k_tab, v_tab)
    flash_phase(nc, seq, heads, q_tab, q_past, k_tab, v_tab, pe_tab, diag_mask, identity, ctx_out)
    ffn_phase(nc, batches, seq, x1, ctx1, w_out, b_out, wr, br, ff1_w, ff1_b, ff2_w, ff2_b, identity, prefix, out)


def rope_table(height, width, pairs):
    q = pairs // 2
    inv = (1.0 / 10000.0 ** (np.arange(q, dtype=np.float32) / q)).astype(np.float32)
    by_row = np.arange(height, dtype=np.float32)[:, None] * inv
    by_col = np.arange(width, dtype=np.float32)[:, None] * inv
    angle = np.concatenate([np.broadcast_to(by_row[:, None], (height, width, q)),
                            np.broadcast_to(by_col[None], (height, width, q))], -1).reshape(height * width, pairs)
    return np.stack([np.cos(angle), np.sin(angle)]).astype(np.float32)


def window_masks(height, width, span=8, ks=7):
    mask = np.full((3, 2, width, span, width), -1e30, np.float32)
    left = np.clip(np.arange(width) - ks // 2, 0, width - ks)
    for kind, (y, first) in enumerate(((0, 0), (2, 4 - ks // 2), (height // 2 - 1, height - span))):
        for a in range(2):
            top = min(max(2 * y + a - ks // 2, 0), height - ks) - first
            for c in range(width):
                mask[kind, a, c, top:top + ks, left[c]:left[c] + ks] = 0
    return np.ascontiguousarray(mask.reshape(3, P, span * width).transpose(1, 0, 2).reshape(P, -1))


def frequencies(dim):
    return np.exp(np.arange(0, dim, 2, dtype=np.float32) * np.float32(-np.log(10000.0) / dim)).astype(np.float64)


def turn_table(seq, dim):
    angle = frequencies(dim)[:, None] * (np.arange(seq) + 1)[None]
    return (np.stack([np.cos(angle), np.sin(angle)], 1) * B_SCALE).astype(np.float32)


def pe_table(seq, dim):
    angle = frequencies(dim)[:, None] * np.arange(2 * seq)[None]
    value = np.stack([np.sin(angle), np.cos(angle)], 1) * PE_SCALE
    high = value.astype(np.float16)
    return np.stack([high, (value - high).astype(np.float16)], 2)


def diagonal_masks():
    r, c = np.arange(P)[:, None], np.arange(P)[None]
    below, above = (c < r).astype(np.float32), (c > r).astype(np.float32)
    above_first = above.copy()
    above_first[0, 0] = 1
    return np.ascontiguousarray(np.concatenate([below, above, below, above_first], 1))


_INS = ["x", "L0_conv_norm1_w", "L0_conv_norm2_w", "L0_conv_w_qkv", "L0_conv_w_proj", "L0_conv_b_proj",
        "L0_conv_ff1_w", "L0_conv_ff1_b", "L0_conv_ff2_w", "L0_conv_ff2_b", "L1_attn_ln_gamma", "L1_attn_ln_beta",
        "L1_attn_Wq", "L1_attn_bq", "L1_attn_Wk", "L1_attn_bk", "L1_attn_Wv", "L1_attn_bv", "L1_attn_Wpos",
        "L1_attn_u_bias", "L1_attn_v_bias", "L1_attn_Wout", "L1_attn_bout", "L1_ffn_wr", "L1_ffn_br", "L1_ffn_w1",
        "L1_ffn_b1", "L1_ffn_w2", "L1_ffn_b2"]


def kernel(**inputs):
    import numpy as _np
    import concourse.bacc as _bacc
    from concourse import mybir as _mybir
    from concourse.bass_utils import run_bass_kernel_spmd as _run

    data = {name: _np.asarray(inputs[name]) for name in _INS}
    height, width, dim = data["x"].shape[1:]
    data["L1_attn_Wpos"] = data["L1_attn_Wpos"].reshape(dim // 2, 2, NH, HD).transpose(3, 2, 1, 0)
    data["L1_ffn_wr"] = data["L1_ffn_wr"].reshape(-1)
    tri = _np.triu(_np.ones((P, P), _np.float32))
    data.update(rope=rope_table(height, width, dim // 2), win_mask=window_masks(height, width),
                turn_tab=turn_table(height * width, dim), pe_tab=pe_table(height * width, dim),
                diag_mask=diagonal_masks(), identity=_np.eye(P, dtype=_np.float32),
                prefix=_np.concatenate([tri, _np.ones((P, P), _np.float32)], 1))

    nc = _bacc.Bacc("TRN2", target_bir_lowering=False, num_devices=1)
    arrays, args = {}, []
    for name, a in data.items():
        a = _np.ascontiguousarray(a)
        arrays[f"in_{name}_dram"] = a
        args.append(nc.dram_tensor(f"in_{name}_dram", a.shape, _mybir.dt.from_np(a.dtype), kind="ExternalInput").ap())
    args.append(nc.dram_tensor("out_0_dram", data["x"].shape, _mybir.dt.float32, kind="ExternalOutput").ap())
    two_layers(nc, *args)
    r = _run(nc, [arrays], core_ids=[0])
    return r.results[0]["out_0_dram"]
```

```python
import numpy as np
import math
import concourse.bass as bass
from concourse import mybir
from contextlib import ExitStack

P = 128
F32 = mybir.dt.float32
F16 = mybir.dt.float16
U32 = mybir.dt.uint32
ALU = mybir.AluOpType
ACT = mybir.ActivationFunctionType
AX_X = mybir.AxisListType.X
ds = bass.ds

PRIME = 2


def made(n, per=1):
    return (n + 1 + PRIME) * per


def made_before(n, back, per=1):
    return (n + 1 + PRIME - back) * per


Q_SCALE = 32.0
B_SCALE = 8.0
PE_SCALE = 128.0
V_SCALE = 32.0
SCORE_SCALE = Q_SCALE * Q_SCALE
assert SCORE_SCALE == B_SCALE * PE_SCALE
P_SCALE = 1024.0


TOK = 512
SUB = TOK // P
C = 256
NH = 4
HD = C // NH


class Mem:

    def __init__(self, nc, ctx, tag):
        self.nc, self.ctx, self.tag = nc, ctx, tag

    def sb(self, name, shape, dt=F32):
        return self.ctx.enter_context(self.nc.sbuf_tensor(f"{self.tag}_{name}", shape, dt))

    def psum(self, name, shape):
        return self.ctx.enter_context(self.nc.psum_tensor(f"{self.tag}_{name}", shape, F32))

    def sem(self, name):
        return self.ctx.enter_context(self.nc.semaphore(f"{self.tag}_{name}"))


def bounded(value, most):
    return value if isinstance(value, int) else value.with_bounds(min_val=0, max_val=most)


def rows(dram, first, n=SUB):
    return dram[ds(first, n * P), :].rearrange("(k p) c -> p k c", p=P)


def spread(vec, n=P):
    return vec.rearrange("(o c) -> o c", o=1).to_broadcast([n, vec.shape[0]])


def columns(vec):
    return vec.rearrange("(k p) -> p k", p=P)


def over_rows(tile):
    return tile[:].rearrange("p (o c) -> p o c", o=1).to_broadcast([P, SUB, tile.shape[1]])


def in_pairs(eng, steps, step):
    with eng.Fori(0, steps // 2 - 1) as i:
        step(2 * i, i, 0, 3)
        step(2 * i + 1, i, 1, 3)
    step(steps - 2, steps // 2 - 1, 0, 2)
    step(steps - 1, steps // 2 - 1, 1, 1)


def qkv_phase(nc, n_tok, seq, x, norm_w, w_qkv, rope, identity, qk_t, v_out):
    steps = n_tok // TOK
    with ExitStack() as ctx:
        m = Mem(nc, ctx, "qkv")
        w_sb = m.sb("w", [P, 2, 3 * C])
        nw = m.sb("nw", [P, C])
        ident = m.sb("id", [P, P])
        x_sb = m.sb("x", [P, 2, SUB, C])
        rope_sb = m.sb("rope", [P, 2, 2, SUB, P])
        junk = m.sb("junk", [P, SUB, C])
        ss = m.sb("ss", [P, 2, SUB])
        ms = m.sb("ms", [P, 2, SUB])
        sd = m.sb("sd", [P, 2, SUB])
        rs = m.sb("rs", [P, 2, SUB])
        xn = m.sb("xn", [P, SUB, C])
        t_v = m.sb("t_v", [P, 2, SUB, P])
        t_p = m.sb("t_p", [P, 2, SUB, P])
        h_sb = m.sb("h", [P, 2, SUB, C])
        ht = m.sb("ht", [P, 2, 2, TOK])
        qk_o = m.sb("qk_o", [P, 2, 4, TOK])
        v_o = m.sb("v_o", [P, 2, SUB, C])
        t_ps = m.psum("t_ps", [P, 2, TOK])
        qk_ps = m.psum("qk_ps", [P, 4, TOK])
        v_ps = m.psum("v_ps", [P, SUB, C])

        const_in = m.sem("const_in")
        x_in = [m.sem(f"x_in{p}") for p in range(2)]
        stored = [m.sem(f"stored{p}") for p in range(2)]
        squared = m.sem("squared")
        meaned = m.sem("meaned")
        rooted = m.sem("rooted")
        inverted = m.sem("inverted")
        normed = m.sem("normed")
        halves = m.sem("halves")
        even_done = m.sem("even_done")
        pool_step = m.sem("pool_step")
        odd_done = m.sem("odd_done")
        turned = m.sem("turned")
        ht_a = m.sem("ht_a")
        ht_b = m.sem("ht_b")
        qk_made = m.sem("qk_made")
        v_made = m.sem("v_made")
        qk_read = m.sem("qk_read")
        v_read = m.sem("v_read")
        block = ctx.enter_context(nc.Block())

        @block.sync
        def _(sp):
            sp.dma_start(w_sb[:], w_qkv.rearrange("(k p) n -> p k n", p=P)).then_inc(const_in, 16)
            sp.dma_start(nw[:], spread(norm_w)).then_inc(const_in, 16)
            sp.dma_start(ident[:], identity).then_inc(const_in, 16)
            for s in stored:
                sp.sem_inc(s, 32)

            def load(t, par):
                sp.wait_ge(even_done, made_before(t, 2))
                sp.wait_ge(odd_done, made_before(t, 2))
                sp.dma_start(x_sb[:, par], rows(x, t * TOK)).then_inc(x_in[par], 16)
                pos = (t % (seq // TOK)) * TOK
                for a in range(2):
                    sp.dma_start(rope_sb[:, par, a], rows(rope[a], pos)).then_inc(x_in[par], 16)

            def store(t, par):
                sp.wait_ge(v_read, made(t))
                sp.wait_ge(qk_read, made(t))
                sp.dma_start(rows(v_out, t * TOK), v_o[:, par]).then_inc(stored[par], 16)
                sp.dma_start(qk_t.rearrange("(m p) t -> p m t", p=P)[:, :, ds(t * TOK, TOK)],
                             qk_o[:, par]).then_inc(stored[par], 16)

            load(0, 0)
            load(1, 1)
            load(2, 0)
            with sp.Fori(0, steps // 2 - 2) as i:
                load(2 * i + 3, 1)
                store(2 * i, 0)
                load(2 * i + 4, 0)
                store(2 * i + 1, 1)
            load(steps - 1, 1)
            for t in range(steps - 4, steps):
                store(t, t % 2)
            for s in stored:
                sp.wait_ge(s, 32 * (steps // 2 + 1))

        @block.scalar
        def _(act):
            for s in (squared, rooted, ht_a, qk_read):
                act.sem_inc(s, PRIME)

            def norm(t, i, par):
                act.wait_ge(x_in[par], 48 * (i + 1))
                for k in range(SUB):
                    sq = nc.scalar.activation(junk[:, k], x_sb[:, par, k], ACT.Square, accum_out=ss[:, par, k:k + 1])
                sq.then_inc(squared, 1)
                act.wait_ge(meaned, made(t))
                nc.scalar.activation(sd[:, par], ms[:, par], ACT.Sqrt).then_inc(rooted, 1)

            def copy_rows(t, par):
                act.wait_ge(turned, made(t))
                nc.scalar.activation(ht[:, par, 0], t_ps[:, 0], ACT.Copy).then_inc(ht_a, 1)

            def step(t, i, par, left):
                if left > 1:
                    copy_rows(t + 1, 1 - par)
                if left > 2:
                    norm(t + 2, i + 1, par)
                act.wait_ge(qk_made, made(t))
                act.wait_ge(stored[par], 32 * (i + 1))
                nc.scalar.activation(qk_o[:, par], qk_ps[:], ACT.Copy).then_inc(qk_read, 1)

            norm(0, 0, 0)
            norm(1, 0, 1)
            copy_rows(0, 0)
            in_pairs(act, steps, step)

        @block.vector
        def _(dve):
            for s in (meaned, inverted, normed, halves, even_done, ht_b, v_read):
                dve.sem_inc(s, PRIME)
            dve.wait_ge(const_in, 48)

            def rotate(t, i, par):
                dve.wait_ge(squared, made(t))
                nc.vector.tensor_scalar(ms[:, par], ss[:, par], 1.0 / C, 1e-6, ALU.mult, ALU.add).then_inc(meaned, 1)
                dve.wait_ge(rooted, made(t))
                nc.vector.reciprocal(rs[:, par], sd[:, par]).then_inc(inverted, 1)
                dve.wait_ge(inverted, made(t))
                dve.wait_ge(x_in[par], 48 * (i + 1))
                dve.wait_ge(odd_done, made_before(t, 1))
                for k in range(SUB):
                    st = nc.vector.scalar_tensor_tensor(out=xn[:, k], in0=x_sb[:, par, k], scalar=rs[:, par, k:k + 1],
                                                        in1=nw[:], op0=ALU.mult, op1=ALU.mult)
                st.then_inc(normed, 1)
                dve.wait_ge(normed, made(t))
                ev, od = xn[:, :, 0::2], xn[:, :, 1::2]
                nc.vector.tensor_tensor(t_v[:, 0], ev, rope_sb[:, par, 0], ALU.mult)
                nc.vector.tensor_tensor(t_v[:, 1], od, rope_sb[:, par, 1], ALU.mult).then_inc(halves, 1)
                dve.wait_ge(halves, made(t))
                dve.wait_ge(turned, made_before(t, 2))
                nc.vector.tensor_tensor(h_sb[:, par, :, 0::2], t_v[:, 0], t_v[:, 1],
                                        ALU.subtract).then_inc(even_done, 1)

            def copy_rows(t, par):
                dve.wait_ge(turned, made(t))
                nc.vector.tensor_copy(ht[:, par, 1], t_ps[:, 1]).then_inc(ht_b, 1)

            def step(t, i, par, left):
                if left > 1:
                    copy_rows(t + 1, 1 - par)
                if left > 2:
                    rotate(t + 2, i + 1, par)
                dve.wait_ge(v_made, made(t))
                dve.wait_ge(stored[par], 32 * (i + 1))
                nc.vector.tensor_copy(v_o[:, par], v_ps[:]).then_inc(v_read, 1)

            rotate(0, 0, 0)
            rotate(1, 0, 1)
            copy_rows(0, 0)
            in_pairs(dve, steps, step)

        @block.gpsimd
        def _(pool):
            for s in (pool_step, odd_done):
                pool.sem_inc(s, PRIME)

            def step(t, par):
                pool.wait_ge(normed, made(t))
                ev, od = xn[:, :, 0::2], xn[:, :, 1::2]
                nc.gpsimd.tensor_tensor(t_p[:, 0], ev, rope_sb[:, par, 1], ALU.mult)
                nc.gpsimd.tensor_tensor(t_p[:, 1], od, rope_sb[:, par, 0], ALU.mult).then_inc(pool_step, 1)
                pool.wait_ge(pool_step, made(t))
                pool.wait_ge(turned, made_before(t, 2))
                nc.gpsimd.tensor_tensor(h_sb[:, par, :, 1::2], t_p[:, 0], t_p[:, 1], ALU.add).then_inc(odd_done, 1)

            with pool.Fori(0, steps // 2) as i:
                step(2 * i, 0)
                step(2 * i + 1, 1)

        @block.tensor
        def _(pe):
            for s in (turned, qk_made, v_made):
                pe.sem_inc(s, PRIME)
            pe.wait_ge(const_in, 48)

            def transposes(t, par):
                pe.wait_ge(even_done, made(t))
                pe.wait_ge(odd_done, made(t))
                pe.wait_ge(ht_a, made_before(t, 1))
                pe.wait_ge(ht_b, made_before(t, 1))
                for k in range(SUB):
                    for c in range(2):
                        tr = nc.tensor.transpose(t_ps[:, c, k * P:(k + 1) * P], h_sb[:, par, k, c * P:(c + 1) * P],
                                                 ident[:])
                tr.then_inc(turned, 1)

            def step(t, i, par, left):
                if left > 1:
                    transposes(t + 1, 1 - par)
                pe.wait_ge(ht_a, made(t))
                pe.wait_ge(ht_b, made(t))
                pe.wait_ge(qk_read, made_before(t, 1))
                for o in range(4):
                    for c in range(2):
                        mm = nc.tensor.matmul(qk_ps[:, o], w_sb[:, c, o * P:(o + 1) * P], ht[:, par, c],
                                              start=(c == 0), stop=(c == 1))
                mm.then_inc(qk_made, 1)
                pe.wait_ge(v_read, made_before(t, 1))
                for k in range(SUB):
                    for c in range(2):
                        mm = nc.tensor.matmul(v_ps[:, k], ht[:, par, c, k * P:(k + 1) * P], w_sb[:, c, 2 * C:3 * C],
                                              start=(c == 0), stop=(c == 1))
                mm.then_inc(v_made, 1)

            transposes(0, 0)
            in_pairs(pe, steps, step)


def window_phase(nc, batches, rows_, cols, qk_t, v, masks, identity, ctx_out):
    KS = 7
    pairs = rows_ // 2
    units = batches * pairs
    span = 8
    assert cols == 64 and span * cols == 512
    last = rows_ - span
    hi_y = pairs - 2
    UB = 4
    with ExitStack() as ctx:
        m = Mem(nc, ctx, "win")
        mask_sb = m.sb("mask", [P, 3 * 512])
        ident = m.sb("id", [P, P])
        q_sb = m.sb("q", [HD, UB, NH, P])
        k_sb = m.sb("k", [HD, UB, NH, 512])
        v_sb = m.sb("v", [P, UB, SUB, C])
        s_sb = m.sb("s", [P, 2, 2, 512])
        mx = m.sb("mx", [P, 2, 2])
        nm = m.sb("nm", [P, 2, 2])
        p_sb = m.sb("p", [P, 2, 2, 512])
        sm = m.sb("sm", [P, 2, 2])
        rs = m.sb("rs", [P, 2, 2])
        pt = m.sb("pt", [P, 2, 2, 512])
        o_sb = m.sb("o", [P, 2, NH, HD])
        s_ps = m.psum("s_ps", [P, 4, 512])
        t_ps = m.psum("t_ps", [P, 2, 512])
        o_ps = m.psum("o_ps", [P, 2, 512])

        const_in = m.sem("const_in")
        qkv_in = [m.sem(f"qkv_in{p}") for p in range(UB)]
        stored = [m.sem(f"stored{p}") for p in range(2)]
        scored = m.sem("scored")
        masked = m.sem("masked")
        maxed = m.sem("maxed")
        negated = m.sem("negated")
        exped = m.sem("exped")
        turned = m.sem("turned")
        pt_a = m.sem("pt_a")
        pt_b = m.sem("pt_b")
        weighed = m.sem("weighed")
        inverted = m.sem("inverted")
        out_made = m.sem("out_made")
        block = ctx.enter_context(nc.Block())

        @block.sync
        def _(sp):
            sp.dma_start(mask_sb[:], masks).then_inc(const_in, 16)
            sp.dma_start(ident[:], identity).then_inc(const_in, 16)
            for s in stored:
                sp.sem_inc(s, 16)

            def load(u, buf, first=False):
                b, y = u // pairs, u % pairs
                inner = (y >= 2) * (y < hi_y)
                top = (2 * y - KS // 2) * inner + last * (y >= hi_y)
                tok = b * (rows_ * cols) + y * P
                key = bounded(b * (rows_ * cols) + top * cols, batches * rows_ * cols - 512)
                if not first:
                    sp.wait_ge(weighed, made(2 * (u - UB) + 1))
                qk = qk_t.rearrange("(a h d) t -> a d h t", a=2, h=NH)
                sp.dma_start(q_sb[:, buf], qk[0][:, :, ds(tok, P)]).then_inc(qkv_in[buf], 16)
                sp.dma_start(k_sb[:, buf], qk[1][:, :, ds(key, 512)]).then_inc(qkv_in[buf], 16)
                sp.dma_start(v_sb[:, buf], rows(v, key)).then_inc(qkv_in[buf], 16)

            def store(u, par):
                sp.wait_ge(out_made, made(2 * u + 1))
                sp.dma_start(ctx_out[ds(u * P, P), :], o_sb[:, par].rearrange("p h d -> p (h d)")
                             ).then_inc(stored[par], 16)

            for u in range(UB):
                load(u, u, first=True)
            with sp.Fori(0, units // UB - 1) as i:
                for a in range(UB):
                    store(UB * i + a, a % 2)
                    load(UB * (i + 1) + a, a)
            for u in range(units - UB, units):
                store(u, u % 2)
            for s in stored:
                sp.wait_ge(s, 16 * (units // 2 + 1))

        def pipeline(eng, scores, turn, weigh, turn_first=False):
            for n in range(2):
                scores(n, 0, n)
            turn(0, 0)

            def item(i, j, left=2 * UB):
                n = 2 * UB * i + j
                if turn_first and left > 1:
                    turn(n + 1, j + 1)
                if left > 2:
                    scores(n + 2, i + (j + 2) // (2 * UB), (j + 2) % (2 * UB))
                weigh(n, i, j)
                if left > 1 and not turn_first:
                    turn(n + 1, j + 1)

            with eng.Fori(0, units // UB - 1) as i:
                for j in range(2 * UB):
                    item(i, j)
            for j in range(2 * UB):
                item(units // UB - 1, j, left=2 * UB - j)

        @block.tensor
        def _(pe):
            for s in (scored, turned, weighed):
                pe.sem_inc(s, PRIME)
            pe.wait_ge(const_in, 32)

            def scores(n, i, j):
                if j % 2 == 0:
                    pe.wait_ge(qkv_in[j // 2], 48 * (i + 1))
                pe.wait_ge(masked, made_before(n, 2))
                for a in range(2):
                    h = 2 * (j % 2) + a
                    mm = nc.tensor.matmul(s_ps[:, h], q_sb[:, j // 2, h], k_sb[:, j // 2, h], start=True, stop=True)
                mm.then_inc(scored, 1)

            def turn(n, j):
                pe.wait_ge(exped, made(n))
                pe.wait_ge(pt_a, made_before(n, 1))
                pe.wait_ge(pt_b, made_before(n, 1))
                for a in range(2):
                    for c in range(4):
                        tr = nc.tensor.transpose(t_ps[:, a, c * P:(c + 1) * P],
                                                 p_sb[:, j % 2, a, c * P:(c + 1) * P], ident[:])
                tr.then_inc(turned, 1)

            def weigh(n, i, j):
                pe.wait_ge(pt_a, made(n))
                pe.wait_ge(pt_b, made(n))
                pe.wait_ge(out_made, made_before(n, 2))
                for a in range(2):
                    h = 2 * (j % 2) + a
                    for c in range(4):
                        mm = nc.tensor.matmul(o_ps[:, j % 2, a * HD:(a + 1) * HD], pt[:, j % 2, a, c * P:(c + 1) * P],
                                              v_sb[:, j // 2, c, h * HD:(h + 1) * HD], start=(c == 0), stop=(c == 3))
                mm.then_inc(weighed, 1)

            pipeline(pe, scores, turn, weigh)

        @block.vector
        def _(dve):
            for s in (masked, maxed, negated, pt_a, inverted, out_made):
                dve.sem_inc(s, PRIME)
            dve.wait_ge(const_in, 32)

            def find_max(n, i, j):
                y = (n // 2) % pairs
                kind = (y >= 2) + (y >= hi_y) if not isinstance(y, int) else int(y >= 2) + int(y >= hi_y)
                dve.wait_ge(scored, made(n))
                dve.wait_ge(exped, made_before(n, 2))
                mk = mask_sb[:, ds(kind * 512, 512)]
                for a in range(2):
                    op = nc.vector.tensor_tensor(s_sb[:, j % 2, a], s_ps[:, 2 * (j % 2) + a], mk, ALU.add)
                op.then_inc(masked, 1)
                dve.wait_ge(masked, made(n))
                nc.vector.tensor_reduce(mx[:, j % 2], s_sb[:, j % 2], AX_X, ALU.max).then_inc(maxed, 1)
                dve.wait_ge(maxed, made(n))
                nc.vector.tensor_scalar(nm[:, j % 2], mx[:, j % 2], -(HD ** -0.5), None, ALU.mult).then_inc(negated, 1)

            def copy_turned(n, j):
                dve.wait_ge(turned, made(n))
                dve.wait_ge(weighed, made_before(n, 2))
                nc.vector.tensor_copy(pt[:, j % 2, 0], t_ps[:, 0]).then_inc(pt_a, 1)

            def finish(n, i, j):
                dve.wait_ge(exped, made(n))
                nc.vector.reciprocal(rs[:, j % 2], sm[:, j % 2]).then_inc(inverted, 1)
                dve.wait_ge(inverted, made(n))
                dve.wait_ge(weighed, made(n))
                if j % 2 == 0:
                    dve.wait_ge(stored[j // 2 % 2], 16 * (UB // 2 * i + j // 4 + 1))
                nc.vector.tensor_tensor(o_sb[:, j // 2 % 2, 2 * (j % 2):2 * (j % 2) + 2],
                                        o_ps[:, j % 2, 0:2 * HD].rearrange("p (h d) -> p h d", h=2),
                                        rs[:, j % 2].rearrange("p (h o) -> p h o", o=1).to_broadcast([P, 2, HD]),
                                        ALU.mult).then_inc(out_made, 1)

            pipeline(dve, find_max, copy_turned, finish)

        @block.scalar
        def _(act):
            act.sem_inc(exped, PRIME)
            act.sem_inc(pt_b, PRIME)

            def exponentials(n, i, j):
                act.wait_ge(negated, made(n))
                act.wait_ge(turned, made_before(n, 2))
                act.wait_ge(inverted, made_before(n, 2))
                for a in range(2):
                    ex = nc.scalar.activation(p_sb[:, j % 2, a], s_sb[:, j % 2, a], ACT.Exp, bias=nm[:, j % 2, a:a + 1],
                                              scale=HD ** -0.5, accum_out=sm[:, j % 2, a:a + 1])
                ex.then_inc(exped, 1)

            def copy_turned(n, j):
                act.wait_ge(turned, made(n))
                act.wait_ge(weighed, made_before(n, 2))
                nc.scalar.activation(pt[:, j % 2, 1], t_ps[:, 1], ACT.Copy).then_inc(pt_b, 1)

            def nothing(n, i, j):
                pass

            pipeline(act, exponentials, copy_turned, nothing, turn_first=True)


def layer0_mlp_phase(nc, n_tok, x, ctx_in, w_proj, b_proj, norm_w, ff1_w, ff1_b, ff2_w, ff2_b, identity, x_out):
    steps = n_tok // TOK
    with ExitStack() as ctx:
        m = Mem(nc, ctx, "mlp")
        wp = m.sb("wp", [P, 2, C])
        w1 = m.sb("w1", [P, 2, 2 * C])
        w2 = m.sb("w2", [P, 2, C])
        nw = m.sb("nw", [P, C])
        bp = m.sb("bp", [P, C])
        b2 = m.sb("b2", [P, C])
        b1 = m.sb("b1", [P, 4])
        ident = m.sb("id", [P, P])
        c_sb = m.sb("c", [P, 2, SUB, C])
        x_sb = m.sb("x", [P, 2, SUB, C])
        xb = m.sb("xb", [P, SUB, C])
        x1 = m.sb("x1", [P, 2, SUB, C])
        x1b = m.sb("x1b", [P, 2, SUB, C])
        junk = m.sb("junk", [P, SUB, C])
        ss = m.sb("ss", [P, SUB])
        ms = m.sb("ms", [P, SUB])
        sd = m.sb("sd", [P, SUB])
        rs = m.sb("rs", [P, SUB])
        xn = m.sb("xn", [P, SUB, C])
        ct = m.sb("ct", [P, 2, TOK])
        nt = m.sb("nt", [P, 2, TOK])
        gate = m.sb("gate", [P, 2, TOK])
        ut = m.sb("ut", [P, 2, TOK])
        x2 = m.sb("x2", [P, 2, SUB, C])
        t_ps = m.psum("t_ps", [P, 2, TOK])
        f_ps = m.psum("f_ps", [P, 4, TOK])
        p_ps = m.psum("p_ps", [P, SUB, C])

        const_in = m.sem("const_in")
        rows_in = [m.sem(f"rows_in{p}") for p in range(2)]
        stored = [m.sem(f"stored{p}") for p in range(2)]
        ctx_turned = m.sem("ctx_turned")
        ct_a, ct_b = m.sem("ct_a"), m.sem("ct_b")
        projected = m.sem("projected")
        xb_made = m.sem("xb_made")
        x1_made = m.sem("x1_made")
        x1b_made = m.sem("x1b_made")
        squared, meaned, rooted, inverted = m.sem("squared"), m.sem("meaned"), m.sem("rooted"), m.sem("inverted")
        normed = m.sem("normed")
        rows_turned = m.sem("rows_turned")
        nt_a, nt_b = m.sem("nt_a"), m.sem("nt_b")
        widened = m.sem("widened")
        gated = m.sem("gated")
        u_made = m.sem("u_made")
        narrowed = m.sem("narrowed")
        x2_made = m.sem("x2_made")
        block = ctx.enter_context(nc.Block())

        @block.sync
        def _(sp):
            sp.dma_start(wp[:], w_proj.rearrange("(k p) n -> p k n", p=P)).then_inc(const_in, 16)
            sp.dma_start(w1[:], ff1_w.rearrange("(k p) n -> p k n", p=P)).then_inc(const_in, 16)
            sp.dma_start(w2[:], ff2_w.rearrange("(k p) n -> p k n", p=P)).then_inc(const_in, 16)
            sp.dma_start(nw[:], spread(norm_w)).then_inc(const_in, 16)
            sp.dma_start(bp[:], spread(b_proj)).then_inc(const_in, 16)
            sp.dma_start(b2[:], spread(ff2_b)).then_inc(const_in, 16)
            sp.dma_start(b1[:], columns(ff1_b), allow_slow_non_contiguous=True).then_inc(const_in, 16)
            sp.dma_start(ident[:], identity).then_inc(const_in, 16)
            for s in stored:
                sp.sem_inc(s, 16)

            def load(t, par):
                sp.wait_ge(ctx_turned, made_before(t, 2))
                sp.wait_ge(xb_made, made_before(t, 2))
                sp.dma_start(c_sb[:, par], rows(ctx_in, t * TOK)).then_inc(rows_in[par], 16)
                sp.dma_start(x_sb[:, par], rows(x, t * TOK)).then_inc(rows_in[par], 16)

            def store(t, par):
                sp.wait_ge(x2_made, made(t))
                sp.dma_start(rows(x_out, t * TOK), x2[:, par]).then_inc(stored[par], 16)

            load(0, 0)
            load(1, 1)
            load(2, 0)
            with sp.Fori(0, steps // 2 - 2) as i:
                load(2 * i + 3, 1)
                store(2 * i, 0)
                load(2 * i + 4, 0)
                store(2 * i + 1, 1)
            load(steps - 1, 1)
            for t in range(steps - 4, steps):
                store(t, t % 2)
            for s in stored:
                sp.wait_ge(s, 16 * (steps // 2 + 1))

        @block.tensor
        def _(pe):
            for s in (ctx_turned, projected, rows_turned, widened, narrowed):
                pe.sem_inc(s, PRIME)
            pe.wait_ge(const_in, 128)

            def context_transposes(t, i, par):
                pe.wait_ge(rows_in[par], 32 * (i + 1))
                pe.wait_ge(nt_a, made_before(t, 2))
                pe.wait_ge(nt_b, made_before(t, 2))
                for k in range(SUB):
                    for c in range(2):
                        tr = nc.tensor.transpose(t_ps[:, c, k * P:(k + 1) * P], c_sb[:, par, k, c * P:(c + 1) * P],
                                                 ident[:])
                tr.then_inc(ctx_turned, 1)

            def project(t):
                pe.wait_ge(ct_a, made(t))
                pe.wait_ge(ct_b, made(t))
                pe.wait_ge(x1_made, made_before(t, 1))
                for k in range(SUB):
                    for c in range(2):
                        mm = nc.tensor.matmul(p_ps[:, k], ct[:, c, k * P:(k + 1) * P], wp[:, c],
                                              start=(c == 0), stop=(c == 1))
                mm.then_inc(projected, 1)

            def row_transposes(t):
                pe.wait_ge(normed, made(t))
                for k in range(SUB):
                    for c in range(2):
                        tr = nc.tensor.transpose(t_ps[:, c, k * P:(k + 1) * P], xn[:, k, c * P:(c + 1) * P], ident[:])
                tr.then_inc(rows_turned, 1)

            def widen(t):
                pe.wait_ge(nt_a, made(t))
                pe.wait_ge(nt_b, made(t))
                pe.wait_ge(u_made, made_before(t, 1))
                for o in range(4):
                    for c in range(2):
                        mm = nc.tensor.matmul(f_ps[:, o], w1[:, c, o * P:(o + 1) * P], nt[:, c],
                                              start=(c == 0), stop=(c == 1))
                mm.then_inc(widened, 1)

            def narrow(t):
                pe.wait_ge(u_made, made(t))
                for k in range(SUB):
                    for c in range(2):
                        mm = nc.tensor.matmul(p_ps[:, k], ut[:, c, k * P:(k + 1) * P], w2[:, c],
                                              start=(c == 0), stop=(c == 1))
                mm.then_inc(narrowed, 1)

            def step(t, i, par, left):
                if left > 2:
                    context_transposes(t + 2, i + 1, par)
                widen(t)
                pe.wait_ge(x2_made, made_before(t, 1))
                if left > 2:
                    project(t + 2)
                if left > 1:
                    row_transposes(t + 1)
                if left > 2:
                    pe.wait_ge(x1_made, made(t + 2))
                narrow(t)

            for t in range(2):
                context_transposes(t, 0, t)
                project(t)
            row_transposes(0)
            in_pairs(pe, steps, step)

        @block.gpsimd
        def _(pool):
            pool.sem_inc(xb_made, PRIME)
            pool.sem_inc(x1b_made, PRIME)
            pool.wait_ge(const_in, 128)

            def step(t, i, par):
                pool.wait_ge(rows_in[par], 32 * (i + 1))
                pool.wait_ge(x1_made, made_before(t, 1))
                nc.gpsimd.tensor_tensor(xb[:], x_sb[:, par], over_rows(bp), ALU.add).then_inc(xb_made, 1)
                pool.wait_ge(x1_made, made(t))
                pool.wait_ge(x2_made, made_before(t, 2))
                nc.gpsimd.tensor_tensor(x1b[:, par], x1[:, par], over_rows(b2), ALU.add).then_inc(x1b_made, 1)

            with pool.Fori(0, steps // 2) as i:
                step(2 * i, i, 0)
                step(2 * i + 1, i, 1)

        @block.scalar
        def _(act):
            for s in (ct_a, squared, rooted, nt_a, gated):
                act.sem_inc(s, PRIME)
            act.wait_ge(const_in, 128)

            def copy_context(t):
                act.wait_ge(ctx_turned, made(t))
                act.wait_ge(projected, made_before(t, 1))
                nc.scalar.activation(ct[:, 0], t_ps[:, 0], ACT.Copy).then_inc(ct_a, 1)

            def norm(t, par):
                act.wait_ge(x1_made, made(t))
                act.wait_ge(meaned, made_before(t, 1))
                for k in range(SUB):
                    sq = nc.scalar.activation(junk[:, k], x1[:, par, k], ACT.Square, accum_out=ss[:, k:k + 1])
                sq.then_inc(squared, 1)
                act.wait_ge(meaned, made(t))
                act.wait_ge(inverted, made_before(t, 1))
                nc.scalar.activation(sd[:], ms[:], ACT.Sqrt).then_inc(rooted, 1)

            def copy_rows(t):
                act.wait_ge(rows_turned, made(t))
                act.wait_ge(widened, made_before(t, 1))
                nc.scalar.activation(nt[:, 0], t_ps[:, 0], ACT.Copy).then_inc(nt_a, 1)

            def step(t, i, par, left):
                if left > 2:
                    copy_context(t + 2)
                act.wait_ge(widened, made(t))
                act.wait_ge(u_made, made_before(t, 1))
                for c in range(2):
                    ge = nc.scalar.activation(gate[:, c], f_ps[:, c], ACT.Gelu, bias=b1[:, c:c + 1])
                ge.then_inc(gated, 1)
                if left > 1:
                    copy_rows(t + 1)
                if left > 2:
                    norm(t + 2, par)

            for t in range(2):
                copy_context(t)
                norm(t, t)
            copy_rows(0)
            in_pairs(act, steps, step)

        @block.vector
        def _(dve):
            for s in (ct_b, x1_made, meaned, inverted, normed, nt_b, u_made, x2_made):
                dve.sem_inc(s, PRIME)
            dve.wait_ge(const_in, 128)

            def copy_context(t):
                dve.wait_ge(ctx_turned, made(t))
                dve.wait_ge(projected, made_before(t, 1))
                nc.vector.tensor_copy(ct[:, 1], t_ps[:, 1]).then_inc(ct_b, 1)

            def residual(t, par):
                dve.wait_ge(projected, made(t))
                dve.wait_ge(xb_made, made(t))
                dve.wait_ge(x1b_made, made_before(t, 2))
                nc.vector.tensor_tensor(x1[:, par], p_ps[:], xb[:], ALU.add).then_inc(x1_made, 1)

            def norm(t, par):
                dve.wait_ge(squared, made(t))
                nc.vector.tensor_scalar(ms[:], ss[:], 1.0 / C, 1e-6, ALU.mult, ALU.add).then_inc(meaned, 1)
                dve.wait_ge(rooted, made(t))
                nc.vector.reciprocal(rs[:], sd[:]).then_inc(inverted, 1)
                dve.wait_ge(inverted, made(t))
                dve.wait_ge(rows_turned, made_before(t, 1))
                for k in range(SUB):
                    st = nc.vector.scalar_tensor_tensor(out=xn[:, k], in0=x1[:, par, k], scalar=rs[:, k:k + 1],
                                                        in1=nw[:], op0=ALU.mult, op1=ALU.mult)
                st.then_inc(normed, 1)

            def copy_rows(t):
                dve.wait_ge(rows_turned, made(t))
                dve.wait_ge(widened, made_before(t, 1))
                nc.vector.tensor_copy(nt[:, 1], t_ps[:, 1]).then_inc(nt_b, 1)

            def step(t, i, par, left):
                if left > 2:
                    copy_context(t + 2)
                dve.wait_ge(gated, made(t))
                dve.wait_ge(narrowed, made_before(t, 1))
                for c in range(2):
                    st = nc.vector.scalar_tensor_tensor(out=ut[:, c], in0=f_ps[:, 2 + c], scalar=b1[:, 2 + c:3 + c],
                                                        in1=gate[:, c], op0=ALU.add, op1=ALU.mult)
                st.then_inc(u_made, 1)
                if left > 2:
                    residual(t + 2, par)
                if left > 1:
                    copy_rows(t + 1)
                if left > 2:
                    norm(t + 2, par)
                dve.wait_ge(narrowed, made(t))
                dve.wait_ge(x1b_made, made(t))
                dve.wait_ge(stored[par], 16 * (i + 1))
                nc.vector.tensor_tensor(x2[:, par], p_ps[:], x1b[:, par], ALU.add).then_inc(x2_made, 1)

            copy_context(0)
            residual(0, 0)
            norm(0, 0)
            copy_context(1)
            residual(1, 1)
            copy_rows(0)
            norm(1, 1)
            in_pairs(dve, steps, step)


def tables_phase(nc, batches, seq, x, gamma, beta, wq, bq, wk, bk, wv, bv, wpos_t, u_bias, v_bias, turn_tab,
                 identity, q_tab, q_past, k_tab, v_tab):
    per_b = seq // TOK
    steps = batches * per_b
    with ExitStack() as ctx:
        m = Mem(nc, ctx, "tab")
        wq_sb = m.sb("wq", [P, 2, NH, 2, HD])
        wk_sb = m.sb("wk", [P, 2, NH, 2, HD])
        wv_sb = m.sb("wv", [P, 2, C])
        wp_sb = m.sb("wp", [HD, NH, 2, P])
        turn = m.sb("turn", [P, 2, seq])
        ga = m.sb("ga", [P, C])
        be = m.sb("be", [P, C])
        bvb = m.sb("bvb", [P, C])
        bvs = m.sb("bvs", [P, C])
        bq_sb = m.sb("bq", [P, NH])
        bk_sb = m.sb("bk", [P, NH])
        ub = m.sb("ub", [P, NH])
        vb = m.sb("vb", [P, NH])
        bqu = m.sb("bqu", [P, NH])
        bqus = m.sb("bqus", [P, NH])
        bqv = m.sb("bqv", [P, NH])
        bks = m.sb("bks", [P, NH])
        ident = m.sb("id", [P, P])
        x_sb = m.sb("x", [P, 2, SUB, C])
        spare = m.sb("spare", [P, 1])
        st1, st2 = m.sb("st1", [P, SUB, 6]), m.sb("st2", [P, SUB, 6])
        mv1, mv2 = m.sb("mv1", [P, SUB, 2]), m.sb("mv2", [P, SUB, 2])
        ve1, ve2 = m.sb("ve1", [P, SUB]), m.sb("ve2", [P, SUB])
        sd1, sd2 = m.sb("sd1", [P, SUB]), m.sb("sd2", [P, SUB])
        rs1, rs2 = m.sb("rs1", [P, SUB]), m.sb("rs2", [P, SUB])
        xn = m.sb("xn", [P, SUB, C])
        xm = m.sb("xm", [P, SUB, C])
        xg = m.sb("xg", [P, SUB, C])
        xa = m.sb("xa", [P, SUB, C])
        ht = m.sb("ht", [P, 2, TOK])
        qs = m.sb("qs", [P, 2, TOK])
        ks = m.sb("ks", [P, 2, TOK])
        qv = m.sb("qv", [HD, 2, TOK])
        prod = m.sb("prod", [P, 2, 4, TOK])
        bs = m.sb("bs", [P, 2, 2, TOK])
        past = m.sb("past", [P, NH, 2])
        qt_o = m.sb("qt_o", [P, NH, 5, TOK], F16)
        kt_o = m.sb("kt_o", [P, NH, 2, TOK], F16)
        vs = m.sb("vs", [P, SUB, C])
        vt_o = m.sb("vt_o", [P, NH, SUB, 2, HD], F16)
        past_o = m.sb("past_o", [P, NH, 2, 2], F16)
        t_ps = m.psum("t_ps", [P, 2, TOK])
        q_ps = m.psum("q_ps", [P, TOK])
        k_ps = m.psum("k_ps", [P, TOK])
        a_ps = m.psum("a_ps", [P, 2, TOK])
        v_ps = m.psum("v_ps", [P, SUB, C])

        const_in = m.sem("const_in")
        bias_made = m.sem("bias_made")
        x_in = [m.sem(f"x_in{p}") for p in range(2)]
        qk_stored = [m.sem(f"qk_stored{h}") for h in range(NH)]
        v_stored, past_stored = m.sem("v_stored"), m.sem("past_stored")
        stats1, mean1, eps1, root1, inv1, norm1 = (m.sem(n) for n in (
            "stats1", "mean1", "eps1", "root1", "inv1", "norm1"))
        stats2, mean2, eps2, root2, inv2, norm2 = (m.sem(n) for n in (
            "stats2", "mean2", "eps2", "root2", "inv2", "norm2"))
        gained, shifted = m.sem("gained"), m.sem("shifted")
        rows_turned, ht_made = m.sem("rows_turned"), m.sem("ht_made")
        queried, keyed, rotated, valued = m.sem("queried"), m.sem("keyed"), m.sem("rotated"), m.sem("valued")
        qs_made, qv_made, ks_made = m.sem("qs_made"), m.sem("qv_made"), m.sem("ks_made")
        products, bs_made = m.sem("products"), m.sem("bs_made")
        b_hi, v_hi = m.sem("b_hi"), m.sem("v_hi")
        b_lo, c_lo, k_lo, v_lo = m.sem("b_lo"), m.sem("c_lo"), m.sem("k_lo"), m.sem("v_lo")
        v_scaled, past_made, past_hi, past_lo = (m.sem(n) for n in ("v_scaled", "past_made", "past_hi", "past_lo"))
        block = ctx.enter_context(nc.Block())
        N_CONST = 22 * 16

        @block.sync
        def _(sp):
            for dst, w in ((wq_sb, wq), (wk_sb, wk)):
                for a in range(2):
                    for c in range(2):
                        sp.dma_start(dst[:, c, :, a, :], w[c * P:(c + 1) * P, :].rearrange("p (h d) -> p h d", h=NH)
                                     ).then_inc(const_in, 16)
            sp.dma_start(wv_sb[:], wv.rearrange("(k p) n -> p k n", p=P)).then_inc(const_in, 16)
            sp.dma_start(wp_sb[:], wpos_t).then_inc(const_in, 16)
            sp.dma_start(turn[:], turn_tab).then_inc(const_in, 16)
            sp.dma_start(ga[:], spread(gamma)).then_inc(const_in, 16)
            sp.dma_start(be[:], spread(beta)).then_inc(const_in, 16)
            sp.dma_start(bvb[:], spread(bv)).then_inc(const_in, 16)
            sp.dma_start(ident[:], identity).then_inc(const_in, 16)
            for dst, vec in ((bq_sb, bq.rearrange("(h d) -> d h", h=NH)), (bk_sb, bk.rearrange("(h d) -> d h", h=NH)),
                             (ub, u_bias.rearrange("h d -> d h")), (vb, v_bias.rearrange("h d -> d h"))):
                for a in range(2 if dst is not vb else 1):
                    sp.dma_start(dst[a * HD:(a + 1) * HD, :], vec, allow_slow_non_contiguous=True
                                 ).then_inc(const_in, 16)
            for s in qk_stored:
                sp.sem_inc(s, 48)
            sp.sem_inc(v_stored, 64)
            sp.sem_inc(past_stored, 16)

            def load(t, par):
                sp.wait_ge(norm1, made_before(t, 2))
                sp.dma_start(x_sb[:, par], rows(x, t * TOK)).then_inc(x_in[par], 16)

            def store_values(t):
                b, k = t // per_b, t % per_b
                sp.wait_ge(v_lo, made(t))
                for h in range(NH):
                    sp.dma_start(v_tab[ds(b * NH + h, 1)].rearrange("o p t d -> p (o t) d")[:, ds(k * SUB, SUB), :],
                                 vt_o[:, h].rearrange("p k a d -> p k (a d)")).then_inc(v_stored, 16)
                sp.wait_ge(past_lo, made(t))
                sp.dma_start(q_past[ds(b * NH, NH)].rearrange("h p n o -> p h (n o)"),
                             past_o[:].rearrange("p h a n -> p h (a n)")).then_inc(past_stored, 16)

            def store(t, first=False):
                b, k = t // per_b, t % per_b
                for h in range(NH):
                    n = NH * t + h
                    q_dst = q_tab[ds(b * NH + h, 1)].rearrange("o p n c -> p (o n) c")
                    sp.wait_ge(b_lo, made(n))
                    sp.wait_ge(c_lo, made(n))
                    sp.dma_start(q_dst[:, :, ds(k * TOK + 1, TOK)], qt_o[:, h]).then_inc(qk_stored[h], 16)
                    sp.dma_start(q_dst[:, :, 0:1], qt_o[:, h, :, TOK - 1:TOK], allow_slow_non_contiguous=True
                                 ).then_inc(qk_stored[h], 16)
                    sp.wait_ge(k_lo, made(n))
                    sp.dma_start(k_tab[ds(b * NH + h, 1)].rearrange("o p a s -> p (o a) s")[:, :, ds(k * TOK, TOK)],
                                 kt_o[:, h]).then_inc(qk_stored[h], 16)
                    if h == 0 and not first:
                        store_values(t - 1)

            load(0, 0)
            load(1, 1)
            load(2, 0)
            load(3, 1)
            store(0, first=True)
            load(4, 0)
            store(1)
            with sp.Fori(1, steps // 2 - 2) as i:
                load(2 * i + 3, 1)
                store(2 * i)
                load(2 * i + 4, 0)
                store(2 * i + 1)
            load(steps - 1, 1)
            for t in range(steps - 4, steps):
                store(t)
            store_values(steps - 1)
            for s in qk_stored:
                sp.wait_ge(s, 48 * (steps + 1))
            sp.wait_ge(v_stored, 64 * (steps + 1))
            sp.wait_ge(past_stored, 16 * (steps + 1))

        def over_steps(eng, step):
            step(0, 0, 0, 3)
            step(1, 0, 1, 3)
            with eng.Fori(1, steps // 2 - 1) as i:
                step(2 * i, i, 0, 3)
                step(2 * i + 1, i, 1, 3)
            step(steps - 2, steps // 2 - 1, 0, 2)
            step(steps - 1, steps // 2 - 1, 1, 1)

        @block.tensor
        def _(pe):
            for s in (rows_turned, queried, keyed, rotated, valued):
                pe.sem_inc(s, PRIME)
            pe.wait_ge(const_in, N_CONST)

            def query(n, h):
                pe.wait_ge(qv_made, made_before(n, 1))
                for c in range(2):
                    mm = nc.tensor.matmul(q_ps[:], wq_sb[:, c, h].rearrange("p a d -> p (a d)"), ht[:, c],
                                          start=(c == 0), stop=(c == 1))
                mm.then_inc(queried, 1)

            def key(n, h):
                pe.wait_ge(ks_made, made_before(n, 1))
                for c in range(2):
                    mm = nc.tensor.matmul(k_ps[:], wk_sb[:, c, h].rearrange("p a d -> p (a d)"), ht[:, c],
                                          start=(c == 0), stop=(c == 1))
                mm.then_inc(keyed, 1)

            def position(n, h):
                pe.wait_ge(qv_made, made(n))
                pe.wait_ge(products, made_before(n, 1))
                for a in range(2):
                    mm = nc.tensor.matmul(a_ps[:, a], wp_sb[:, h, a], qv[:, h % 2], start=True, stop=True)
                mm.then_inc(rotated, 1)

            def transposes(t):
                pe.wait_ge(shifted, made(t))
                for k in range(SUB):
                    for c in range(2):
                        tr = nc.tensor.transpose(t_ps[:, c, k * P:(k + 1) * P], xa[:, k, c * P:(c + 1) * P], ident[:])
                tr.then_inc(rows_turned, 1)

            def step(t, i, par, left):
                pe.wait_ge(ht_made, made(t))
                query(NH * t, 0)
                key(NH * t, 0)
                pe.wait_ge(v_scaled, made_before(t, 1))
                for h in range(NH):
                    n = NH * t + h
                    for c in range(2):
                        mm = nc.tensor.matmul(v_ps[:, h], ht[:, c, h * P:(h + 1) * P], wv_sb[:, c],
                                              start=(c == 0), stop=(c == 1))
                    if h < NH - 1:
                        query(n + 1, h + 1)
                        key(n + 1, h + 1)
                    else:
                        mm.then_inc(valued, 1)
                        if left > 1:
                            transposes(t + 1)
                    position(n, h)

            transposes(0)
            over_steps(pe, step)

        @block.scalar
        def _(act):
            for s in (root1, root2, ht_made, qs_made, qv_made, ks_made, b_hi, v_hi):
                act.sem_inc(s, PRIME)
            act.wait_ge(bias_made, 4)

            def roots(t, which):
                eps, inv, root, ve, sd = ((eps1, inv1, root1, ve1, sd1), (eps2, inv2, root2, ve2, sd2))[which]
                act.wait_ge(eps, made(t))
                act.wait_ge(inv, made_before(t, 1))
                nc.scalar.activation(sd[:], ve[:], ACT.Sqrt).then_inc(root, 1)

            def head(t, n, h):
                hp = h % 2
                act.wait_ge(queried, made(n))
                act.wait_ge(c_lo, made_before(n, 2))
                nc.scalar.activation(qs[:, hp], q_ps[:], ACT.Identity, bias=bqus[:, h:h + 1], scale=Q_SCALE)
                act.wait_ge(qk_stored[h], 48 * (t + 1))
                nc.scalar.activation(qt_o[:, h, 4], q_ps[:], ACT.Identity, bias=bqus[:, h:h + 1], scale=Q_SCALE
                                     ).then_inc(qs_made, 1)
                act.wait_ge(rotated, made_before(n, 2))
                nc.scalar.activation(qv[:, hp], q_ps[0:HD], ACT.Identity, bias=bqv[0:HD, h:h + 1]
                                     ).then_inc(qv_made, 1)
                act.wait_ge(keyed, made(n))
                act.wait_ge(k_lo, made_before(n, 2))
                nc.scalar.activation(ks[:, hp], k_ps[:], ACT.Identity, bias=bks[:, h:h + 1], scale=Q_SCALE)
                nc.scalar.activation(kt_o[:, h, 0], k_ps[:], ACT.Identity, bias=bks[:, h:h + 1], scale=Q_SCALE
                                     ).then_inc(ks_made, 1)

            def turned_high(n, h):
                act.wait_ge(bs_made, made(n))
                nc.scalar.activation(qt_o[:, h, 0:4:2], bs[:, h % 2], ACT.Copy).then_inc(b_hi, 1)

            def values_high(t):
                act.wait_ge(v_scaled, made(t))
                act.wait_ge(v_stored, 64 * (t + 1))
                nc.scalar.activation(vt_o[:, :, :, 0, :], vs[:].rearrange("p k (h d) -> p h k d", h=NH), ACT.Copy
                                     ).then_inc(v_hi, 1)

            def copy_rows(t):
                act.wait_ge(rows_turned, made(t))
                act.wait_ge(valued, made_before(t, 1))
                nc.scalar.activation(ht[:], t_ps[:], ACT.Copy).then_inc(ht_made, 1)

            def step(t, i, par, left):
                first = isinstance(t, int) and t == 0
                for h in range(NH):
                    head(t, NH * t + h, h)
                    if h == 3 and left > 2:
                        roots(t + 2, 0)
                    if not (first and h < 2):
                        turned_high(NH * t + h - 2, (h - 2) % NH)
                    if h == 1 and not first:
                        values_high(t - 1)
                if left > 1:
                    copy_rows(t + 1)
                if left > 2:
                    roots(t + 2, 1)

            roots(0, 0)
            roots(0, 1)
            copy_rows(0)
            roots(1, 0)
            roots(1, 1)
            over_steps(act, step)
            turned_high(NH * steps - 2, 2)
            turned_high(NH * steps - 1, 3)
            values_high(steps - 1)

        @block.vector
        def _(dve):
            for s in (stats1, mean1, eps1, inv1, norm1, stats2, mean2, eps2, inv2, norm2, products, c_lo, k_lo,
                      v_scaled, past_made, past_hi, past_lo):
                dve.sem_inc(s, PRIME)
            dve.wait_ge(const_in, N_CONST)
            nc.vector.tensor_tensor(bqu[:], bq_sb[:], ub[:], ALU.add).then_inc(bias_made, 1)
            nc.vector.tensor_tensor(bqv[0:HD], bq_sb[0:HD], vb[0:HD], ALU.add)
            nc.vector.tensor_scalar(bvs[:], bvb[:], V_SCALE, None, ALU.mult).then_inc(bias_made, 1)
            nc.vector.tensor_scalar(bks[:], bk_sb[:], Q_SCALE, None, ALU.mult).then_inc(bias_made, 1)
            dve.wait_ge(bias_made, 3)
            nc.vector.tensor_scalar(bqus[:], bqu[:], Q_SCALE, None, ALU.mult).then_inc(bias_made, 1)

            def moments(t, src, st, mv, ve, stats, mean, eps):
                for k in range(SUB):
                    op = nc.vector.bn_stats(st[:, k], src[:, k])
                op.then_inc(stats, 1)
                dve.wait_ge(stats, made(t))
                nc.vector.tensor_copy(spare[:], st[:, 0, 0:1])
                for k in range(SUB):
                    op = nc.vector.bn_aggr(mv[:, k], st[:, k])
                op.then_inc(mean, 1)
                dve.wait_ge(mean, made(t))
                nc.vector.tensor_scalar(ve[:], mv[:, :, 1], 1e-5, None, ALU.add).then_inc(eps, 1)

            def centre(t, dst, src, mv, sd, rs, root, inv, norm):
                dve.wait_ge(root, made(t))
                nc.vector.reciprocal(rs[:], sd[:]).then_inc(inv, 1)
                dve.wait_ge(inv, made(t))
                for k in range(SUB):
                    op = nc.vector.tensor_scalar(dst[:, k], src[:, k], mv[:, k, 0:1], rs[:, k:k + 1],
                                                 ALU.subtract, ALU.mult)
                op.then_inc(norm, 1)

            def norm_a(t, i, par):
                dve.wait_ge(x_in[par], 16 * (i + 1))
                moments(t, x_sb[:, par], st1, mv1, ve1, stats1, mean1, eps1)

            def norm_b(t, par):
                centre(t, xn, x_sb[:, par], mv1, sd1, rs1, root1, inv1, norm1)
                dve.wait_ge(norm1, made(t))
                moments(t, xn, st2, mv2, ve2, stats2, mean2, eps2)

            def norm_c(t):
                dve.wait_ge(gained, made_before(t, 1))
                centre(t, xm, xn, mv2, sd2, rs2, root2, inv2, norm2)

            def head(t, n, h):
                hp = h % 2
                col = (t % per_b) * TOK
                cos, sin = turn[:, 0, ds(col, TOK)], turn[:, 1, ds(col, TOK)]
                dve.wait_ge(qs_made, made(n))
                nc.vector.tensor_tensor(qt_o[HD:P, h, 4], qs[HD:P, hp], qt_o[HD:P, h, 4], ALU.subtract
                                        ).then_inc(c_lo, 1)
                dve.wait_ge(ks_made, made(n))
                nc.vector.tensor_tensor(kt_o[:, h, 1], ks[:, hp], kt_o[:, h, 0], ALU.subtract).then_inc(k_lo, 1)
                dve.wait_ge(rotated, made(n))
                dve.wait_ge(past_lo, made_before(t, 1))
                nc.vector.tensor_scalar(past[:, h], a_ps[:, :, TOK - 1], B_SCALE, None, ALU.mult
                                        ).then_inc(past_made, 1)
                dve.wait_ge(bs_made, made_before(n, 2))
                nc.vector.tensor_tensor(prod[:, hp, 0], a_ps[:, 0], cos, ALU.mult)
                nc.vector.tensor_tensor(prod[:, hp, 1], a_ps[:, 1], sin, ALU.mult)
                nc.vector.tensor_tensor(prod[:, hp, 2], a_ps[:, 1], cos, ALU.mult)
                nc.vector.tensor_tensor(prod[:, hp, 3], a_ps[:, 0], sin, ALU.mult).then_inc(products, 1)

            def step(t, i, par, left):
                for h in range(NH):
                    head(t, NH * t + h, h)
                    if left > 2 and h == 1:
                        norm_a(t + 2, i + 1, par)
                    if left > 2 and h == 2:
                        norm_b(t + 2, par)
                    if h == 3:
                        values(t)
                    if left > 2 and h == 3:
                        norm_c(t + 2)

            def values(t):
                dve.wait_ge(valued, made(t))
                dve.wait_ge(v_lo, made_before(t, 1))
                nc.vector.scalar_tensor_tensor(out=vs[:], in0=v_ps[:], scalar=V_SCALE, in1=over_rows(bvs),
                                               op0=ALU.mult, op1=ALU.add).then_inc(v_scaled, 1)
                dve.wait_ge(past_made, NH * (t + 1) + PRIME)
                dve.wait_ge(past_stored, 16 * (t + 1))
                nc.vector.tensor_copy(past_o[:, :, :, 0], past[:]).then_inc(past_hi, 1)
                dve.wait_ge(past_hi, made(t))
                nc.vector.tensor_tensor(past_o[:, :, :, 1], past[:], past_o[:, :, :, 0], ALU.subtract
                                        ).then_inc(past_lo, 1)

            for t in range(2):
                norm_a(t, 0, t)
                norm_b(t, t)
                norm_c(t)
            over_steps(dve, step)

        @block.gpsimd
        def _(pool):
            for s in (gained, shifted, bs_made, b_lo, v_lo):
                pool.sem_inc(s, PRIME)
            pool.wait_ge(const_in, N_CONST)

            def affine(t):
                pool.wait_ge(norm2, made(t))
                nc.gpsimd.tensor_tensor(xg[:], xm[:], over_rows(ga), ALU.mult).then_inc(gained, 1)
                pool.wait_ge(gained, made(t))
                pool.wait_ge(rows_turned, made_before(t, 1))
                nc.gpsimd.tensor_tensor(xa[:], xg[:], over_rows(be), ALU.add).then_inc(shifted, 1)

            def sums(n, hp):
                pool.wait_ge(products, made(n))
                pool.wait_ge(b_hi, made_before(n, 2))
                pool.wait_ge(b_lo, made_before(n, 2))
                nc.gpsimd.tensor_tensor(bs[:, hp, 0], prod[:, hp, 0], prod[:, hp, 1], ALU.add)
                nc.gpsimd.tensor_tensor(bs[:, hp, 1], prod[:, hp, 2], prod[:, hp, 3], ALU.subtract
                                        ).then_inc(bs_made, 1)

            def turned_low(n, h):
                pool.wait_ge(b_hi, made(n))
                nc.gpsimd.tensor_tensor(qt_o[:, h, 1:4:2], bs[:, h % 2], qt_o[:, h, 0:4:2], ALU.subtract
                                        ).then_inc(b_lo, 1)

            def values_low(t):
                pool.wait_ge(v_hi, made(t))
                nc.gpsimd.tensor_tensor(vt_o[:, :, :, 1, :], vs[:].rearrange("p k (h d) -> p h k d", h=NH),
                                        vt_o[:, :, :, 0, :], ALU.subtract).then_inc(v_lo, 1)

            def step(t, i, par, left):
                first = isinstance(t, int) and t == 0
                for h in range(NH):
                    if not (first and h < 2):
                        turned_low(NH * t + h - 2, (h - 2) % NH)
                    sums(NH * t + h, h % 2)
                    if h == 1 and left > 1:
                        affine(t + 1)
                    if h == 2 and not first:
                        values_low(t - 1)

            affine(0)
            over_steps(pool, step)
            turned_low(NH * steps - 2, 2)
            turned_low(NH * steps - 1, 3)
            values_low(steps - 1)


def ffn_phase(nc, batches, seq, x, ctx_in, w_out, b_out, wr, br, ff1_w, ff1_b, ff2_w, ff2_b, identity, prefix, out):
    per_b = seq // TOK
    steps = batches * per_b
    tiles = batches * seq // P
    bt = seq // P
    keep = seq // 2 - 1
    F = ff1_w.shape[1]
    MF = F // P
    CH = MF // 2
    with ExitStack() as ctx:
        m = Mem(nc, ctx, "ffn")
        z0 = m.sb("z0", [P, tiles * C])
        z1 = m.sb("z1", [P, tiles * C])
        wo = m.sb("wo", [P, 2, C])
        w1 = m.sb("w1", [P, 2, F])
        w2 = m.sb("w2", [P, MF, C])
        bo = m.sb("bo", [P, C])
        b1 = m.sb("b1", [P, MF])
        b2 = m.sb("b2", [P, C])
        wrb = m.sb("wrb", [P, C])
        brb = m.sb("brb", [P, 1])
        ident = m.sb("id", [P, P])
        pre = m.sb("pre", [P, 2 * P])
        c_sb = m.sb("c", [P, SUB, C])
        x_sb = m.sb("x", [P, SUB, C])
        xb = m.sb("xb", [P, SUB, C])
        t1 = m.sb("t1", [P, SUB, C])
        xf = m.sb("xf", [P, SUB, C])
        junk = m.sb("junk", [P, SUB, C])
        st = m.sb("st", [P, SUB, 6])
        mv = m.sb("mv", [P, SUB, 2])
        ve, sd, rs = m.sb("ve", [P, SUB]), m.sb("sd", [P, SUB]), m.sb("rs", [P, SUB])
        w_row = m.sb("w_row", [P, SUB])
        spare = m.sb("spare", [P, 1])
        w_all = m.sb("w_all", [P, tiles])
        ct = m.sb("ct", [P, 2, TOK])
        nt = m.sb("nt", [P, 2, TOK])
        gt = m.sb("gt", [P, MF, TOK])
        t_ps = m.psum("t_ps", [P, 2, TOK])
        f_ps = m.psum("f_ps", [P, 4, TOK])
        p_ps = m.psum("p_ps", [P, SUB, C])

        const_in, rows_in, wrapped = m.sem("const_in"), m.sem("rows_in"), m.sem("wrapped")
        ctx_turned, ct_a, ct_b, projected = m.sem("ctx_turned"), m.sem("ct_a"), m.sem("ct_b"), m.sem("projected")
        xb_made, t1_made, stats, mean = m.sem("xb_made"), m.sem("t1_made"), m.sem("stats"), m.sem("mean")
        eps, root, inv, normed = m.sem("eps"), m.sem("root"), m.sem("inv"), m.sem("normed")
        z0_made, routed, weighted = m.sem("z0_made"), m.sem("routed"), m.sem("weighted")
        rows_turned, nt_a, nt_b = m.sem("rows_turned"), m.sem("nt_a"), m.sem("nt_b")
        widened, gated, narrowed, z1_made = m.sem("widened"), m.sem("gated"), m.sem("narrowed"), m.sem("z1_made")
        step_done, counted, chosen, stored = m.sem("sel_step"), m.sem("counted"), m.sem("chosen"), m.sem("stored")
        out_made = m.sem("out_made")

        ke = m.sb("ke", [P, batches, bt], U32)
        fl = m.sb("fl", [P, batches, bt], U32)
        hb = m.sb("hb", [P, batches, bt], U32)
        lb = m.sb("lb", [P, batches, bt], U32)
        hi = m.sb("hi", [P, batches, bt])
        lo = m.sb("lo", [P, batches, bt])
        cmp_ = m.sb("cmp", [P, batches, bt])
        over = m.sb("over", [P, batches, bt])
        tie = m.sb("tie", [P, batches, bt])
        low_key = m.sb("low_key", [P, batches, bt])
        pad = bt
        scan = m.sb("scan", [P, 2, batches, pad + bt])
        cur = m.sb("cur", [P, 2, batches])
        cand = m.sb("cand", [P, batches])
        bit = m.sb("bit", [P, 2])
        cnt = m.sb("cnt", [P, batches])
        inc = m.sb("inc", [P, batches])
        want = m.sb("want", [P, 3, batches])
        fac = m.sb("fac", [P, tiles])
        block = ctx.enter_context(nc.Block())
        N_CONST = 11 * 16

        @block.sync
        def _(sp):
            for dst, src in ((wo[:], w_out.rearrange("(k p) n -> p k n", p=P)),
                             (w1[:], ff1_w.rearrange("(k p) n -> p k n", p=P)),
                             (w2[:], ff2_w.rearrange("(k p) n -> p k n", p=P)), (bo[:], spread(b_out)),
                             (b2[:], spread(ff2_b)), (wrb[:], spread(wr)), (brb[:], spread(br)),
                             (ident[:], identity), (pre[:], prefix)):
                sp.dma_start(dst, src).then_inc(const_in, 16)
            sp.dma_start(b1[:], columns(ff1_b), allow_slow_non_contiguous=True).then_inc(const_in, 16)
            sp.dma_start(ctx_in[:, seq, :], ctx_in[:, 0, :]).then_inc(const_in, 16)
            sp.wait_ge(const_in, N_CONST)

            def load(t):
                sp.wait_ge(ctx_turned, made_before(t, 1))
                sp.wait_ge(xb_made, made_before(t, 1))
                first = (t // per_b) * (seq + 1) + (t % per_b) * TOK + 1
                sp.dma_start(c_sb[:], rows(ctx_in.rearrange("b r c -> (b r) c"), first)).then_inc(rows_in, 16)
                sp.dma_start(x_sb[:], rows(x, t * TOK)).then_inc(rows_in, 16)

            with sp.Fori(0, steps) as t:
                load(t)
            with sp.Fori(0, steps) as t:
                sp.wait_ge(out_made, t + 1)
                sp.dma_start(rows(out, t * TOK), z0[:, ds(t * (SUB * C), SUB * C)].rearrange(
                    "p (k c) -> p k c", k=SUB)).then_inc(stored, 16)
            sp.wait_ge(stored, 16 * steps)

        @block.tensor
        def _(pe):
            for s in (ctx_turned, projected, rows_turned, narrowed):
                pe.sem_inc(s, PRIME)
            pe.sem_inc(widened, 2 * CH)
            pe.wait_ge(const_in, N_CONST)

            def context_transposes(t):
                pe.wait_ge(rows_in, 32 * (t + 1))
                pe.wait_ge(nt_a, made_before(t, 2))
                pe.wait_ge(nt_b, made_before(t, 2))
                for k in range(SUB):
                    for c in range(2):
                        tr = nc.tensor.transpose(t_ps[:, c, k * P:(k + 1) * P], c_sb[:, k, c * P:(c + 1) * P], ident[:])
                tr.then_inc(ctx_turned, 1)

            def project(t):
                pe.wait_ge(ct_a, made(t))
                pe.wait_ge(ct_b, made(t))
                pe.wait_ge(t1_made, made_before(t, 1))
                for k in range(SUB):
                    for c in range(2):
                        mm = nc.tensor.matmul(p_ps[:, k], ct[:, c, k * P:(k + 1) * P], wo[:, c],
                                              start=(c == 0), stop=(c == 1))
                mm.then_inc(projected, 1)

            def row_transposes(t):
                pe.wait_ge(normed, made(t))
                for k in range(SUB):
                    for c in range(2):
                        tr = nc.tensor.transpose(t_ps[:, c, k * P:(k + 1) * P], xf[:, k, c * P:(c + 1) * P], ident[:])
                tr.then_inc(rows_turned, 1)

            def widen(t):
                pe.wait_ge(nt_a, made(t))
                pe.wait_ge(nt_b, made(t))
                for q in range(CH):
                    pe.wait_ge(gated, CH * t + q - 1 + 2 * CH)
                    for o in range(2):
                        for c in range(2):
                            mm = nc.tensor.matmul(f_ps[:, 2 * (q % 2) + o], w1[:, c, (2 * q + o) * P:(2 * q + o + 1) * P],
                                                  nt[:, c], start=(c == 0), stop=(c == 1))
                    mm.then_inc(widened, 1)

            def narrow(t):
                pe.wait_ge(gated, CH * (t + 1) + 2 * CH)
                for k in range(SUB):
                    for c in range(MF):
                        mm = nc.tensor.matmul(p_ps[:, k], gt[:, c, k * P:(k + 1) * P], w2[:, c],
                                              start=(c == 0), stop=(c == MF - 1))
                mm.then_inc(narrowed, 1)

            def step(t, left=3):
                if left > 2:
                    context_transposes(t + 2)
                widen(t)
                pe.wait_ge(z1_made, made_before(t, 1))
                if left > 2:
                    project(t + 2)
                if left > 1:
                    row_transposes(t + 1)
                if left > 2:
                    pe.wait_ge(t1_made, made(t + 2))
                narrow(t)

            for t in range(2):
                context_transposes(t)
                project(t)
            row_transposes(0)
            with pe.Fori(0, steps - 2) as t:
                step(t)
            step(steps - 2, 2)
            step(steps - 1, 1)

            ones = pre[:, P:2 * P]
            with pe.Fori(0, 33) as n:
                pe.wait_ge(counted, n + 1)
                nc.tensor.matmul(t_ps[:, 0, 0:batches], ones, cnt[:], start=True, stop=True).then_inc(chosen, 1)
            pe.wait_ge(counted, 34)
            nc.tensor.matmul(t_ps[:, 0, 0:batches], ones, cnt[:], start=True, stop=True).then_inc(chosen, 1)
            tie_rows = tie[:].rearrange("p b t -> p (b t)")
            nc.tensor.matmul(t_ps[:, 1, 0:tiles], pre[:, 0:P], tie_rows, start=True, stop=True)
            nc.tensor.matmul(p_ps[:, 0, 0:tiles], ones, tie_rows, start=True, stop=True).then_inc(chosen, 1)

        @block.gpsimd
        def _(pool):
            for s in (xb_made, z0_made):
                pool.sem_inc(s, PRIME)
            pool.wait_ge(const_in, N_CONST)
            with pool.Fori(0, steps) as t:
                pool.wait_ge(rows_in, 32 * (t + 1))
                pool.wait_ge(t1_made, made_before(t, 1))
                nc.gpsimd.tensor_tensor(xb[:], x_sb[:], over_rows(bo), ALU.add).then_inc(xb_made, 1)
                pool.wait_ge(normed, made(t))
                nc.gpsimd.tensor_tensor(z0[:, ds(t * (SUB * C), SUB * C)].rearrange("p (k c) -> p k c", k=SUB),
                                        t1[:], xf[:], ALU.add).then_inc(z0_made, 1)

        @block.scalar
        def _(act):
            for s in (ct_a, root, nt_a):
                act.sem_inc(s, PRIME)
            act.sem_inc(gated, 2 * CH)
            act.wait_ge(const_in, N_CONST)

            def copy_context(t):
                act.wait_ge(ctx_turned, made(t))
                act.wait_ge(projected, made_before(t, 1))
                nc.scalar.activation(ct[:, 0], t_ps[:, 0], ACT.Copy).then_inc(ct_a, 1)

            def deviation(t):
                act.wait_ge(eps, made(t))
                act.wait_ge(inv, made_before(t, 1))
                nc.scalar.activation(sd[:], ve[:], ACT.Sqrt).then_inc(root, 1)

            def copy_rows(t):
                act.wait_ge(rows_turned, made(t))
                act.wait_ge(widened, CH * t + 2 * CH)
                nc.scalar.activation(nt[:, 0], t_ps[:, 0], ACT.Copy).then_inc(nt_a, 1)

            def step(t, left=3):
                if left > 2:
                    copy_context(t + 2)
                act.wait_ge(narrowed, made_before(t, 1))
                for q in range(CH):
                    act.wait_ge(widened, CH * t + q + 1 + 2 * CH)
                    for o in range(2):
                        ge = nc.scalar.activation(gt[:, 2 * q + o], f_ps[:, 2 * (q % 2) + o], ACT.Gelu_apprx_tanh,
                                                  bias=b1[:, 2 * q + o:2 * q + o + 1])
                    ge.then_inc(gated, 1)
                if left > 1:
                    copy_rows(t + 1)
                if left > 2:
                    deviation(t + 2)

            copy_context(0)
            deviation(0)
            copy_context(1)
            copy_rows(0)
            deviation(1)
            with act.Fori(0, steps - 2) as t:
                step(t)
            step(steps - 2, 2)
            step(steps - 1, 1)

        @block.vector
        def _(dve):
            for s in (ct_b, t1_made, stats, mean, eps, inv, normed, routed, weighted, nt_b, z1_made):
                dve.sem_inc(s, PRIME)
            dve.wait_ge(const_in, N_CONST)

            def copy_context(t):
                dve.wait_ge(ctx_turned, made(t))
                dve.wait_ge(projected, made_before(t, 1))
                nc.vector.tensor_copy(ct[:, 1], t_ps[:, 1]).then_inc(ct_b, 1)

            def residual(t):
                dve.wait_ge(projected, made(t))
                dve.wait_ge(xb_made, made(t))
                dve.wait_ge(z0_made, made_before(t, 1))
                nc.vector.tensor_tensor(t1[:], p_ps[:], xb[:], ALU.add).then_inc(t1_made, 1)

            def norm(t):
                dve.wait_ge(t1_made, made(t))
                for k in range(SUB):
                    op = nc.vector.bn_stats(st[:, k], t1[:, k])
                op.then_inc(stats, 1)
                dve.wait_ge(stats, made(t))
                nc.vector.tensor_copy(spare[:], st[:, 0, 0:1])
                for k in range(SUB):
                    op = nc.vector.bn_aggr(mv[:, k], st[:, k])
                op.then_inc(mean, 1)
                dve.wait_ge(mean, made(t))
                nc.vector.tensor_scalar(ve[:], mv[:, :, 1], 1e-5, None, ALU.add).then_inc(eps, 1)
                dve.wait_ge(root, made(t))
                nc.vector.reciprocal(rs[:], sd[:]).then_inc(inv, 1)
                dve.wait_ge(inv, made(t))
                dve.wait_ge(rows_turned, made_before(t, 1))
                for k in range(SUB):
                    op = nc.vector.tensor_scalar(xf[:, k], t1[:, k], mv[:, k, 0:1], rs[:, k:k + 1],
                                                 ALU.subtract, ALU.mult)
                op.then_inc(normed, 1)

            def route(t):
                dve.wait_ge(normed, made(t))
                for k in range(SUB):
                    op = nc.vector.tensor_tensor_reduce(out=junk[:, k], in0=xf[:, k], in1=wrb[:], scale=1.0, scalar=0.0,
                                                        op0=ALU.mult, op1=ALU.add, accum_out=w_row[:, k:k + 1])
                op.then_inc(routed, 1)
                dve.wait_ge(routed, made(t))
                nc.vector.tensor_scalar(w_all[:, ds(t * SUB, SUB)], w_row[:], brb[:, 0:1], None, ALU.add
                                        ).then_inc(weighted, 1)

            def copy_rows(t):
                dve.wait_ge(rows_turned, made(t))
                dve.wait_ge(widened, CH * t + 2 * CH)
                nc.vector.tensor_copy(nt[:, 1], t_ps[:, 1]).then_inc(nt_b, 1)

            def step(t, left=3):
                if left > 2:
                    copy_context(t + 2)
                    residual(t + 2)
                if left > 1:
                    copy_rows(t + 1)
                if left > 2:
                    norm(t + 2)
                    route(t + 2)
                dve.wait_ge(narrowed, made(t))
                nc.vector.tensor_tensor(z1[:, ds(t * (SUB * C), SUB * C)].rearrange("p (k c) -> p k c", k=SUB),
                                        p_ps[:], over_rows(b2), ALU.add).then_inc(z1_made, 1)

            copy_context(0)
            residual(0)
            norm(0)
            route(0)
            copy_context(1)
            residual(1)
            copy_rows(0)
            norm(1)
            route(1)
            with dve.Fori(0, steps - 2) as t:
                step(t)
            step(steps - 2, 2)
            step(steps - 1, 1)

            done = [0]

            def chained(ins):
                done[0] += 1
                ins.then_inc(step_done, 1)
                dve.wait_ge(step_done, done[0])

            dve.wait_ge(weighted, made(steps - 1))
            wv = w_all[:].rearrange("p (b t) -> p b t", b=batches)
            chained(nc.vector.tensor_scalar(fl[:].bitcast(mybir.dt.int32), wv.bitcast(mybir.dt.int32), 31, -2 ** 31,
                                            ALU.arith_shift_right, ALU.bitwise_or))
            chained(nc.vector.tensor_tensor(ke[:], wv.bitcast(U32), fl[:], ALU.bitwise_xor))
            nc.vector.tensor_scalar(hb[:], ke[:], 16, None, ALU.logical_shift_right)
            chained(nc.vector.tensor_scalar(lb[:], ke[:], 65535, None, ALU.bitwise_and))
            nc.vector.tensor_copy(hi[:], hb[:])
            nc.vector.tensor_copy(lo[:], lb[:])
            nc.vector.memset(want[:, 0], float(keep))
            nc.vector.memset(bit[:], 32768.0)
            nc.vector.memset(scan[:], 0.0)
            chained(nc.vector.memset(cur[:], 0.0))

            def count(key, op, least, base=None):
                for b in range(batches):
                    ins = nc.vector.tensor_scalar(cmp_[:, b], key[:, b], least[:, b:b + 1], 0.0, op, ALU.add,
                                                  accum_out=cnt[:, b:b + 1])
                ins.then_inc(counted, 1)

            first_loop = done[0]

            def largest(key, half, first):
                start = done[0]
                with dve.Fori(0, 16) as n:
                    base = start + 3 * n
                    nc.vector.tensor_scalar(cand[:], cur[:, half], bit[:, half:half + 1], None, ALU.add
                                            ).then_inc(step_done, 1)
                    dve.wait_ge(step_done, base + 1)
                    count(key, ALU.is_ge, cand)
                    dve.wait_ge(chosen, first + n + 1)
                    nc.vector.tensor_tensor(inc[:], t_ps[:, 0, 0:batches], want[:, half], ALU.is_ge
                                            ).then_inc(step_done, 1)
                    dve.wait_ge(step_done, base + 2)
                    nc.vector.scalar_tensor_tensor(out=cur[:, half], in0=inc[:], scalar=bit[:, half:half + 1],
                                                   in1=cur[:, half], op0=ALU.mult, op1=ALU.add)
                    nc.vector.tensor_scalar(bit[:, half:half + 1], bit[:, half:half + 1], 0.5, None, ALU.mult
                                            ).then_inc(step_done, 1)
                    dve.wait_ge(step_done, base + 3)
                done[0] += 48

            largest(hi, 0, 0)
            count(hi, ALU.is_gt, cur[:, 0])
            for b in range(batches):
                nc.vector.tensor_scalar(over[:, b], hi[:, b], cur[:, 0, b:b + 1], None, ALU.is_gt)
                op = nc.vector.tensor_scalar(tie[:, b], hi[:, b], cur[:, 0, b:b + 1], None, ALU.is_equal)
            chained(op)
            chained(nc.vector.scalar_tensor_tensor(out=low_key[:], in0=lo[:], scalar=1.0, in1=tie[:],
                                                   op0=ALU.add, op1=ALU.mult))
            chained(nc.vector.tensor_scalar(low_key[:], low_key[:], -1.0, None, ALU.add))
            dve.wait_ge(chosen, 17)
            chained(nc.vector.tensor_tensor(want[:, 1], want[:, 0], t_ps[:, 0, 0:batches], ALU.subtract))
            largest(low_key, 1, 17)
            for b in range(batches):
                nc.vector.tensor_scalar(tie[:, b], low_key[:, b], cur[:, 1, b:b + 1], None, ALU.is_equal)
            count(low_key, ALU.is_gt, cur[:, 1])
            dve.wait_ge(counted, 34)
            chained(nc.vector.tensor_tensor(over[:], over[:], cmp_[:], ALU.add))
            dve.wait_ge(chosen, 35)
            chained(nc.vector.tensor_tensor(want[:, 2], want[:, 1], t_ps[:, 0, 0:batches], ALU.subtract))
            tot = p_ps[:, 0, 0:tiles].rearrange("p (b t) -> p b t", b=batches)
            chained(nc.vector.tensor_copy(scan[:, 0, :, pad:], tot))
            side, d = 0, 1
            while d < bt:
                chained(nc.vector.tensor_tensor(scan[:, 1 - side, :, pad:], scan[:, side, :, pad:],
                                                scan[:, side, :, pad - d:pad + bt - d], ALU.add))
                side, d = 1 - side, 2 * d
            rank = low_key
            chained(nc.vector.tensor_tensor(rank[:], scan[:, side, :, pad:], tot, ALU.subtract))
            chained(nc.vector.tensor_tensor(rank[:], rank[:], t_ps[:, 1, 0:tiles].rearrange(
                "p (b t) -> p b t", b=batches), ALU.add))
            for b in range(batches):
                op = nc.vector.tensor_scalar(cmp_[:, b], rank[:, b], want[:, 2, b:b + 1], None, ALU.is_le)
            chained(op)
            chained(nc.vector.tensor_tensor(tie[:], tie[:], cmp_[:], ALU.mult))
            chained(nc.vector.tensor_tensor(over[:], over[:], tie[:], ALU.add))
            chained(nc.vector.tensor_tensor(fac[:].rearrange("p (b t) -> p b t", b=batches), over[:], wv, ALU.mult))
            dve.wait_ge(z0_made, made(steps - 1))
            dve.wait_ge(z1_made, made(steps - 1))
            with dve.Fori(0, steps) as t:
                for k in range(SUB):
                    tile = ds(t * (SUB * C) + k * C, C)
                    op = nc.vector.scalar_tensor_tensor(out=z0[:, tile], in0=z1[:, tile],
                                                        scalar=fac[:, ds(t * SUB + k, 1)], in1=z0[:, tile],
                                                        op0=ALU.mult, op1=ALU.add)
                op.then_inc(out_made, 1)


def flash_phase(nc, seq, heads, q_tab, q_past, k_tab, v_tab, pe_tab, diag_masks, identity, ctx_out):
    tiles = seq // P
    blocks = seq // 512
    spi = seq // 1024
    n_tiles = heads * tiles
    dim = 256
    sc = 1.0 / (math.sqrt(dim) * SCORE_SCALE)

    with ExitStack() as ctx:
        def sb(name, shape, dt):
            return ctx.enter_context(nc.sbuf_tensor(name, shape, dt))

        def psum(name, shape):
            return ctx.enter_context(nc.psum_tensor(name, shape, F32))

        def sem(name):
            return ctx.enter_context(nc.semaphore(name))

        pe_sb = sb("pe_sb", [P, 2, 2, 2 * seq], F16)
        k_sb = sb("k_sb", [P, 2 * 2 * seq], F16)
        v_sb = sb("v_sb", [P, 2 * tiles * P], F16)
        q_sb = sb("q_sb", [P, 2, 9 * P], F16)
        mask_sb = sb("mask_sb", [P, 2 * 256], F32)
        id_sb = sb("fid_sb", [P, P], F32)
        p_sb = sb("p_sb", [P, 2, 1024], F32)
        hi_sb = sb("hi_sb", [P, 2, 8, P], F16)
        lo_sb = sb("lo_sb", [P, 2, 8, P], F16)
        dmask = sb("dmask", [P, 256], F32)
        dsum = sb("dsum", [P, P], F32)
        NS = 2 * spi
        blk_max = sb("blk_max", [P, NS], F32)
        run_max = sb("run_max", [P, NS], F32)
        max_step = sb("max_step", [P, NS], F32)
        neg_max = sb("neg_max", [P, NS], F32)
        corr = sb("corr", [P, NS], F32)
        row_sum = sb("row_sum", [P, NS], F32)
        tot = sb("tot", [P, NS], F32)
        o_acc = sb("o_acc", [P, NS, P], F32)
        o_sum = sb("o_sum", [P, 64], F32)
        r_tot = sb("r_tot", [P, 1], F32)
        o_out = sb("o_out", [P, 2, 64], F32)

        s_ps = psum("s_ps", [P, 2, 1024])
        t_ps = psum("t_ps", [P, 8, P])
        o_ps = psum("o_ps", [P, 512])
        d_ps = psum("d_ps", [P, 512])

        const_in = sem("f_const_in")
        q_in = [sem(f"f_q_in{p}") for p in range(2)]
        kv_in = sem("f_kv_in")
        scored = sem("f_scored")
        exped = sem("f_exped")
        turned = sem("f_turned")
        hi_made = sem("f_hi_made")
        lo_made = sem("f_lo_made")
        pv_made = sem("f_pv_made")
        maxed = sem("f_maxed")
        o_added = sem("f_o_added")
        diag_read = sem("f_diag_read")
        ctx_made = sem("f_ctx_made")
        stored = sem("f_stored")
        out_free = sem("f_out_free")
        dve_step = sem("f_dve_step")
        fin_step = sem("f_fin_step")

        def head_of(g):
            return g // tiles

        def over_tiles(eng, query_tile):
            with eng.Fori(0, n_tiles // 4 - 1) as q4:
                for r in range(4):
                    query_tile(4 * q4 + r, r)
            for r in range(4):
                query_tile(n_tiles - 4 + r, r, last=r == 3)

        block = ctx.enter_context(nc.Block())

        @block.sync
        def _(sp):
            sp.dma_start(pe_sb[:], pe_tab).then_inc(const_in, 16)
            sp.dma_start(mask_sb[:], diag_masks).then_inc(const_in, 16)
            sp.dma_start(id_sb[:], identity).then_inc(const_in, 16)

            def load_kv(h):
                par = h % 2
                sp.dma_start(k_sb[:, ds(par * (2 * seq), 2 * seq)],
                             k_tab[ds(h, 1)].rearrange("o p a s -> p (o a s)")).then_inc(kv_in, 16)
                sp.dma_start(v_sb[:, ds(par * (tiles * P), tiles * P)],
                             v_tab[ds(h, 1)].rearrange("o p t d -> p (o t d)")).then_inc(kv_in, 16)

            def load_q(g, par, first=False):
                sp.wait_ge(scored, spi * g + PRIME)
                h, i = g // tiles, g % tiles
                q = q_sb[:, par, :].rearrange("p (n c) -> p n c", c=P)
                src = q_tab[ds(h, 1)].rearrange("o p n c -> p (o n) c")
                if first:
                    sp.dma_start(q[:, 0:4, 1:P], src[:, 0:4, 2:P + 1]).then_inc(q_in[par], 16)
                    sp.dma_start(q[:, 0:4, 0:1], q_past[ds(h, 1)].rearrange("o p n c -> p (o n) c"),
                                 allow_slow_non_contiguous=True).then_inc(q_in[par], 16)
                    sp.dma_start(q[:, 4:9, :], src[:, :, 0:P]).then_inc(q_in[par], 16)
                else:
                    sp.dma_start(q[:, 0:4, :], src[:, 0:4, ds(i * P + 1, P)]).then_inc(q_in[par], 16)
                    sp.dma_start(q[:, 4:8, :], src[:, 0:4, ds(i * P, P)]).then_inc(q_in[par], 16)
                    sp.dma_start(q[:, 8:9, :], src[:, 4:5, ds(i * P, P)]).then_inc(q_in[par], 16)

            load_kv(0)
            with sp.Fori(0, heads - 1) as h:
                g0 = h * tiles
                load_q(g0, 0, first=True)
                load_q(g0 + 1, 1)
                load_q(g0 + 2, 0)
                load_q(g0 + 3, 1)
                sp.wait_ge(pv_made, spi * g0 + PRIME)
                sp.wait_ge(kv_in, 32 * (h + 1))
                load_kv(h + 1)
                with sp.Fori(2, tiles // 2) as i2:
                    load_q(g0 + 2 * i2, 0)
                    load_q(g0 + 2 * i2 + 1, 1)
            load_q((heads - 1) * tiles, 0, first=True)
            load_q((heads - 1) * tiles + 1, 1)
            with sp.Fori(1, tiles // 2) as i2:
                load_q((heads - 1) * tiles + 2 * i2, 0)
                load_q((heads - 1) * tiles + 2 * i2 + 1, 1)

        @block.tensor
        def _(pe):
            pe.sem_inc(scored, PRIME + spi)
            pe.sem_inc(turned, PRIME)
            pe.sem_inc(pv_made, PRIME)
            pe.wait_ge(const_in, 48)

            def scores(g, r, s, half):
                h = head_of(g)
                par = r % 2
                i4 = (g % tiles) // 4
                kb = (h % 2) * (2 * seq)
                j = 2 * s + half
                out = s_ps[:, s % 2, half * 512:(half + 1) * 512]
                q = q_sb[:, par, :]
                content = q[:, 8 * P:9 * P]

                def part(sel, n):
                    if isinstance(sel, int):
                        return q[:, sel * 512 + n * P:sel * 512 + (n + 1) * P]
                    return q_sb[:, par, ds(sel * 512 + n * P, P)]

                def position(to, sel, first, n_keys, start=False):
                    for a in range(2):
                        for n, b in ((0, 0), (1, 0), (0, 1)):
                            mm = nc.tensor.matmul(to, part(sel, 2 * a + n), pe_sb[:, a, b, ds(first, n_keys)],
                                                  start=start and a + n + b == 0, stop=a == 1 and b == 1,
                                                  skip_group_check=True)
                    return mm

                if s == 0 and half == 0:
                    pe.wait_ge(q_in[par], 48 * (g // 2 + 1))
                    pe.wait_ge(kv_in, 32 * (h + 1))
                    col = i4 * 512
                    for a in range(2):
                        nc.tensor.matmul(out, content, k_sb[:, ds(kb + a * seq + col, 512)],
                                         start=(a == 0), stop=(a == 1), skip_group_check=True)
                    if r < 3:
                        position(out[:, (r + 1) * P:512], 0, col + (r + 1) * P, (3 - r) * P)
                    if r > 0:
                        position(out[:, 0:r * P], 1, col + seq, r * P)
                    pe.wait_ge(diag_read, made_before(g, 1))
                    for sel in (1, 0):
                        position(d_ps[:, (1 - sel) * P:(2 - sel) * P], sel, col + r * P + sel * seq, P, start=True)
                    return None
                col = ((i4 + j) % blocks) * 512
                past = (i4 + j) >= blocks
                for a in range(2):
                    nc.tensor.matmul(out, content, k_sb[:, ds(kb + a * seq + col, 512)],
                                     start=(a == 0), stop=False, skip_group_check=True)
                mm = position(out, past, (i4 + j) * 512, 512)
                return mm

            def turn(n, s):
                pe.wait_ge(exped, made(n))
                pe.wait_ge(lo_made, made_before(n, 1))
                for k in range(8):
                    tr = nc.tensor.transpose(t_ps[:, k, :], p_sb[:, s % 2, k * P:(k + 1) * P], id_sb[:])
                tr.then_inc(turned, 1)

            def weigh(g, n, s):
                h = head_of(g)
                i4 = (g % tiles) // 4
                vb = (h % 2) * (tiles * P)
                pe.wait_ge(hi_made, made(n))
                pe.wait_ge(o_added, made_before(n, 1))

                def tile_of(k):
                    return ((i4 + 2 * s + k // 4) % blocks) * 4 + k % 4

                for k in range(8):
                    nc.tensor.matmul(o_ps[:, 0:P], hi_sb[:, s % 2, k, :], v_sb[:, ds(vb + tile_of(k) * P, P)],
                                     start=(k == 0), stop=False, skip_group_check=True)
                pe.wait_ge(lo_made, made(n))
                for k in range(8):
                    mm = nc.tensor.matmul(o_ps[:, 0:64], lo_sb[:, s % 2, k, :], v_sb[:, ds(vb + tile_of(k) * P, 64)],
                                          start=False, stop=(k == 7), skip_group_check=True)
                mm.then_inc(pv_made, 1)

            def query_tile(g, r, last=False):
                for s in range(spi):
                    n = spi * g + s
                    turn(n, s)
                    ahead, s2 = (s + 2) // spi, (s + 2) % spi
                    if not (last and ahead):
                        scores(g + ahead, (r + ahead) % 4, s2, 0)
                        scores(g + ahead, (r + ahead) % 4, s2, 1).then_inc(scored, 1)
                    weigh(g, n, s)

            for s in range(2):
                scores(s // spi, s // spi, s % spi, 0)
                scores(s // spi, s // spi, s % spi, 1).then_inc(scored, 1)
            over_tiles(pe, query_tile)

        @block.vector
        def _(dve):
            for s_ in (lo_made, maxed, o_added, diag_read, ctx_made):
                dve.sem_inc(s_, PRIME)
            dve.wait_ge(const_in, 48)

            def row_max(g, r, s):
                par = r % 2
                n = spi * g + s
                x = par * spi + s
                base = CHAIN * g
                dve.wait_ge(scored, n + 1 + PRIME + spi)
                if s == 0:
                    variant = (g % tiles) < 1
                    nc.vector.tensor_tensor(dmask[:], d_ps[:, 0:256], mask_sb[:, ds(variant * 256, 256)],
                                            ALU.mult).then_inc(diag_read, 1)
                    dve.wait_ge(diag_read, made(g))
                    nc.vector.tensor_tensor(dsum[:], dmask[:, 0:P], dmask[:, P:2 * P],
                                            ALU.add).then_inc(dve_step, 1)
                    dve.wait_ge(dve_step, base + 1)
                    nc.vector.tensor_tensor(s_ps[:, 0, r * P:(r + 1) * P], s_ps[:, 0, r * P:(r + 1) * P], dsum[:],
                                            ALU.add).then_inc(dve_step, 1)
                    dve.wait_ge(dve_step, base + 2)
                    nc.vector.tensor_reduce(run_max[:, x:x + 1], s_ps[:, s % 2, :], AX_X, ALU.max).then_inc(dve_step, 1)
                    dve.wait_ge(dve_step, base + 3)
                else:
                    nc.vector.tensor_reduce(blk_max[:, x:x + 1], s_ps[:, s % 2, :], AX_X, ALU.max).then_inc(dve_step, 1)
                    dve.wait_ge(dve_step, base + 3 + 2 * s - 1)
                    nc.vector.tensor_tensor(run_max[:, x:x + 1], blk_max[:, x:x + 1], run_max[:, x - 1:x],
                                            ALU.max).then_inc(dve_step, 1)
                    dve.wait_ge(dve_step, base + 3 + 2 * s)
                if s:
                    nc.vector.tensor_tensor(max_step[:, x:x + 1], run_max[:, x - 1:x], run_max[:, x:x + 1],
                                            ALU.subtract)
                nc.vector.tensor_scalar(neg_max[:, x:x + 1], run_max[:, x:x + 1], -sc, math.log(P_SCALE),
                                        ALU.mult, ALU.add).then_inc(maxed, 1)

            CHAIN = 3 + 2 * (spi - 1)

            def low_part(n, s):
                dve.wait_ge(hi_made, made(n))
                dve.wait_ge(pv_made, made_before(n, 2))
                nc.vector.tensor_tensor(lo_sb[:, s % 2, :, :], t_ps[:], hi_sb[:, s % 2, :, :],
                                        ALU.subtract).then_inc(lo_made, 1)

            def add_output(g, par, s):
                n = spi * g + s
                x = par * spi + s
                dve.wait_ge(exped, made(n))
                dve.wait_ge(pv_made, made(n))
                if s:
                    dve.wait_ge(o_added, made_before(n, 1))
                    nc.vector.scalar_tensor_tensor(out=tot[:, x:x + 1], in0=tot[:, x - 1:x], scalar=corr[:, x:x + 1],
                                                   in1=row_sum[:, x:x + 1], op0=ALU.mult, op1=ALU.add)
                    nc.vector.scalar_tensor_tensor(out=o_acc[:, x, :], in0=o_acc[:, x - 1, :], scalar=corr[:, x:x + 1],
                                                   in1=o_ps[:, 0:P], op0=ALU.mult, op1=ALU.add).then_inc(o_added, 1)
                else:
                    nc.vector.tensor_copy(tot[:, x:x + 1], row_sum[:, x:x + 1])
                    nc.vector.tensor_copy(o_acc[:, x, :], o_ps[:, 0:P]).then_inc(o_added, 1)

            def finish(g, par):
                x = par * spi + spi - 1
                dve.wait_ge(o_added, made(spi * g + spi - 1))
                nc.vector.reciprocal(r_tot[:], tot[:, x:x + 1]).then_inc(fin_step, 1)
                nc.vector.tensor_tensor(o_sum[:], o_acc[:, x, 0:64], o_acc[:, x, 64:128], ALU.add).then_inc(fin_step, 1)
                dve.wait_ge(fin_step, 2 * g + 2)
                dve.wait_ge(out_free, made_before(g, 2))
                nc.vector.tensor_scalar(o_out[:, par, :], o_sum[:], r_tot[:, 0:1], 1.0 / V_SCALE,
                                        ALU.mult, ALU.mult).then_inc(ctx_made, 1)

            def query_tile(g, r, last=False):
                par = r % 2
                for s in range(spi):
                    ahead, s2 = (s + 1) // spi, (s + 1) % spi
                    if not (last and ahead):
                        row_max(g + ahead, (r + ahead) % 4, s2)
                    low_part(spi * g + s, s)
                    add_output(g, par, s)
                finish(g, par)

            row_max(0, 0, 0)
            over_tiles(dve, query_tile)

        @block.scalar
        def _(act):
            act.sem_inc(exped, PRIME)
            act.sem_inc(hi_made, PRIME)

            def exponentials(g, par, s):
                n = spi * g + s
                x = par * spi + s
                act.wait_ge(maxed, made(n))
                act.wait_ge(turned, made_before(n, 2))
                if s:
                    nc.scalar.activation(corr[:, x:x + 1], max_step[:, x:x + 1], ACT.Exp, scale=sc)
                nc.scalar.activation(p_sb[:, s % 2, :], s_ps[:, s % 2, :], ACT.Exp, bias=neg_max[:, x:x + 1],
                                     scale=sc, accum_out=row_sum[:, x:x + 1]).then_inc(exped, 1)

            def high_part(n, s):
                act.wait_ge(turned, made(n))
                act.wait_ge(pv_made, made_before(n, 2))
                nc.scalar.activation(hi_sb[:, s % 2, :, :], t_ps[:], ACT.Copy).then_inc(hi_made, 1)

            def query_tile(g, r, last=False):
                for s in range(spi):
                    high_part(spi * g + s, s)
                    ahead, s2 = (s + 1) // spi, (s + 1) % spi
                    if not (last and ahead):
                        exponentials(g + ahead, (r + ahead) % 2, s2)

            exponentials(0, 0, 0)
            over_tiles(act, query_tile)

        @block.gpsimd
        def _(pool):
            pool.sem_inc(out_free, PRIME)
            with pool.Fori(0, n_tiles // 2) as g2:
                for par in range(2):
                    g = 2 * g2 + par
                    pool.wait_ge(ctx_made, made(g))
                    pool.dma_start(ctx_out(g), o_out[:, par, :]).then_inc(stored, 16)
                    pool.wait_ge(stored, 16 * (g + 1))
                    pool.sem_inc(out_free, 1)


def two_layers(nc, x, norm1_w, norm2_w, w_qkv, w_proj, b_proj, l0_ff1_w, l0_ff1_b, l0_ff2_w, l0_ff2_b, gamma, beta,
               wq, bq, wk, bk, wv, bv, wpos_t, u_bias, v_bias, w_out, b_out, wr, br, ff1_w, ff1_b, ff2_w, ff2_b,
               rope, win_mask, turn_tab, pe_tab, diag_mask, identity, prefix, out):
    batches, height, width, c = x.shape
    seq = height * width
    n = batches * seq
    heads = batches * NH
    tiles = seq // P

    def scratch(name, shape, dt=F32):
        return nc.dram_tensor(name, shape, dt).ap()

    x = x.rearrange("b h w c -> (b h w) c")
    out = out.rearrange("b h w c -> (b h w) c")
    qk_t = scratch("qk_t", (2 * c, n))
    v_rows = scratch("v_rows", (n, c))
    ctx0 = scratch("ctx0", (n, c))
    x1 = scratch("x1", (n, c))
    q_tab = scratch("q_tab", (heads, P, 5, 1 + seq), F16)
    q_past = scratch("q_past", (heads, P, 4, 1), F16)
    k_tab = scratch("k_tab", (heads, P, 2, seq), F16)
    v_tab = scratch("v_tab", (heads, P, tiles, P), F16)
    ctx1 = scratch("ctx1", (batches, 1 + seq, c))
    ctx1_rows = ctx1.rearrange("b r c -> (b r) c")

    def ctx_out(g):
        b, h, i = g // (NH * tiles), (g // tiles) % NH, g % tiles
        return ctx1_rows[ds(b * (seq + 1) + i * P, P), ds(h * HD, HD)]

    qkv_phase(nc, n, seq, x, norm1_w, w_qkv, rope, identity, qk_t, v_rows)
    window_phase(nc, batches, height, width, qk_t, v_rows, win_mask, identity, ctx0)
    layer0_mlp_phase(nc, n, x, ctx0, w_proj, b_proj, norm2_w, l0_ff1_w, l0_ff1_b, l0_ff2_w, l0_ff2_b, identity, x1)
    tables_phase(nc, batches, seq, x1, gamma, beta, wq, bq, wk, bk, wv, bv, wpos_t, u_bias, v_bias, turn_tab,
                 identity, q_tab, q_past, k_tab, v_tab)
    flash_phase(nc, seq, heads, q_tab, q_past, k_tab, v_tab, pe_tab, diag_mask, identity, ctx_out)
    ffn_phase(nc, batches, seq, x1, ctx1, w_out, b_out, wr, br, ff1_w, ff1_b, ff2_w, ff2_b, identity, prefix, out)


def rope_table(height, width, pairs):
    q = pairs // 2
    inv = (1.0 / 10000.0 ** (np.arange(q, dtype=np.float32) / q)).astype(np.float32)
    by_row = np.arange(height, dtype=np.float32)[:, None] * inv
    by_col = np.arange(width, dtype=np.float32)[:, None] * inv
    angle = np.concatenate([np.broadcast_to(by_row[:, None], (height, width, q)),
                            np.broadcast_to(by_col[None], (height, width, q))], -1).reshape(height * width, pairs)
    return np.stack([np.cos(angle), np.sin(angle)]).astype(np.float32)


def window_masks(height, width, span=8, ks=7):
    mask = np.full((3, 2, width, span, width), -1e30, np.float32)
    left = np.clip(np.arange(width) - ks // 2, 0, width - ks)
    for kind, (y, first) in enumerate(((0, 0), (2, 4 - ks // 2), (height // 2 - 1, height - span))):
        for a in range(2):
            top = min(max(2 * y + a - ks // 2, 0), height - ks) - first
            for c in range(width):
                mask[kind, a, c, top:top + ks, left[c]:left[c] + ks] = 0
    return np.ascontiguousarray(mask.reshape(3, P, span * width).transpose(1, 0, 2).reshape(P, -1))


def frequencies(dim):
    return np.exp(np.arange(0, dim, 2, dtype=np.float32) * np.float32(-np.log(10000.0) / dim)).astype(np.float64)


def turn_table(seq, dim):
    angle = frequencies(dim)[:, None] * (np.arange(seq) + 1)[None]
    return (np.stack([np.cos(angle), np.sin(angle)], 1) * B_SCALE).astype(np.float32)


def pe_table(seq, dim):
    angle = frequencies(dim)[:, None] * np.arange(2 * seq)[None]
    value = np.stack([np.sin(angle), np.cos(angle)], 1) * PE_SCALE
    high = value.astype(np.float16)
    return np.stack([high, (value - high).astype(np.float16)], 2)


def diagonal_masks():
    r, c = np.arange(P)[:, None], np.arange(P)[None]
    below, above = (c < r).astype(np.float32), (c > r).astype(np.float32)
    above_first = above.copy()
    above_first[0, 0] = 1
    return np.ascontiguousarray(np.concatenate([below, above, below, above_first], 1))


_INS = ["x", "L0_conv_norm1_w", "L0_conv_norm2_w", "L0_conv_w_qkv", "L0_conv_w_proj", "L0_conv_b_proj",
        "L0_conv_ff1_w", "L0_conv_ff1_b", "L0_conv_ff2_w", "L0_conv_ff2_b", "L1_attn_ln_gamma", "L1_attn_ln_beta",
        "L1_attn_Wq", "L1_attn_bq", "L1_attn_Wk", "L1_attn_bk", "L1_attn_Wv", "L1_attn_bv", "L1_attn_Wpos",
        "L1_attn_u_bias", "L1_attn_v_bias", "L1_attn_Wout", "L1_attn_bout", "L1_ffn_wr", "L1_ffn_br", "L1_ffn_w1",
        "L1_ffn_b1", "L1_ffn_w2", "L1_ffn_b2"]


def kernel(**inputs):
    import numpy as _np
    import concourse.bacc as _bacc
    from concourse import mybir as _mybir
    from concourse.bass_utils import run_bass_kernel_spmd as _run

    data = {name: _np.asarray(inputs[name]) for name in _INS}
    height, width, dim = data["x"].shape[1:]
    data["L1_attn_Wpos"] = data["L1_attn_Wpos"].reshape(dim // 2, 2, NH, HD).transpose(3, 2, 1, 0)
    data["L1_ffn_wr"] = data["L1_ffn_wr"].reshape(-1)
    tri = _np.triu(_np.ones((P, P), _np.float32))
    data.update(rope=rope_table(height, width, dim // 2), win_mask=window_masks(height, width),
                turn_tab=turn_table(height * width, dim), pe_tab=pe_table(height * width, dim),
                diag_mask=diagonal_masks(), identity=_np.eye(P, dtype=_np.float32),
                prefix=_np.concatenate([tri, _np.ones((P, P), _np.float32)], 1))

    nc = _bacc.Bacc("TRN2", target_bir_lowering=False, num_devices=1)
    arrays, args = {}, []
    for name, a in data.items():
        a = _np.ascontiguousarray(a)
        arrays[f"in_{name}_dram"] = a
        args.append(nc.dram_tensor(f"in_{name}_dram", a.shape, _mybir.dt.from_np(a.dtype), kind="ExternalInput").ap())
    args.append(nc.dram_tensor("out_0_dram", data["x"].shape, _mybir.dt.float32, kind="ExternalOutput").ap())
    two_layers(nc, *args)
    r = _run(nc, [arrays], core_ids=[0])
    return r.results[0]["out_0_dram"]
```

```python
import numpy as np
import math
import concourse.bass as bass
from concourse import mybir
from contextlib import ExitStack

P = 128
F32 = mybir.dt.float32
F16 = mybir.dt.float16
U32 = mybir.dt.uint32
ALU = mybir.AluOpType
ACT = mybir.ActivationFunctionType
AX_X = mybir.AxisListType.X
ds = bass.ds

PRIME = 2


def made(n, per=1):
    return (n + 1 + PRIME) * per


def made_before(n, back, per=1):
    return (n + 1 + PRIME - back) * per


Q_SCALE = 32.0
B_SCALE = 8.0
PE_SCALE = 128.0
V_SCALE = 32.0
SCORE_SCALE = Q_SCALE * Q_SCALE
assert SCORE_SCALE == B_SCALE * PE_SCALE
P_SCALE = 1024.0


TOK = 512
SUB = TOK // P
C = 256
NH = 4
HD = C // NH

W_SCALE = 64.0
ROW_SCALE = 16.0
GATE_SCALE = 8.0


class Mem:

    def __init__(self, nc, ctx, tag):
        self.nc, self.ctx, self.tag = nc, ctx, tag
        self.sems = []

    def sb(self, name, shape, dt=F32):
        return self.ctx.enter_context(self.nc.sbuf_tensor(f"{self.tag}_{name}", shape, dt))

    def psum(self, name, shape):
        return self.ctx.enter_context(self.nc.psum_tensor(f"{self.tag}_{name}", shape, F32))

    def sem(self, name):
        s = self.nc.alloc_semaphore(name=f"{self.tag}_{name}")
        self.sems.append(s)
        return s

    def clear_semaphores(self):
        self.nc.clear_and_free_semaphores(self.sems)
        self.nc.all_engine_barrier()


def bounded(value, most):
    return value if isinstance(value, int) else value.with_bounds(min_val=0, max_val=most)


def rows(dram, first, n=SUB):
    return dram[ds(first, n * P), :].rearrange("(k p) c -> p k c", p=P)


def spread(vec, n=P):
    return vec.rearrange("(o c) -> o c", o=1).to_broadcast([n, vec.shape[0]])


def columns(vec):
    return vec.rearrange("(k p) -> p k", p=P)


def over_rows(tile):
    return tile[:].rearrange("p (o c) -> p o c", o=1).to_broadcast([P, SUB, tile.shape[1]])


def in_pairs(eng, steps, step):
    with eng.Fori(0, steps // 2 - 1) as i:
        step(2 * i, i, 0, 3)
        step(2 * i + 1, i, 1, 3)
    step(steps - 2, steps // 2 - 1, 0, 2)
    step(steps - 1, steps // 2 - 1, 1, 1)


def qkv_phase(nc, n_tok, seq, x, norm_w, w_qkv, rope, identity, qk_t, v_out):
    steps = n_tok // TOK
    with ExitStack() as ctx:
        m = Mem(nc, ctx, "qkv")
        w_sb = m.sb("w", [P, 2, 3 * C])
        nw = m.sb("nw", [P, C])
        ident = m.sb("id", [P, P])
        x_sb = m.sb("x", [P, 2, SUB, C])
        rope_sb = m.sb("rope", [P, 2, 2, SUB, P])
        junk = m.sb("junk", [P, SUB, C])
        ss = m.sb("ss", [P, 2, SUB])
        ms = m.sb("ms", [P, 2, SUB])
        sd = m.sb("sd", [P, 2, SUB])
        rs = m.sb("rs", [P, 2, SUB])
        xn = m.sb("xn", [P, SUB, C])
        t_v = m.sb("t_v", [P, 2, SUB, P])
        t_p = m.sb("t_p", [P, 2, SUB, P])
        h_sb = m.sb("h", [P, 2, SUB, C])
        ht = m.sb("ht", [P, 2, 2, TOK])
        qk_o = m.sb("qk_o", [P, 2, 2, 4, TOK], F16)
        v_o = m.sb("v_o", [P, 2, SUB, 2, C], F16)
        t_ps = m.psum("t_ps", [P, 2, TOK])
        qk_ps = m.psum("qk_ps", [P, 4, TOK])
        v_ps = m.psum("v_ps", [P, SUB, C])

        const_in = m.sem("const_in")
        x_in = [m.sem(f"x_in{p}") for p in range(2)]
        stored = [m.sem(f"stored{p}") for p in range(2)]
        squared = m.sem("squared")
        meaned = m.sem("meaned")
        rooted = m.sem("rooted")
        inverted = m.sem("inverted")
        normed = m.sem("normed")
        halves = m.sem("halves")
        even_done = m.sem("even_done")
        pool_step = m.sem("pool_step")
        odd_done = m.sem("odd_done")
        turned = m.sem("turned")
        ht_a = m.sem("ht_a")
        ht_b = m.sem("ht_b")
        qk_made = m.sem("qk_made")
        v_made = m.sem("v_made")
        qk_hi, qk_lo = m.sem("qk_hi"), m.sem("qk_lo")
        v_hi, v_lo = m.sem("v_hi"), m.sem("v_lo")
        ctx.callback(m.clear_semaphores)
        block = ctx.enter_context(nc.Block())

        @block.sync
        def _(sp):
            for s in stored:
                sp.sem_inc(s, 48)

            def load(t, par):
                sp.wait_ge(even_done, made_before(t, 2))
                sp.wait_ge(odd_done, made_before(t, 2))
                sp.dma_start(x_sb[:, par], rows(x, t * TOK)).then_inc(x_in[par], 16)
                pos = (t % (seq // TOK)) * TOK
                for a in range(2):
                    sp.dma_start(rope_sb[:, par, a], rows(rope[a], pos)).then_inc(x_in[par], 16)

            def store(t, par):
                sp.wait_ge(qk_lo, made(t))
                sp.wait_ge(v_lo, made(t))
                sp.dma_start(rows(v_out, t * TOK), v_o[:, par].rearrange("p k a c -> p k (a c)")
                             ).then_inc(stored[par], 16)
                for a in range(2):
                    sp.dma_start(qk_t[a].rearrange("(m p) t -> p m t", p=P)[:, :, ds(t * TOK, TOK)],
                                 qk_o[:, par, a]).then_inc(stored[par], 16)

            load(0, 0)
            sp.dma_start(nw[:], spread(norm_w)).then_inc(const_in, 16)
            sp.dma_start(ident[:], identity).then_inc(const_in, 16)
            sp.dma_start(w_sb[:], w_qkv.rearrange("(k p) n -> p k n", p=P)).then_inc(const_in, 16)
            load(1, 1)
            load(2, 0)
            with sp.Fori(0, steps // 2 - 2) as i:
                load(2 * i + 3, 1)
                store(2 * i, 0)
                load(2 * i + 4, 0)
                store(2 * i + 1, 1)
            load(steps - 1, 1)
            for t in range(steps - 4, steps):
                store(t, t % 2)
            for s in stored:
                sp.wait_ge(s, 48 * (steps // 2 + 1))

        @block.scalar
        def _(act):
            for s in (squared, rooted, ht_a, qk_hi, v_hi):
                act.sem_inc(s, PRIME)

            def norm(t, i, par):
                act.wait_ge(x_in[par], 48 * (i + 1))
                for k in range(SUB):
                    sq = nc.scalar.activation(junk[:, k], x_sb[:, par, k], ACT.Square, accum_out=ss[:, par, k:k + 1])
                sq.then_inc(squared, 1)
                act.wait_ge(meaned, made(t))
                nc.scalar.activation(sd[:, par], ms[:, par], ACT.Sqrt).then_inc(rooted, 1)

            def copy_rows(t, par):
                act.wait_ge(turned, made(t))
                nc.scalar.activation(ht[:, par, 0], t_ps[:, 0], ACT.Copy).then_inc(ht_a, 1)

            def step(t, i, par, left):
                if left > 1:
                    copy_rows(t + 1, 1 - par)
                if left > 2:
                    norm(t + 2, i + 1, par)
                act.wait_ge(qk_made, made(t))
                act.wait_ge(stored[par], 48 * (i + 1))
                nc.scalar.activation(qk_o[:, par, 0], qk_ps[:], ACT.Copy, scale=Q_SCALE).then_inc(qk_hi, 1)
                act.wait_ge(v_made, made(t))
                nc.scalar.activation(v_o[:, par, :, 0], v_ps[:], ACT.Copy, scale=V_SCALE).then_inc(v_hi, 1)

            norm(0, 0, 0)
            norm(1, 0, 1)
            copy_rows(0, 0)
            in_pairs(act, steps, step)

        @block.vector
        def _(dve):
            for s in (meaned, inverted, normed, halves, even_done, ht_b, qk_lo, v_lo):
                dve.sem_inc(s, PRIME)
            dve.wait_ge(const_in, 48)

            def rotate(t, i, par):
                dve.wait_ge(squared, made(t))
                nc.vector.tensor_scalar(ms[:, par], ss[:, par], 1.0 / C, 1e-6, ALU.mult, ALU.add).then_inc(meaned, 1)
                dve.wait_ge(rooted, made(t))
                nc.vector.reciprocal(rs[:, par], sd[:, par]).then_inc(inverted, 1)
                dve.wait_ge(inverted, made(t))
                dve.wait_ge(x_in[par], 48 * (i + 1))
                dve.wait_ge(odd_done, made_before(t, 1))
                for k in range(SUB):
                    st = nc.vector.scalar_tensor_tensor(out=xn[:, k], in0=x_sb[:, par, k], scalar=rs[:, par, k:k + 1],
                                                        in1=nw[:], op0=ALU.mult, op1=ALU.mult)
                st.then_inc(normed, 1)
                dve.wait_ge(normed, made(t))
                ev, od = xn[:, :, 0::2], xn[:, :, 1::2]
                nc.vector.tensor_tensor(t_v[:, 0], ev, rope_sb[:, par, 0], ALU.mult)
                nc.vector.tensor_tensor(t_v[:, 1], od, rope_sb[:, par, 1], ALU.mult).then_inc(halves, 1)
                dve.wait_ge(halves, made(t))
                dve.wait_ge(turned, made_before(t, 2))
                nc.vector.tensor_tensor(h_sb[:, par, :, 0::2], t_v[:, 0], t_v[:, 1],
                                        ALU.subtract).then_inc(even_done, 1)

            def copy_rows(t, par):
                dve.wait_ge(turned, made(t))
                nc.vector.tensor_copy(ht[:, par, 1], t_ps[:, 1]).then_inc(ht_b, 1)

            def step(t, i, par, left):
                if left > 1:
                    copy_rows(t + 1, 1 - par)
                if left > 2:
                    rotate(t + 2, i + 1, par)
                dve.wait_ge(qk_hi, made(t))
                nc.vector.scalar_tensor_tensor(out=qk_o[:, par, 1], in0=qk_ps[:], scalar=Q_SCALE, in1=qk_o[:, par, 0],
                                               op0=ALU.mult, op1=ALU.subtract).then_inc(qk_lo, 1)
                dve.wait_ge(v_hi, made(t))
                nc.vector.scalar_tensor_tensor(out=v_o[:, par, :, 1], in0=v_ps[:], scalar=V_SCALE,
                                               in1=v_o[:, par, :, 0], op0=ALU.mult, op1=ALU.subtract
                                               ).then_inc(v_lo, 1)

            rotate(0, 0, 0)
            rotate(1, 0, 1)
            copy_rows(0, 0)
            in_pairs(dve, steps, step)

        @block.gpsimd
        def _(pool):
            for s in (pool_step, odd_done):
                pool.sem_inc(s, PRIME)

            def step(t, par):
                pool.wait_ge(normed, made(t))
                ev, od = xn[:, :, 0::2], xn[:, :, 1::2]
                nc.gpsimd.tensor_tensor(t_p[:, 0], ev, rope_sb[:, par, 1], ALU.mult)
                nc.gpsimd.tensor_tensor(t_p[:, 1], od, rope_sb[:, par, 0], ALU.mult).then_inc(pool_step, 1)
                pool.wait_ge(pool_step, made(t))
                pool.wait_ge(turned, made_before(t, 2))
                nc.gpsimd.tensor_tensor(h_sb[:, par, :, 1::2], t_p[:, 0], t_p[:, 1], ALU.add).then_inc(odd_done, 1)

            with pool.Fori(0, steps // 2) as i:
                step(2 * i, 0)
                step(2 * i + 1, 1)

        @block.tensor
        def _(pe):
            for s in (turned, qk_made, v_made):
                pe.sem_inc(s, PRIME)
            pe.wait_ge(const_in, 48)

            def transposes(t, par):
                pe.wait_ge(even_done, made(t))
                pe.wait_ge(odd_done, made(t))
                pe.wait_ge(ht_a, made_before(t, 1))
                pe.wait_ge(ht_b, made_before(t, 1))
                for k in range(SUB):
                    for c in range(2):
                        tr = nc.tensor.transpose(t_ps[:, c, k * P:(k + 1) * P], h_sb[:, par, k, c * P:(c + 1) * P],
                                                 ident[:])
                tr.then_inc(turned, 1)

            def step(t, i, par, left):
                if left > 1:
                    transposes(t + 1, 1 - par)
                pe.wait_ge(ht_a, made(t))
                pe.wait_ge(ht_b, made(t))
                pe.wait_ge(qk_lo, made_before(t, 1))
                for o in range(4):
                    for c in range(2):
                        mm = nc.tensor.matmul(qk_ps[:, o], w_sb[:, c, o * P:(o + 1) * P], ht[:, par, c],
                                              start=(c == 0), stop=(c == 1))
                mm.then_inc(qk_made, 1)
                pe.wait_ge(v_lo, made_before(t, 1))
                for k in range(SUB):
                    for c in range(2):
                        mm = nc.tensor.matmul(v_ps[:, k], ht[:, par, c, k * P:(k + 1) * P], w_sb[:, c, 2 * C:3 * C],
                                              start=(c == 0), stop=(c == 1))
                mm.then_inc(v_made, 1)

            transposes(0, 0)
            in_pairs(pe, steps, step)


def window_phase(nc, batches, rows_, cols, qk_t, v, masks, identity, ctx_out):
    KS = 7
    pairs = rows_ // 2
    units = batches * pairs
    span = 8
    assert cols == 64 and span * cols == 512
    last = rows_ - span
    hi_y = pairs - 2
    EXP_SCALE = HD ** -0.5 / SCORE_SCALE
    UB = 4
    with ExitStack() as ctx:
        m = Mem(nc, ctx, "win")
        mask_sb = m.sb("mask", [P, 3 * 512])
        ident = m.sb("id", [P, P])
        mask_u = m.sb("mask_u", [P, 512])
        spare = m.sb("spare", [P, 1])
        q_sb = m.sb("q", [P, UB, NH, P], F16)
        q_lo = m.sb("q_lo", [HD, UB, NH, P], F16)
        k_sb = m.sb("k", [P, UB, NH, 512], F16)
        v_sb = m.sb("v", [P, UB, SUB, 2, C], F16)
        s_sb = m.sb("s", [P, 2, 2, 512])
        mx = m.sb("mx", [P, 2, 2])
        nm = m.sb("nm", [P, 2, 2])
        p_sb = m.sb("p", [P, 2, 2, 512])
        sm = m.sb("sm", [P, 2, 2])
        rs = m.sb("rs", [P, 2, 2])
        pt = m.sb("pt", [P, 2, 2, 2, 512], F16)
        o_sb = m.sb("o", [P, 2, NH, HD])
        s_ps = m.psum("s_ps", [P, 4, 512])
        t_ps = m.psum("t_ps", [P, 2, 512])
        o_ps = m.psum("o_ps", [P, 2, 512])

        const_in = m.sem("const_in")
        qkv_in = [m.sem(f"qkv_in{p}") for p in range(UB)]
        stored = [m.sem(f"stored{p}") for p in range(2)]
        scored = m.sem("scored")
        masked = m.sem("masked")
        maxed = m.sem("maxed")
        negated = m.sem("negated")
        exped = m.sem("exped")
        turned = m.sem("turned")
        pt_hi = m.sem("pt_hi")
        pt_lo = m.sem("pt_lo")
        weighed = m.sem("weighed")
        inverted = m.sem("inverted")
        out_made = m.sem("out_made")
        ctx.callback(m.clear_semaphores)
        block = ctx.enter_context(nc.Block())

        @block.sync
        def _(sp):
            sp.dma_start(mask_sb[:], masks).then_inc(const_in, 16)
            sp.dma_start(ident[:], identity).then_inc(const_in, 16)
            for s in stored:
                sp.sem_inc(s, 16)

            def load(u, buf, first=False):
                b, y = u // pairs, u % pairs
                inner = (y >= 2) * (y < hi_y)
                top = (2 * y - KS // 2) * inner + last * (y >= hi_y)
                tok = b * (rows_ * cols) + y * P
                key = bounded(b * (rows_ * cols) + top * cols, batches * rows_ * cols - 512)
                if not first:
                    sp.wait_ge(weighed, made(2 * (u - UB) + 1))
                hi, lo = (qk_t[a].rearrange("(a h d) t -> a d h t", a=2, h=NH) for a in range(2))
                q_cols, k_cols = ds(tok, P), ds(key, 512)
                for dst, src in ((q_sb[0:HD, buf], hi[0][:, :, q_cols]), (q_sb[HD:P, buf], hi[0][:, :, q_cols]),
                                 (q_lo[:, buf], lo[0][:, :, q_cols]), (k_sb[0:HD, buf], hi[1][:, :, k_cols]),
                                 (k_sb[HD:P, buf], lo[1][:, :, k_cols]),
                                 (v_sb[:, buf].rearrange("p k a c -> p k (a c)"), rows(v, key))):
                    sp.dma_start(dst, src).then_inc(qkv_in[buf], 16)

            def store(u, par):
                sp.wait_ge(out_made, made(2 * u + 1))
                sp.dma_start(ctx_out[ds(u * P, P), :], o_sb[:, par].rearrange("p h d -> p (h d)")
                             ).then_inc(stored[par], 16)

            for u in range(UB):
                load(u, u, first=True)
            with sp.Fori(0, units // UB - 1) as i:
                for a in range(UB):
                    store(UB * i + a, a % 2)
                    load(UB * (i + 1) + a, a)
            for u in range(units - UB, units):
                store(u, u % 2)
            for s in stored:
                sp.wait_ge(s, 16 * (units // 2 + 1))

        def pipeline(eng, scores, turn, weigh, turn_first=False):
            for n in range(2):
                scores(n, 0, n)
            turn(0, 0)

            def item(i, j, left=2 * UB):
                n = 2 * UB * i + j
                if turn_first and left > 1:
                    turn(n + 1, j + 1)
                if left > 2:
                    scores(n + 2, i + (j + 2) // (2 * UB), (j + 2) % (2 * UB))
                weigh(n, i, j)
                if left > 1 and not turn_first:
                    turn(n + 1, j + 1)

            with eng.Fori(0, units // UB - 1) as i:
                for j in range(2 * UB):
                    item(i, j)
            for j in range(2 * UB):
                item(units // UB - 1, j, left=2 * UB - j)

        @block.tensor
        def _(pe):
            for s in (scored, weighed):
                pe.sem_inc(s, PRIME)
            pe.sem_inc(turned, 2 * PRIME)
            pe.wait_ge(const_in, 32)

            def scores(n, i, j):
                if j % 2 == 0:
                    pe.wait_ge(qkv_in[j // 2], 96 * (i + 1))
                pe.wait_ge(maxed, made_before(n, 2))
                for a in range(2):
                    h = 2 * (j % 2) + a
                    nc.tensor.matmul(s_ps[:, h], q_sb[:, j // 2, h], k_sb[:, j // 2, h], start=True, stop=False)
                    mm = nc.tensor.matmul(s_ps[:, h], q_lo[:, j // 2, h], k_sb[0:HD, j // 2, h],
                                          start=False, stop=True)
                mm.then_inc(scored, 1)

            def turn(n, j):
                pe.wait_ge(exped, made(n))
                for a in range(2):
                    pe.wait_ge(pt_lo, made_before(n, 1, 2) - 1 + a)
                    for c in range(4):
                        tr = nc.tensor.transpose(t_ps[:, a, c * P:(c + 1) * P],
                                                 p_sb[:, j % 2, a, c * P:(c + 1) * P], ident[:])
                    tr.then_inc(turned, 1)

            def weigh(n, i, j):
                pe.wait_ge(out_made, made_before(n, 2))
                for a in range(2):
                    pe.wait_ge(pt_lo, made(n, 2) - 1 + a)
                    h = 2 * (j % 2) + a
                    for c in range(4):
                        for x, y in ((0, 0), (0, 1), (1, 0)):
                            mm = nc.tensor.matmul(o_ps[:, j % 2, a * HD:(a + 1) * HD],
                                                  pt[:, j % 2, x, a, c * P:(c + 1) * P],
                                                  v_sb[:, j // 2, c, y, h * HD:(h + 1) * HD],
                                                  start=(x + y + c == 0), stop=(x == 1 and c == 3))
                mm.then_inc(weighed, 1)

            pipeline(pe, scores, turn, weigh)

        @block.vector
        def _(dve):
            for s in (masked, maxed, negated, inverted, out_made):
                dve.sem_inc(s, PRIME)
            dve.sem_inc(pt_lo, 2 * PRIME)
            dve.wait_ge(const_in, 32)

            def find_max(n, i, j):
                if j % 2 == 0:
                    y = (n // 2) % pairs
                    kind = (y >= 2) + (y >= hi_y) if not isinstance(y, int) else int(y >= 2) + int(y >= hi_y)
                    dve.wait_ge(maxed, made_before(n, 1))
                    nc.vector.tensor_copy(mask_u[:], mask_sb[:, ds(kind * 512, 512)]).then_inc(masked, 1)
                    dve.wait_ge(masked, made(n // 2))
                dve.wait_ge(scored, made(n))
                dve.wait_ge(exped, made_before(n, 2))
                nc.vector.tensor_copy(spare[:], mask_u[:, 0:1])
                for a in range(2):
                    op = nc.vector.tensor_tensor_reduce(out=s_sb[:, j % 2, a], in0=s_ps[:, 2 * (j % 2) + a],
                                                        in1=mask_u[:], scale=1.0, scalar=-3e38, op0=ALU.add,
                                                        op1=ALU.max, accum_out=mx[:, j % 2, a:a + 1])
                op.then_inc(maxed, 1)
                dve.wait_ge(maxed, made(n))
                nc.vector.tensor_scalar(nm[:, j % 2], mx[:, j % 2], -EXP_SCALE, math.log(P_SCALE), ALU.mult, ALU.add
                                        ).then_inc(negated, 1)

            def low_part(n, j):
                dve.wait_ge(weighed, made_before(n, 2))
                for a in range(2):
                    dve.wait_ge(pt_hi, made(n, 2) - 1 + a)
                    nc.vector.tensor_tensor(pt[:, j % 2, 1, a], t_ps[:, a], pt[:, j % 2, 0, a], ALU.subtract
                                            ).then_inc(pt_lo, 1)

            def finish(n, i, j):
                dve.wait_ge(exped, made(n))
                nc.vector.reciprocal(rs[:, j % 2], sm[:, j % 2]).then_inc(inverted, 1)
                dve.wait_ge(inverted, made(n))
                dve.wait_ge(weighed, made(n))
                if j % 2 == 0:
                    dve.wait_ge(stored[j // 2 % 2], 16 * (UB // 2 * i + j // 4 + 1))
                nc.vector.scalar_tensor_tensor(out=o_sb[:, j // 2 % 2, 2 * (j % 2):2 * (j % 2) + 2],
                                               in0=o_ps[:, j % 2, 0:2 * HD].rearrange("p (h d) -> p h d", h=2),
                                               scalar=1.0 / V_SCALE,
                                               in1=rs[:, j % 2].rearrange("p (h o) -> p h o", o=1).to_broadcast(
                                                   [P, 2, HD]), op0=ALU.mult, op1=ALU.mult).then_inc(out_made, 1)

            pipeline(dve, find_max, low_part, finish)

        @block.scalar
        def _(act):
            act.sem_inc(exped, PRIME)
            act.sem_inc(pt_hi, 2 * PRIME)

            def exponentials(n, i, j):
                act.wait_ge(negated, made(n))
                act.wait_ge(turned, made_before(n, 2, 2))
                act.wait_ge(inverted, made_before(n, 2))
                for a in range(2):
                    ex = nc.scalar.activation(p_sb[:, j % 2, a], s_sb[:, j % 2, a], ACT.Exp, bias=nm[:, j % 2, a:a + 1],
                                              scale=EXP_SCALE, accum_out=sm[:, j % 2, a:a + 1])
                ex.then_inc(exped, 1)

            def high_part(n, j):
                act.wait_ge(weighed, made_before(n, 2))
                for a in range(2):
                    act.wait_ge(turned, made(n, 2) - 1 + a)
                    nc.scalar.activation(pt[:, j % 2, 0, a], t_ps[:, a], ACT.Copy).then_inc(pt_hi, 1)

            def nothing(n, i, j):
                pass

            pipeline(act, exponentials, high_part, nothing, turn_first=True)


def layer0_mlp_phase(nc, n_tok, x, ctx_in, w_proj, b_proj, norm_w, ff1_w, ff1_b, ff2_w, ff2_b, identity, x_out):
    steps = n_tok // TOK
    wide_scale = ROW_SCALE * W_SCALE
    with ExitStack() as ctx:
        m = Mem(nc, ctx, "mlp")
        wp = m.sb("wp", [P, 2, C])
        w1_in = m.sb("w1_in", [P, 2, 2 * C])
        w1 = m.sb("w1", [P, 2, 2, 2 * C], F16)
        w2 = m.sb("w2", [P, 2, C])
        nw = m.sb("nw", [P, C])
        bp = m.sb("bp", [P, C])
        b2 = m.sb("b2", [P, C])
        b1 = m.sb("b1", [P, 4])
        b1_wide = m.sb("b1_wide", [P, 4])
        ident = m.sb("id", [P, P])
        c_sb = m.sb("c", [P, 2, SUB, C])
        x_sb = m.sb("x", [P, 2, SUB, C])
        xb = m.sb("xb", [P, SUB, C])
        x1 = m.sb("x1", [P, 2, SUB, C])
        x1b = m.sb("x1b", [P, 2, SUB, C])
        junk = m.sb("junk", [P, SUB, C])
        ss = m.sb("ss", [P, SUB])
        ms = m.sb("ms", [P, SUB])
        sd = m.sb("sd", [P, SUB])
        rs = m.sb("rs", [P, SUB])
        xn = m.sb("xn", [P, SUB, C])
        ct = m.sb("ct", [P, 2, TOK])
        nt = m.sb("nt", [P, 2, 2, TOK], F16)
        gate = m.sb("gate", [P, 2, TOK])
        ut = m.sb("ut", [P, 2, TOK])
        x2 = m.sb("x2", [P, 2, SUB, C])
        t_ps = m.psum("t_ps", [P, 2, TOK])
        f_ps = m.psum("f_ps", [P, 4, TOK])
        p_ps = m.psum("p_ps", [P, SUB, C])

        const_in = m.sem("const_in")
        rows_in = [m.sem(f"rows_in{p}") for p in range(2)]
        stored = [m.sem(f"stored{p}") for p in range(2)]
        ctx_turned = m.sem("ctx_turned")
        ct_a, ct_b = m.sem("ct_a"), m.sem("ct_b")
        projected = m.sem("projected")
        xb_made = m.sem("xb_made")
        x1_made = m.sem("x1_made")
        x1b_made = m.sem("x1b_made")
        squared, meaned, rooted, inverted = m.sem("squared"), m.sem("meaned"), m.sem("rooted"), m.sem("inverted")
        normed = m.sem("normed")
        rows_turned = m.sem("rows_turned")
        nt_a, nt_b = m.sem("nt_a"), m.sem("nt_b")
        weights_hi, weights_split = m.sem("weights_hi"), m.sem("weights_split")
        widened = m.sem("widened")
        gated = m.sem("gated")
        u_made = m.sem("u_made")
        narrowed = m.sem("narrowed")
        x2_made = m.sem("x2_made")
        ctx.callback(m.clear_semaphores)
        block = ctx.enter_context(nc.Block())

        @block.sync
        def _(sp):
            for s in stored:
                sp.sem_inc(s, 16)

            def load(t, par):
                sp.wait_ge(ctx_turned, made_before(t, 2))
                sp.wait_ge(xb_made, made_before(t, 2))
                sp.dma_start(c_sb[:, par], rows(ctx_in, t * TOK)).then_inc(rows_in[par], 16)
                sp.dma_start(x_sb[:, par], rows(x, t * TOK)).then_inc(rows_in[par], 16)

            def store(t, par):
                sp.wait_ge(x2_made, made(t))
                sp.dma_start(rows(x_out, t * TOK), x2[:, par]).then_inc(stored[par], 16)

            load(0, 0)
            sp.dma_start(wp[:], w_proj.rearrange("(k p) n -> p k n", p=P)).then_inc(const_in, 16)
            sp.dma_start(w1_in[:], ff1_w.rearrange("(k p) n -> p k n", p=P)).then_inc(const_in, 16)
            sp.dma_start(w2[:], ff2_w.rearrange("(k p) n -> p k n", p=P)).then_inc(const_in, 16)
            sp.dma_start(nw[:], spread(norm_w)).then_inc(const_in, 16)
            sp.dma_start(bp[:], spread(b_proj)).then_inc(const_in, 16)
            sp.dma_start(b2[:], spread(ff2_b)).then_inc(const_in, 16)
            sp.dma_start(b1[:], columns(ff1_b), allow_slow_non_contiguous=True).then_inc(const_in, 16)
            sp.dma_start(ident[:], identity).then_inc(const_in, 16)
            load(1, 1)
            load(2, 0)
            with sp.Fori(0, steps // 2 - 2) as i:
                load(2 * i + 3, 1)
                store(2 * i, 0)
                load(2 * i + 4, 0)
                store(2 * i + 1, 1)
            load(steps - 1, 1)
            for t in range(steps - 4, steps):
                store(t, t % 2)
            for s in stored:
                sp.wait_ge(s, 16 * (steps // 2 + 1))

        @block.tensor
        def _(pe):
            for s in (ctx_turned, projected, rows_turned, widened, narrowed):
                pe.sem_inc(s, PRIME)
            pe.wait_ge(const_in, 128)

            def context_transposes(t, i, par):
                pe.wait_ge(rows_in[par], 32 * (i + 1))
                pe.wait_ge(nt_a, made_before(t, 2))
                pe.wait_ge(nt_b, made_before(t, 2))
                for k in range(SUB):
                    for c in range(2):
                        tr = nc.tensor.transpose(t_ps[:, c, k * P:(k + 1) * P], c_sb[:, par, k, c * P:(c + 1) * P],
                                                 ident[:])
                tr.then_inc(ctx_turned, 1)

            def project(t):
                pe.wait_ge(ct_a, made(t))
                pe.wait_ge(ct_b, made(t))
                pe.wait_ge(x1_made, made_before(t, 1))
                for k in range(SUB):
                    for c in range(2):
                        mm = nc.tensor.matmul(p_ps[:, k], ct[:, c, k * P:(k + 1) * P], wp[:, c],
                                              start=(c == 0), stop=(c == 1))
                mm.then_inc(projected, 1)

            def row_transposes(t):
                pe.wait_ge(normed, made(t))
                for k in range(SUB):
                    for c in range(2):
                        tr = nc.tensor.transpose(t_ps[:, c, k * P:(k + 1) * P], xn[:, k, c * P:(c + 1) * P], ident[:])
                tr.then_inc(rows_turned, 1)

            def widen(t):
                pe.wait_ge(nt_a, made(t))
                pe.wait_ge(nt_b, made(t))
                pe.wait_ge(u_made, made_before(t, 1))
                for o in range(4):
                    for a, b in ((0, 0), (0, 1), (1, 0)):
                        for c in range(2):
                            mm = nc.tensor.matmul(f_ps[:, o], w1[:, a, c, o * P:(o + 1) * P], nt[:, b, c],
                                                  start=(a + b + c == 0), stop=(a == 1 and c == 1))
                mm.then_inc(widened, 1)

            def narrow(t):
                pe.wait_ge(u_made, made(t))
                for k in range(SUB):
                    for c in range(2):
                        mm = nc.tensor.matmul(p_ps[:, k], ut[:, c, k * P:(k + 1) * P], w2[:, c],
                                              start=(c == 0), stop=(c == 1))
                mm.then_inc(narrowed, 1)

            def step(t, i, par, left):
                if left > 2:
                    context_transposes(t + 2, i + 1, par)
                widen(t)
                pe.wait_ge(x2_made, made_before(t, 1))
                if left > 2:
                    project(t + 2)
                if left > 1:
                    row_transposes(t + 1)
                if left > 2:
                    pe.wait_ge(x1_made, made(t + 2))
                narrow(t)

            for t in range(2):
                context_transposes(t, 0, t)
                project(t)
            row_transposes(0)
            pe.wait_ge(weights_split, 2)
            in_pairs(pe, steps, step)

        @block.gpsimd
        def _(pool):
            pool.sem_inc(xb_made, PRIME)
            pool.sem_inc(x1b_made, PRIME)
            pool.wait_ge(const_in, 128)

            def step(t, i, par):
                pool.wait_ge(rows_in[par], 32 * (i + 1))
                pool.wait_ge(x1_made, made_before(t, 1))
                nc.gpsimd.tensor_tensor(xb[:], x_sb[:, par], over_rows(bp), ALU.add).then_inc(xb_made, 1)
                pool.wait_ge(x1_made, made(t))
                pool.wait_ge(x2_made, made_before(t, 2))
                nc.gpsimd.tensor_tensor(x1b[:, par], x1[:, par], over_rows(b2), ALU.add).then_inc(x1b_made, 1)

            with pool.Fori(0, steps // 2) as i:
                step(2 * i, i, 0)
                step(2 * i + 1, i, 1)

        @block.scalar
        def _(act):
            for s in (ct_a, squared, rooted, nt_a, gated):
                act.sem_inc(s, PRIME)
            act.wait_ge(const_in, 128)

            def copy_context(t):
                act.wait_ge(ctx_turned, made(t))
                act.wait_ge(projected, made_before(t, 1))
                nc.scalar.activation(ct[:, 0], t_ps[:, 0], ACT.Copy).then_inc(ct_a, 1)

            def norm(t, par):
                act.wait_ge(x1_made, made(t))
                act.wait_ge(meaned, made_before(t, 1))
                for k in range(SUB):
                    sq = nc.scalar.activation(junk[:, k], x1[:, par, k], ACT.Square, accum_out=ss[:, k:k + 1])
                sq.then_inc(squared, 1)
                act.wait_ge(meaned, made(t))
                act.wait_ge(inverted, made_before(t, 1))
                nc.scalar.activation(sd[:], ms[:], ACT.Sqrt).then_inc(rooted, 1)

            def copy_rows(t):
                act.wait_ge(rows_turned, made(t))
                act.wait_ge(widened, made_before(t, 1))
                nc.scalar.activation(nt[:, 0], t_ps[:], ACT.Copy, scale=ROW_SCALE).then_inc(nt_a, 1)

            def step(t, i, par, left):
                if left > 2:
                    copy_context(t + 2)
                act.wait_ge(widened, made(t))
                act.wait_ge(u_made, made_before(t, 1))
                for c in range(2):
                    ge = nc.scalar.activation(gate[:, c], f_ps[:, c], ACT.Gelu, bias=b1[:, c:c + 1],
                                              scale=1.0 / wide_scale)
                ge.then_inc(gated, 1)
                if left > 1:
                    copy_rows(t + 1)
                if left > 2:
                    norm(t + 2, par)

            nc.scalar.activation(w1[:, 0], w1_in[:], ACT.Copy, scale=W_SCALE).then_inc(weights_hi, 1)
            copy_context(0)
            norm(0, 0)
            copy_context(1)
            copy_rows(0)
            norm(1, 1)
            in_pairs(act, steps, step)

        @block.vector
        def _(dve):
            for s in (ct_b, x1_made, meaned, inverted, normed, nt_b, u_made, x2_made):
                dve.sem_inc(s, PRIME)
            dve.wait_ge(const_in, 128)

            def copy_context(t):
                dve.wait_ge(ctx_turned, made(t))
                dve.wait_ge(projected, made_before(t, 1))
                nc.vector.tensor_copy(ct[:, 1], t_ps[:, 1]).then_inc(ct_b, 1)

            def residual(t, par):
                dve.wait_ge(projected, made(t))
                dve.wait_ge(xb_made, made(t))
                dve.wait_ge(x1b_made, made_before(t, 2))
                nc.vector.tensor_tensor(x1[:, par], p_ps[:], xb[:], ALU.add).then_inc(x1_made, 1)

            def norm(t, par):
                dve.wait_ge(squared, made(t))
                nc.vector.tensor_scalar(ms[:], ss[:], 1.0 / C, 1e-6, ALU.mult, ALU.add).then_inc(meaned, 1)
                dve.wait_ge(rooted, made(t))
                nc.vector.reciprocal(rs[:], sd[:]).then_inc(inverted, 1)
                dve.wait_ge(inverted, made(t))
                dve.wait_ge(rows_turned, made_before(t, 1))
                for k in range(SUB):
                    st = nc.vector.scalar_tensor_tensor(out=xn[:, k], in0=x1[:, par, k], scalar=rs[:, k:k + 1],
                                                        in1=nw[:], op0=ALU.mult, op1=ALU.mult)
                st.then_inc(normed, 1)

            def copy_rows(t):
                dve.wait_ge(rows_turned, made(t))
                dve.wait_ge(widened, made_before(t, 1))
                dve.wait_ge(nt_a, made(t))
                nc.vector.scalar_tensor_tensor(out=nt[:, 1], in0=t_ps[:], scalar=ROW_SCALE, in1=nt[:, 0],
                                               op0=ALU.mult, op1=ALU.subtract).then_inc(nt_b, 1)

            def step(t, i, par, left):
                if left > 2:
                    copy_context(t + 2)
                dve.wait_ge(gated, made(t))
                dve.wait_ge(narrowed, made_before(t, 1))
                for c in range(2):
                    st = nc.vector.scalar_tensor_tensor(out=ut[:, c], in0=f_ps[:, 2 + c], scalar=b1_wide[:, 2 + c:3 + c],
                                                        in1=gate[:, c], op0=ALU.add, op1=ALU.mult)
                st.then_inc(u_made, 1)
                if left > 2:
                    residual(t + 2, par)
                if left > 1:
                    copy_rows(t + 1)
                if left > 2:
                    norm(t + 2, par)
                dve.wait_ge(narrowed, made(t))
                dve.wait_ge(x1b_made, made(t))
                dve.wait_ge(stored[par], 16 * (i + 1))
                nc.vector.scalar_tensor_tensor(out=x2[:, par], in0=p_ps[:], scalar=1.0 / wide_scale, in1=x1b[:, par],
                                               op0=ALU.mult, op1=ALU.add).then_inc(x2_made, 1)

            copy_context(0)
            residual(0, 0)
            norm(0, 0)
            copy_context(1)
            residual(1, 1)
            dve.wait_ge(weights_hi, 1)
            nc.vector.scalar_tensor_tensor(out=w1[:, 1], in0=w1_in[:], scalar=W_SCALE, in1=w1[:, 0],
                                           op0=ALU.mult, op1=ALU.subtract).then_inc(weights_split, 1)
            nc.vector.tensor_scalar(b1_wide[:], b1[:], wide_scale, None, ALU.mult).then_inc(weights_split, 1)
            copy_rows(0)
            norm(1, 1)
            dve.wait_ge(weights_split, 2)
            in_pairs(dve, steps, step)


def tables_phase(nc, batches, seq, x, gamma, beta, wq, bq, wk, bk, wv, bv, wpos_t, u_bias, v_bias, turn_tab,
                 identity, q_tab, q_past, k_tab, v_tab, pe_sb, pe_tab, pe_in):
    per_b = seq // TOK
    steps = batches * per_b
    with ExitStack() as ctx:
        m = Mem(nc, ctx, "tab")
        wq_sb = m.sb("wq", [P, 2, NH, 2, HD])
        wk_sb = m.sb("wk", [P, 2, NH, 2, HD])
        wv_sb = m.sb("wv", [P, 2, C])
        wp_sb = m.sb("wp", [HD, NH, 2, P])
        turn = m.sb("turn", [P, 2, 2, TOK])
        ga = m.sb("ga", [P, C])
        be = m.sb("be", [P, C])
        bvb = m.sb("bvb", [P, C])
        bvs = m.sb("bvs", [P, C])
        bq_sb = m.sb("bq", [P, NH])
        bk_sb = m.sb("bk", [P, NH])
        ub = m.sb("ub", [P, NH])
        vb = m.sb("vb", [P, NH])
        bqu = m.sb("bqu", [P, NH])
        bqus = m.sb("bqus", [P, NH])
        bqv = m.sb("bqv", [P, NH])
        bks = m.sb("bks", [P, NH])
        ident = m.sb("id", [P, P])
        x_sb = m.sb("x", [P, 2, SUB, C])
        spare = m.sb("spare", [P, 1])
        st1, st2 = m.sb("st1", [P, SUB, 6]), m.sb("st2", [P, SUB, 6])
        mv1, mv2 = m.sb("mv1", [P, SUB, 2]), m.sb("mv2", [P, SUB, 2])
        ve1, ve2 = m.sb("ve1", [P, SUB]), m.sb("ve2", [P, SUB])
        sd1, sd2 = m.sb("sd1", [P, SUB]), m.sb("sd2", [P, SUB])
        rs1, rs2 = m.sb("rs1", [P, SUB]), m.sb("rs2", [P, SUB])
        xn = m.sb("xn", [P, SUB, C])
        xm = m.sb("xm", [P, SUB, C])
        xg = m.sb("xg", [P, SUB, C])
        xa = m.sb("xa", [P, SUB, C])
        ht = m.sb("ht", [P, 2, TOK])
        qs = m.sb("qs", [P, 2, TOK])
        ks = m.sb("ks", [P, 2, TOK])
        qv = m.sb("qv", [HD, 2, TOK])
        prod = m.sb("prod", [P, 2, 4, TOK])
        bs = m.sb("bs", [P, 2, 2, TOK])
        past = m.sb("past", [P, NH, 2])
        qt_o = m.sb("qt_o", [P, NH, 5, TOK], F16)
        kt_o = m.sb("kt_o", [P, NH, 2, TOK], F16)
        vs = m.sb("vs", [P, SUB, C])
        vt_o = m.sb("vt_o", [P, NH, SUB, 2, HD], F16)
        past_o = m.sb("past_o", [P, NH, 2, 2], F16)
        t_ps = m.psum("t_ps", [P, 2, TOK])
        q_ps = m.psum("q_ps", [P, TOK])
        k_ps = m.psum("k_ps", [P, TOK])
        a_ps = m.psum("a_ps", [P, 2, TOK])
        v_ps = m.psum("v_ps", [P, SUB, C])

        const_in, affine_in = m.sem("const_in"), m.sem("affine_in")
        bias_made = m.sem("bias_made")
        x_in = [m.sem(f"x_in{p}") for p in range(2)]
        qk_stored = [m.sem(f"qk_stored{h}") for h in range(NH)]
        turn_in = [m.sem(f"turn_in{p}") for p in range(2)]
        v_stored, past_stored = m.sem("v_stored"), m.sem("past_stored")
        stats1, mean1, eps1, root1, inv1, norm1 = (m.sem(n) for n in (
            "stats1", "mean1", "eps1", "root1", "inv1", "norm1"))
        stats2, mean2, eps2, root2, inv2, norm2 = (m.sem(n) for n in (
            "stats2", "mean2", "eps2", "root2", "inv2", "norm2"))
        gained, shifted = m.sem("gained"), m.sem("shifted")
        rows_turned, ht_made = m.sem("rows_turned"), m.sem("ht_made")
        queried, keyed, rotated, valued = m.sem("queried"), m.sem("keyed"), m.sem("rotated"), m.sem("valued")
        qs_made, qv_made, ks_made = m.sem("qs_made"), m.sem("qv_made"), m.sem("ks_made")
        products, bs_made = m.sem("products"), m.sem("bs_made")
        b_hi, v_hi = m.sem("b_hi"), m.sem("v_hi")
        b_lo, c_lo, k_lo, v_lo = m.sem("b_lo"), m.sem("c_lo"), m.sem("k_lo"), m.sem("v_lo")
        v_scaled, past_made, past_hi, past_lo = (m.sem(n) for n in ("v_scaled", "past_made", "past_hi", "past_lo"))
        ctx.callback(m.clear_semaphores)
        block = ctx.enter_context(nc.Block())
        N_CONST = 18 * 16

        @block.sync
        def _(sp):
            for s in qk_stored:
                sp.sem_inc(s, 48)
            sp.sem_inc(v_stored, 64)
            sp.sem_inc(past_stored, 16)

            def load(t, par):
                sp.wait_ge(norm1, made_before(t, 2))
                sp.dma_start(x_sb[:, par], rows(x, t * TOK)).then_inc(x_in[par], 16)

            def load_turn(t, par):
                sp.dma_start(turn[:, par], turn_tab[:, :, ds((t % per_b) * TOK, TOK)]).then_inc(turn_in[par], 16)

            def store_values(t):
                b, k = t // per_b, t % per_b
                sp.wait_ge(v_lo, made(t))
                for h in range(NH):
                    sp.dma_start(v_tab[ds(b * NH + h, 1)].rearrange("o p t d -> p (o t) d")[:, ds(k * SUB, SUB), :],
                                 vt_o[:, h].rearrange("p k a d -> p k (a d)")).then_inc(v_stored, 16)
                sp.wait_ge(past_lo, made(t))
                sp.dma_start(q_past[ds(b * NH, NH)].rearrange("h p n o -> p h (n o)"),
                             past_o[:].rearrange("p h a n -> p h (a n)")).then_inc(past_stored, 16)

            def store(t, par, first=False, last=False):
                b, k = t // per_b, t % per_b
                for h in range(NH):
                    n = NH * t + h
                    q_dst = q_tab[ds(b * NH + h, 1)].rearrange("o p n c -> p (o n) c")
                    sp.wait_ge(b_lo, made(n))
                    sp.wait_ge(c_lo, made(n))
                    sp.dma_start(q_dst[:, :, ds(k * TOK + 1, TOK)], qt_o[:, h]).then_inc(qk_stored[h], 16)
                    sp.dma_start(q_dst[:, :, 0:1], qt_o[:, h, :, TOK - 1:TOK], allow_slow_non_contiguous=True
                                 ).then_inc(qk_stored[h], 16)
                    sp.wait_ge(k_lo, made(n))
                    sp.dma_start(k_tab[ds(b * NH + h, 1)].rearrange("o p a s -> p (o a) s")[:, :, ds(k * TOK, TOK)],
                                 kt_o[:, h]).then_inc(qk_stored[h], 16)
                    if h == 0 and not first:
                        store_values(t - 1)
                if not last:
                    load_turn(t + 2, par)

            load(0, 0)
            sp.dma_start(ga[:], spread(gamma)).then_inc(affine_in, 16)
            sp.dma_start(be[:], spread(beta)).then_inc(affine_in, 16)
            sp.dma_start(ident[:], identity).then_inc(affine_in, 16)
            for dst, w in ((wq_sb, wq), (wk_sb, wk)):
                for a in range(2):
                    for c in range(2):
                        sp.dma_start(dst[:, c, :, a, :], w[c * P:(c + 1) * P, :].rearrange("p (h d) -> p h d", h=NH)
                                     ).then_inc(const_in, 16)
            sp.dma_start(wv_sb[:], wv.rearrange("(k p) n -> p k n", p=P)).then_inc(const_in, 16)
            sp.dma_start(wp_sb[:], wpos_t).then_inc(const_in, 16)
            sp.dma_start(bvb[:], spread(bv)).then_inc(const_in, 16)
            for dst, vec in ((bq_sb, bq.rearrange("(h d) -> d h", h=NH)), (bk_sb, bk.rearrange("(h d) -> d h", h=NH)),
                             (ub, u_bias.rearrange("h d -> d h")), (vb, v_bias.rearrange("h d -> d h"))):
                for a in range(2 if dst is not vb else 1):
                    sp.dma_start(dst[a * HD:(a + 1) * HD, :], vec, allow_slow_non_contiguous=True
                                 ).then_inc(const_in, 16)
            load(1, 1)
            load_turn(0, 0)
            load_turn(1, 1)
            load(2, 0)
            load(3, 1)
            store(0, 0, first=True)
            load(4, 0)
            store(1, 1)
            with sp.Fori(1, steps // 2 - 2) as i:
                load(2 * i + 3, 1)
                store(2 * i, 0)
                load(2 * i + 4, 0)
                store(2 * i + 1, 1)
            load(steps - 1, 1)
            for t in range(steps - 4, steps):
                store(t, t % 2, last=t >= steps - 2)
            store_values(steps - 1)
            for s in qk_stored:
                sp.wait_ge(s, 48 * (steps + 1))
            sp.wait_ge(v_stored, 64 * (steps + 1))
            sp.wait_ge(past_stored, 16 * (steps + 1))

        def over_steps(eng, step):
            step(0, 0, 0, 3)
            step(1, 0, 1, 3)
            with eng.Fori(1, steps // 2 - 1) as i:
                step(2 * i, i, 0, 3)
                step(2 * i + 1, i, 1, 3)
            step(steps - 2, steps // 2 - 1, 0, 2)
            step(steps - 1, steps // 2 - 1, 1, 1)

        @block.tensor
        def _(pe):
            for s in (rows_turned, queried, keyed, rotated, valued):
                pe.sem_inc(s, PRIME)
            pe.wait_ge(affine_in, 48)

            def query(n, h):
                pe.wait_ge(qv_made, made_before(n, 1))
                for c in range(2):
                    mm = nc.tensor.matmul(q_ps[:], wq_sb[:, c, h].rearrange("p a d -> p (a d)"), ht[:, c],
                                          start=(c == 0), stop=(c == 1))
                mm.then_inc(queried, 1)

            def key(n, h):
                pe.wait_ge(ks_made, made_before(n, 1))
                for c in range(2):
                    mm = nc.tensor.matmul(k_ps[:], wk_sb[:, c, h].rearrange("p a d -> p (a d)"), ht[:, c],
                                          start=(c == 0), stop=(c == 1))
                mm.then_inc(keyed, 1)

            def position(n, h):
                pe.wait_ge(qv_made, made(n))
                pe.wait_ge(products, made_before(n, 1))
                for a in range(2):
                    mm = nc.tensor.matmul(a_ps[:, a], wp_sb[:, h, a], qv[:, h % 2], start=True, stop=True)
                mm.then_inc(rotated, 1)

            def transposes(t):
                pe.wait_ge(shifted, made(t))
                for k in range(SUB):
                    for c in range(2):
                        tr = nc.tensor.transpose(t_ps[:, c, k * P:(k + 1) * P], xa[:, k, c * P:(c + 1) * P], ident[:])
                tr.then_inc(rows_turned, 1)

            def step(t, i, par, left):
                pe.wait_ge(ht_made, made(t))
                query(NH * t, 0)
                key(NH * t, 0)
                pe.wait_ge(v_scaled, made_before(t, 1))
                for h in range(NH):
                    n = NH * t + h
                    for c in range(2):
                        mm = nc.tensor.matmul(v_ps[:, h], ht[:, c, h * P:(h + 1) * P], wv_sb[:, c],
                                              start=(c == 0), stop=(c == 1))
                    if h < NH - 1:
                        query(n + 1, h + 1)
                        key(n + 1, h + 1)
                    else:
                        mm.then_inc(valued, 1)
                        if left > 1:
                            transposes(t + 1)
                    position(n, h)

            transposes(0)
            pe.wait_ge(const_in, N_CONST)
            over_steps(pe, step)

        @block.scalar
        def _(act):
            for s in (root1, root2, ht_made, qs_made, qv_made, ks_made, b_hi, v_hi):
                act.sem_inc(s, PRIME)

            def roots(t, which):
                eps, inv, root, ve, sd = ((eps1, inv1, root1, ve1, sd1), (eps2, inv2, root2, ve2, sd2))[which]
                act.wait_ge(eps, made(t))
                act.wait_ge(inv, made_before(t, 1))
                nc.scalar.activation(sd[:], ve[:], ACT.Sqrt).then_inc(root, 1)

            def head(t, n, h):
                hp = h % 2
                act.wait_ge(queried, made(n))
                act.wait_ge(c_lo, made_before(n, 2))
                nc.scalar.activation(qs[:, hp], q_ps[:], ACT.Identity, bias=bqus[:, h:h + 1], scale=Q_SCALE)
                act.wait_ge(qk_stored[h], 48 * (t + 1))
                nc.scalar.activation(qt_o[:, h, 4], q_ps[:], ACT.Identity, bias=bqus[:, h:h + 1], scale=Q_SCALE
                                     ).then_inc(qs_made, 1)
                act.wait_ge(rotated, made_before(n, 2))
                nc.scalar.activation(qv[:, hp], q_ps[0:HD], ACT.Identity, bias=bqv[0:HD, h:h + 1]
                                     ).then_inc(qv_made, 1)
                act.wait_ge(keyed, made(n))
                act.wait_ge(k_lo, made_before(n, 2))
                nc.scalar.activation(ks[:, hp], k_ps[:], ACT.Identity, bias=bks[:, h:h + 1], scale=Q_SCALE)
                nc.scalar.activation(kt_o[:, h, 0], k_ps[:], ACT.Identity, bias=bks[:, h:h + 1], scale=Q_SCALE
                                     ).then_inc(ks_made, 1)

            def turned_high(n, h):
                act.wait_ge(bs_made, made(n))
                nc.scalar.activation(qt_o[:, h, 0:4:2], bs[:, h % 2], ACT.Copy).then_inc(b_hi, 1)

            def values_high(t):
                act.wait_ge(v_scaled, made(t))
                act.wait_ge(v_stored, 64 * (t + 1))
                nc.scalar.activation(vt_o[:, :, :, 0, :], vs[:].rearrange("p k (h d) -> p h k d", h=NH), ACT.Copy
                                     ).then_inc(v_hi, 1)

            def copy_rows(t):
                act.wait_ge(rows_turned, made(t))
                act.wait_ge(valued, made_before(t, 1))
                nc.scalar.activation(ht[:], t_ps[:], ACT.Copy).then_inc(ht_made, 1)

            def step(t, i, par, left):
                first = isinstance(t, int) and t == 0
                for h in range(NH):
                    head(t, NH * t + h, h)
                    if h == 0 and left > 1:
                        roots(t + 1, 1)
                    if h == 3 and left > 2:
                        roots(t + 2, 0)
                    if not (first and h < 2):
                        turned_high(NH * t + h - 2, (h - 2) % NH)
                    if h == 1 and not first:
                        values_high(t - 1)
                if left > 1:
                    copy_rows(t + 1)
                if isinstance(t, int) and t == 1:
                    for k in range(4):
                        cols = slice(k * seq // 2, (k + 1) * seq // 2)
                        act.dma_start(pe_sb[:, :, :, cols], pe_tab[:, :, :, cols]).then_inc(pe_in, 16)

            roots(0, 0)
            roots(0, 1)
            copy_rows(0)
            roots(1, 0)
            act.wait_ge(bias_made, 4)
            over_steps(act, step)
            turned_high(NH * steps - 2, 2)
            turned_high(NH * steps - 1, 3)
            values_high(steps - 1)

        @block.vector
        def _(dve):
            for s in (stats1, mean1, eps1, inv1, norm1, stats2, mean2, eps2, inv2, norm2, products, c_lo, k_lo,
                      v_scaled, past_made, past_hi, past_lo):
                dve.sem_inc(s, PRIME)
            def moments(t, src, st, mv, ve, stats, mean, eps):
                for k in range(SUB):
                    op = nc.vector.bn_stats(st[:, k], src[:, k])
                op.then_inc(stats, 1)
                dve.wait_ge(stats, made(t))
                nc.vector.tensor_copy(spare[:], st[:, 0, 0:1])
                for k in range(SUB):
                    op = nc.vector.bn_aggr(mv[:, k], st[:, k])
                op.then_inc(mean, 1)
                dve.wait_ge(mean, made(t))
                nc.vector.tensor_scalar(ve[:], mv[:, :, 1], 1e-5, None, ALU.add).then_inc(eps, 1)

            def centre(t, dst, src, mv, sd, rs, root, inv, norm):
                dve.wait_ge(root, made(t))
                nc.vector.reciprocal(rs[:], sd[:]).then_inc(inv, 1)
                dve.wait_ge(inv, made(t))
                for k in range(SUB):
                    op = nc.vector.tensor_scalar(dst[:, k], src[:, k], mv[:, k, 0:1], rs[:, k:k + 1],
                                                 ALU.subtract, ALU.mult)
                op.then_inc(norm, 1)

            def norm_a(t, i, par):
                dve.wait_ge(x_in[par], 16 * (i + 1))
                moments(t, x_sb[:, par], st1, mv1, ve1, stats1, mean1, eps1)

            def norm_b(t, par):
                centre(t, xn, x_sb[:, par], mv1, sd1, rs1, root1, inv1, norm1)

            def norm_c(t):
                dve.wait_ge(norm1, made(t))
                moments(t, xn, st2, mv2, ve2, stats2, mean2, eps2)

            def norm_d(t):
                dve.wait_ge(gained, made_before(t, 1))
                centre(t, xm, xn, mv2, sd2, rs2, root2, inv2, norm2)

            def head(t, n, h, i, par):
                hp = h % 2
                cos, sin = turn[:, par, 0], turn[:, par, 1]
                dve.wait_ge(qs_made, made(n))
                nc.vector.tensor_tensor(qt_o[HD:P, h, 4], qs[HD:P, hp], qt_o[HD:P, h, 4], ALU.subtract
                                        ).then_inc(c_lo, 1)
                dve.wait_ge(ks_made, made(n))
                nc.vector.tensor_tensor(kt_o[:, h, 1], ks[:, hp], kt_o[:, h, 0], ALU.subtract).then_inc(k_lo, 1)
                dve.wait_ge(rotated, made(n))
                dve.wait_ge(turn_in[par], 16 * (i + 1))
                dve.wait_ge(past_lo, made_before(t, 1))
                nc.vector.tensor_scalar(past[:, h], a_ps[:, :, TOK - 1], B_SCALE, None, ALU.mult
                                        ).then_inc(past_made, 1)
                dve.wait_ge(bs_made, made_before(n, 2))
                nc.vector.tensor_tensor(prod[:, hp, 0], a_ps[:, 0], cos, ALU.mult)
                nc.vector.tensor_tensor(prod[:, hp, 1], a_ps[:, 1], sin, ALU.mult)
                nc.vector.tensor_tensor(prod[:, hp, 2], a_ps[:, 1], cos, ALU.mult)
                nc.vector.tensor_tensor(prod[:, hp, 3], a_ps[:, 0], sin, ALU.mult).then_inc(products, 1)

            def step(t, i, par, left):
                for h in range(NH):
                    head(t, NH * t + h, h, i, par)
                    if left > 2 and h == 1:
                        norm_a(t + 2, i + 1, par)
                    if left > 2 and h == 2:
                        norm_b(t + 2, par)
                    if h == 3:
                        values(t)
                    if left > 2 and h == 3:
                        norm_c(t + 2)
                    if left > 1 and h == 0:
                        norm_d(t + 1)

            def values(t):
                dve.wait_ge(valued, made(t))
                dve.wait_ge(v_lo, made_before(t, 1))
                nc.vector.scalar_tensor_tensor(out=vs[:], in0=v_ps[:], scalar=V_SCALE, in1=over_rows(bvs),
                                               op0=ALU.mult, op1=ALU.add).then_inc(v_scaled, 1)
                dve.wait_ge(past_made, NH * (t + 1) + PRIME)
                dve.wait_ge(past_stored, 16 * (t + 1))
                nc.vector.tensor_copy(past_o[:, :, :, 0], past[:]).then_inc(past_hi, 1)
                dve.wait_ge(past_hi, made(t))
                nc.vector.tensor_tensor(past_o[:, :, :, 1], past[:], past_o[:, :, :, 0], ALU.subtract
                                        ).then_inc(past_lo, 1)

            for t in range(2):
                norm_a(t, 0, t)
                norm_b(t, t)
                norm_c(t)
                if t == 0:
                    norm_d(t)
            dve.wait_ge(const_in, N_CONST)
            nc.vector.tensor_tensor(bqu[:], bq_sb[:], ub[:], ALU.add).then_inc(bias_made, 1)
            nc.vector.tensor_tensor(bqv[0:HD], bq_sb[0:HD], vb[0:HD], ALU.add)
            nc.vector.tensor_scalar(bvs[:], bvb[:], V_SCALE, None, ALU.mult).then_inc(bias_made, 1)
            nc.vector.tensor_scalar(bks[:], bk_sb[:], Q_SCALE, None, ALU.mult).then_inc(bias_made, 1)
            dve.wait_ge(bias_made, 3)
            nc.vector.tensor_scalar(bqus[:], bqu[:], Q_SCALE, None, ALU.mult).then_inc(bias_made, 1)
            over_steps(dve, step)

        @block.gpsimd
        def _(pool):
            for s in (gained, shifted, bs_made, b_lo, v_lo):
                pool.sem_inc(s, PRIME)
            pool.wait_ge(affine_in, 48)

            def affine(t):
                pool.wait_ge(norm2, made(t))
                nc.gpsimd.tensor_tensor(xg[:], xm[:], over_rows(ga), ALU.mult).then_inc(gained, 1)
                pool.wait_ge(gained, made(t))
                pool.wait_ge(rows_turned, made_before(t, 1))
                nc.gpsimd.tensor_tensor(xa[:], xg[:], over_rows(be), ALU.add).then_inc(shifted, 1)

            def sums(n, hp):
                pool.wait_ge(products, made(n))
                pool.wait_ge(b_hi, made_before(n, 2))
                pool.wait_ge(b_lo, made_before(n, 2))
                nc.gpsimd.tensor_tensor(bs[:, hp, 0], prod[:, hp, 0], prod[:, hp, 1], ALU.add)
                nc.gpsimd.tensor_tensor(bs[:, hp, 1], prod[:, hp, 2], prod[:, hp, 3], ALU.subtract
                                        ).then_inc(bs_made, 1)

            def turned_low(n, h):
                pool.wait_ge(b_hi, made(n))
                nc.gpsimd.tensor_tensor(qt_o[:, h, 1:4:2], bs[:, h % 2], qt_o[:, h, 0:4:2], ALU.subtract
                                        ).then_inc(b_lo, 1)

            def values_low(t):
                pool.wait_ge(v_hi, made(t))
                nc.gpsimd.tensor_tensor(vt_o[:, :, :, 1, :], vs[:].rearrange("p k (h d) -> p h k d", h=NH),
                                        vt_o[:, :, :, 0, :], ALU.subtract).then_inc(v_lo, 1)

            def step(t, i, par, left):
                first = isinstance(t, int) and t == 0
                for h in range(NH):
                    if not (first and h < 2):
                        turned_low(NH * t + h - 2, (h - 2) % NH)
                    if h == 1 and left > 1:
                        affine(t + 1)
                    sums(NH * t + h, h % 2)
                    if h == 2 and not first:
                        values_low(t - 1)

            affine(0)
            over_steps(pool, step)
            turned_low(NH * steps - 2, 2)
            turned_low(NH * steps - 1, 3)
            values_low(steps - 1)


def ffn_phase(nc, batches, seq, x, ctx_in, w_out, b_out, wr, br, ff1_w, ff1_b, ff2_w, ff2_b, identity, prefix, out):
    per_b = seq // TOK
    steps = batches * per_b
    tiles = batches * seq // P
    bt = seq // P
    keep = seq // 2 - 1
    F = ff1_w.shape[1]
    MF = F // P
    DIGITS = 8
    CH = MF // 2
    with ExitStack() as ctx:
        m = Mem(nc, ctx, "ffn")
        z0 = m.sb("z0", [P, tiles * C])
        z1 = m.sb("z1", [P, tiles * C])
        wo = m.sb("wo", [P, 2, C])
        w1 = m.sb("w1", [P, 2, 2, F], F16)
        w2 = m.sb("w2", [P, 2, MF, C], F16)
        w1_in = z1[:, 0:2 * F].rearrange("p (k n) -> p k n", k=2)
        w2_in = z1[:, 2 * F:2 * F + MF * C].rearrange("p (k n) -> p k n", k=MF)
        bo = m.sb("bo", [P, C])
        b1 = m.sb("b1", [P, MF])
        b2 = m.sb("b2", [P, C])
        wrb = m.sb("wrb", [P, C])
        brb = m.sb("brb", [P, 1])
        ident = m.sb("id", [P, P])
        pre = m.sb("pre", [P, 2 * P])
        c_sb = m.sb("c", [P, SUB, C])
        x_sb = m.sb("x", [P, SUB, C])
        xb = m.sb("xb", [P, SUB, C])
        t1 = m.sb("t1", [P, SUB, C])
        xf = m.sb("xf", [P, SUB, C])
        junk = m.sb("junk", [P, SUB, C])
        st = m.sb("st", [P, SUB, 6])
        mv = m.sb("mv", [P, SUB, 2])
        ve, sd, rs = m.sb("ve", [P, SUB]), m.sb("sd", [P, SUB]), m.sb("rs", [P, SUB])
        w_row = m.sb("w_row", [P, SUB])
        spare = m.sb("spare", [P, 1])
        w_all = m.sb("w_all", [P, tiles])
        ct = m.sb("ct", [P, 2, TOK])
        nt = m.sb("nt", [P, 2, 2, TOK], F16)
        g_sb = m.sb("g_sb", [P, 2, 2, TOK])
        gt = m.sb("gt", [P, 2, MF, TOK], F16)
        t_ps = m.psum("t_ps", [P, 2, TOK])
        f_ps = m.psum("f_ps", [P, 4, TOK])
        p_ps = m.psum("p_ps", [P, SUB, C])

        const_in, rows_in, wrapped = m.sem("const_in"), m.sem("rows_in"), m.sem("wrapped")
        ctx_turned, ct_a, ct_b, projected = m.sem("ctx_turned"), m.sem("ct_a"), m.sem("ct_b"), m.sem("projected")
        xb_made, t1_made, stats, mean = m.sem("xb_made"), m.sem("t1_made"), m.sem("stats"), m.sem("mean")
        eps, root, inv, normed = m.sem("eps"), m.sem("root"), m.sem("inv"), m.sem("normed")
        z0_made, routed, weighted = m.sem("z0_made"), m.sem("routed"), m.sem("weighted")
        rows_turned, nt_a, nt_b = m.sem("rows_turned"), m.sem("nt_a"), m.sem("nt_b")
        weights_in, weights_hi, weights_split = m.sem("weights_in"), m.sem("weights_hi"), m.sem("weights_split")
        gate_hi, gate_lo = m.sem("gate_hi"), m.sem("gate_lo")
        widened, gated, narrowed, z1_made = m.sem("widened"), m.sem("gated"), m.sem("narrowed"), m.sem("z1_made")
        step_done, counted, chosen, stored = m.sem("sel_step"), m.sem("counted"), m.sem("chosen"), m.sem("stored")
        out_made = m.sem("out_made")

        def choice_tile(k):
            flat = c_sb[:].rearrange("p k c -> p (k c)")[:, k * tiles:(k + 1) * tiles]
            return flat.rearrange("p (b t) -> p b t", b=batches)

        ke, fl, hb, lb = (choice_tile(k).bitcast(U32) for k in range(4))
        hi, lo, cmp_, over, tie, low_key = (choice_tile(k) for k in range(4, 10))
        passes = (cmp_, choice_tile(14), choice_tile(15))
        pad = bt
        scan = c_sb[:].rearrange("p k c -> p (k c)")[:, 10 * tiles:14 * tiles].rearrange(
            "p (a b t) -> p a b t", a=2, b=batches)
        cur = m.sb("cur", [P, 2, batches])
        cand = m.sb("cand", [P, 3, batches])
        digit = m.sb("digit", [P, 3, batches])
        steps_up = m.sb("steps_up", [P, batches])
        unit = m.sb("unit", [P, 2])
        cnt = m.sb("cnt", [P, 3, batches])
        inc = m.sb("inc", [P, 3, batches])
        want = m.sb("want", [P, 3, batches])
        fac = m.sb("fac", [P, tiles])
        ctx.callback(m.clear_semaphores)
        block = ctx.enter_context(nc.Block())
        N_CONST = 8 * 16

        @block.sync
        def _(sp):
            def load(t):
                sp.wait_ge(ctx_turned, made_before(t, 1))
                sp.wait_ge(xb_made, made_before(t, 1))
                first = (t // per_b) * (seq + 1) + (t % per_b) * TOK + 1
                sp.dma_start(c_sb[:], rows(ctx_in.rearrange("b r c -> (b r) c"), first)).then_inc(rows_in, 16)
                sp.dma_start(x_sb[:], rows(x, t * TOK)).then_inc(rows_in, 16)

            load(0)
            for dst, src in ((wo[:], w_out.rearrange("(k p) n -> p k n", p=P)),
                             (bo[:], spread(b_out)),
                             (b2[:], spread(ff2_b)), (wrb[:], spread(wr)), (brb[:], spread(br)),
                             (ident[:], identity), (pre[:], prefix)):
                sp.dma_start(dst, src).then_inc(const_in, 16)
            sp.dma_start(b1[:], columns(ff1_b), allow_slow_non_contiguous=True).then_inc(const_in, 16)
            for dst, src in ((w1_in, ff1_w), (w2_in, ff2_w)):
                sp.dma_start(dst, src.rearrange("(k p) n -> p k n", p=P)).then_inc(weights_in, 16)
            sp.dma_start(ctx_in[:, seq, :], ctx_in[:, 0, :]).then_inc(wrapped, 16)
            sp.wait_ge(wrapped, 16)
            with sp.Fori(1, steps) as t:
                load(t)
            with sp.Fori(0, steps) as t:
                sp.wait_ge(out_made, t + 1)
                sp.dma_start(rows(out, t * TOK), z0[:, ds(t * (SUB * C), SUB * C)].rearrange(
                    "p (k c) -> p k c", k=SUB)).then_inc(stored, 16)
            sp.wait_ge(stored, 16 * steps)

        @block.tensor
        def _(pe):
            for s in (ctx_turned, projected, rows_turned, narrowed):
                pe.sem_inc(s, PRIME)
            pe.sem_inc(widened, 2 * CH)
            pe.wait_ge(const_in, N_CONST)

            def context_transposes(t):
                pe.wait_ge(rows_in, 32 * (t + 1))
                pe.wait_ge(nt_a, made_before(t, 2))
                pe.wait_ge(nt_b, made_before(t, 2))
                for k in range(SUB):
                    for c in range(2):
                        tr = nc.tensor.transpose(t_ps[:, c, k * P:(k + 1) * P], c_sb[:, k, c * P:(c + 1) * P], ident[:])
                tr.then_inc(ctx_turned, 1)

            def project(t):
                pe.wait_ge(ct_a, made(t))
                pe.wait_ge(ct_b, made(t))
                pe.wait_ge(t1_made, made_before(t, 1))
                for k in range(SUB):
                    for c in range(2):
                        mm = nc.tensor.matmul(p_ps[:, k], ct[:, c, k * P:(k + 1) * P], wo[:, c],
                                              start=(c == 0), stop=(c == 1))
                mm.then_inc(projected, 1)

            def row_transposes(t):
                pe.wait_ge(normed, made(t))
                for k in range(SUB):
                    for c in range(2):
                        tr = nc.tensor.transpose(t_ps[:, c, k * P:(k + 1) * P], xf[:, k, c * P:(c + 1) * P], ident[:])
                tr.then_inc(rows_turned, 1)

            def widen(t):
                pe.wait_ge(nt_a, made(t))
                pe.wait_ge(nt_b, made(t))
                for q in range(CH):
                    pe.wait_ge(gated, CH * t + q - 1 + 2 * CH)
                    for o in range(2):
                        cols = slice((2 * q + o) * P, (2 * q + o + 1) * P)
                        for a, b in ((0, 0), (0, 1), (1, 0)):
                            for c in range(2):
                                mm = nc.tensor.matmul(f_ps[:, 2 * (q % 2) + o], w1[:, a, c, cols], nt[:, b, c],
                                                      start=(a + b + c == 0), stop=(a == 1 and c == 1))
                    mm.then_inc(widened, 1)

            def narrow(t):
                pe.wait_ge(gate_lo, CH * (t + 1) + 2 * CH)
                for k in range(SUB):
                    for c in range(MF):
                        for a, b in ((0, 0), (0, 1), (1, 0)):
                            mm = nc.tensor.matmul(p_ps[:, k], gt[:, a, c, k * P:(k + 1) * P], w2[:, b, c],
                                                  start=(a + b + c == 0), stop=(a == 1 and c == MF - 1))
                mm.then_inc(narrowed, 1)

            def step(t, left=3):
                if left > 2:
                    context_transposes(t + 2)
                widen(t)
                pe.wait_ge(z1_made, made_before(t, 1))
                if left > 2:
                    project(t + 2)
                if left > 1:
                    row_transposes(t + 1)
                if left > 2:
                    pe.wait_ge(t1_made, made(t + 2))
                narrow(t)

            for t in range(2):
                context_transposes(t)
                project(t)
            row_transposes(0)
            pe.wait_ge(weights_split, 1)
            with pe.Fori(0, steps - 2) as t:
                step(t)
            step(steps - 2, 2)
            step(steps - 1, 1)

            ones = pre[:, P:2 * P]
            counts = cnt[:].rearrange("p j b -> p (j b)")
            with pe.Fori(0, 2 * DIGITS + 1) as n:
                pe.wait_ge(counted, n + 1)
                nc.tensor.matmul(t_ps[:, 0, 0:3 * batches], ones, counts, start=True, stop=True).then_inc(chosen, 1)
            pe.wait_ge(counted, 2 * DIGITS + 2)
            nc.tensor.matmul(t_ps[:, 0, 0:3 * batches], ones, counts, start=True, stop=True).then_inc(chosen, 1)
            tie_rows = tie[:].rearrange("p b t -> p (b t)")
            nc.tensor.matmul(t_ps[:, 1, 0:tiles], pre[:, 0:P], tie_rows, start=True, stop=True)
            nc.tensor.matmul(p_ps[:, 0, 0:tiles], ones, tie_rows, start=True, stop=True).then_inc(chosen, 1)

        @block.gpsimd
        def _(pool):
            for s in (xb_made, z0_made):
                pool.sem_inc(s, PRIME)
            pool.wait_ge(const_in, N_CONST)
            with pool.Fori(0, steps) as t:
                pool.wait_ge(rows_in, 32 * (t + 1))
                pool.wait_ge(t1_made, made_before(t, 1))
                nc.gpsimd.tensor_tensor(xb[:], x_sb[:], over_rows(bo), ALU.add).then_inc(xb_made, 1)
                pool.wait_ge(normed, made(t))
                nc.gpsimd.tensor_tensor(z0[:, ds(t * (SUB * C), SUB * C)].rearrange("p (k c) -> p k c", k=SUB),
                                        t1[:], xf[:], ALU.add).then_inc(z0_made, 1)

        @block.scalar
        def _(act):
            for s in (ct_a, root, nt_a):
                act.sem_inc(s, PRIME)
            act.sem_inc(gated, 2 * CH)
            act.sem_inc(gate_hi, 2 * CH)
            act.wait_ge(const_in, N_CONST)

            def copy_context(t):
                act.wait_ge(ctx_turned, made(t))
                act.wait_ge(projected, made_before(t, 1))
                nc.scalar.activation(ct[:, 0], t_ps[:, 0], ACT.Copy).then_inc(ct_a, 1)

            def deviation(t):
                act.wait_ge(eps, made(t))
                act.wait_ge(inv, made_before(t, 1))
                nc.scalar.activation(sd[:], ve[:], ACT.Sqrt).then_inc(root, 1)

            def copy_rows(t):
                act.wait_ge(rows_turned, made(t))
                act.wait_ge(widened, CH * t + 2 * CH)
                nc.scalar.activation(nt[:, 0], t_ps[:], ACT.Copy, scale=ROW_SCALE).then_inc(nt_a, 1)

            def step(t, left=3):
                if left > 2:
                    copy_context(t + 2)
                act.wait_ge(narrowed, made_before(t, 1))
                for q in range(CH):
                    act.wait_ge(widened, CH * t + q + 1 + 2 * CH)
                    act.wait_ge(gate_lo, CH * t + q - 1 + 2 * CH)
                    for o in range(2):
                        ge = nc.scalar.activation(g_sb[:, q % 2, o], f_ps[:, 2 * (q % 2) + o], ACT.Gelu_apprx_tanh,
                                                  bias=b1[:, 2 * q + o:2 * q + o + 1],
                                                  scale=1.0 / (ROW_SCALE * W_SCALE))
                    ge.then_inc(gated, 1)
                    act.wait_ge(gated, CH * t + q + 1 + 2 * CH)
                    nc.scalar.activation(gt[:, 0, 2 * q:2 * q + 2], g_sb[:, q % 2], ACT.Copy, scale=GATE_SCALE
                                         ).then_inc(gate_hi, 1)
                if left > 1:
                    copy_rows(t + 1)
                if left > 2:
                    deviation(t + 2)

            copy_context(0)
            deviation(0)
            copy_context(1)
            act.wait_ge(weights_in, 32)
            nc.scalar.activation(w1[:, 0], w1_in, ACT.Copy, scale=W_SCALE)
            nc.scalar.activation(w2[:, 0], w2_in, ACT.Copy, scale=W_SCALE).then_inc(weights_hi, 1)
            copy_rows(0)
            deviation(1)
            with act.Fori(0, steps - 2) as t:
                step(t)
            step(steps - 2, 2)
            step(steps - 1, 1)

        @block.vector
        def _(dve):
            for s in (ct_b, t1_made, stats, mean, eps, inv, normed, routed, weighted, nt_b, z1_made):
                dve.sem_inc(s, PRIME)
            dve.sem_inc(gate_lo, 2 * CH)
            dve.wait_ge(const_in, N_CONST)
            def copy_context(t):
                dve.wait_ge(ctx_turned, made(t))
                dve.wait_ge(projected, made_before(t, 1))
                nc.vector.tensor_copy(ct[:, 1], t_ps[:, 1]).then_inc(ct_b, 1)

            def residual(t):
                dve.wait_ge(projected, made(t))
                dve.wait_ge(xb_made, made(t))
                dve.wait_ge(z0_made, made_before(t, 1))
                nc.vector.tensor_tensor(t1[:], p_ps[:], xb[:], ALU.add).then_inc(t1_made, 1)

            def norm(t):
                dve.wait_ge(t1_made, made(t))
                for k in range(SUB):
                    op = nc.vector.bn_stats(st[:, k], t1[:, k])
                op.then_inc(stats, 1)
                dve.wait_ge(stats, made(t))
                nc.vector.tensor_copy(spare[:], st[:, 0, 0:1])
                for k in range(SUB):
                    op = nc.vector.bn_aggr(mv[:, k], st[:, k])
                op.then_inc(mean, 1)
                dve.wait_ge(mean, made(t))
                nc.vector.tensor_scalar(ve[:], mv[:, :, 1], 1e-5, None, ALU.add).then_inc(eps, 1)
                dve.wait_ge(root, made(t))
                nc.vector.reciprocal(rs[:], sd[:]).then_inc(inv, 1)
                dve.wait_ge(inv, made(t))
                dve.wait_ge(rows_turned, made_before(t, 1))
                for k in range(SUB):
                    op = nc.vector.tensor_scalar(xf[:, k], t1[:, k], mv[:, k, 0:1], rs[:, k:k + 1],
                                                 ALU.subtract, ALU.mult)
                op.then_inc(normed, 1)

            def route(t):
                dve.wait_ge(normed, made(t))
                for k in range(SUB):
                    op = nc.vector.tensor_tensor_reduce(out=junk[:, k], in0=xf[:, k], in1=wrb[:], scale=1.0, scalar=0.0,
                                                        op0=ALU.mult, op1=ALU.add, accum_out=w_row[:, k:k + 1])
                op.then_inc(routed, 1)
                dve.wait_ge(routed, made(t))
                nc.vector.tensor_scalar(w_all[:, ds(t * SUB, SUB)], w_row[:], brb[:, 0:1], None, ALU.add
                                        ).then_inc(weighted, 1)

            def copy_rows(t):
                dve.wait_ge(rows_turned, made(t))
                dve.wait_ge(widened, CH * t + 2 * CH)
                dve.wait_ge(nt_a, made(t))
                nc.vector.scalar_tensor_tensor(out=nt[:, 1], in0=t_ps[:], scalar=ROW_SCALE, in1=nt[:, 0],
                                               op0=ALU.mult, op1=ALU.subtract).then_inc(nt_b, 1)

            def step(t, left=3):
                if left > 2:
                    copy_context(t + 2)
                dve.wait_ge(narrowed, made_before(t, 1))
                for q in range(CH):
                    dve.wait_ge(gate_hi, CH * t + q + 1 + 2 * CH)
                    nc.vector.scalar_tensor_tensor(out=gt[:, 1, 2 * q:2 * q + 2], in0=g_sb[:, q % 2],
                                                   scalar=GATE_SCALE, in1=gt[:, 0, 2 * q:2 * q + 2],
                                                   op0=ALU.mult, op1=ALU.subtract).then_inc(gate_lo, 1)
                if left > 2:
                    residual(t + 2)
                if left > 1:
                    copy_rows(t + 1)
                if left > 2:
                    norm(t + 2)
                    route(t + 2)
                dve.wait_ge(narrowed, made(t))
                nc.vector.scalar_tensor_tensor(out=z1[:, ds(t * (SUB * C), SUB * C)].rearrange(
                    "p (k c) -> p k c", k=SUB), in0=p_ps[:], scalar=1.0 / (GATE_SCALE * W_SCALE), in1=over_rows(b2),
                    op0=ALU.mult, op1=ALU.add).then_inc(z1_made, 1)

            copy_context(0)
            residual(0)
            norm(0)
            route(0)
            copy_context(1)
            residual(1)
            copy_rows(0)
            dve.wait_ge(weights_hi, 1)
            nc.vector.scalar_tensor_tensor(out=w1[:, 1], in0=w1_in, scalar=W_SCALE, in1=w1[:, 0],
                                           op0=ALU.mult, op1=ALU.subtract)
            nc.vector.scalar_tensor_tensor(out=w2[:, 1], in0=w2_in, scalar=W_SCALE, in1=w2[:, 0],
                                           op0=ALU.mult, op1=ALU.subtract).then_inc(weights_split, 1)
            norm(1)
            route(1)
            with dve.Fori(0, steps - 2) as t:
                step(t)
            step(steps - 2, 2)
            step(steps - 1, 1)

            done = [0]

            def chained(ins):
                done[0] += 1
                ins.then_inc(step_done, 1)
                dve.wait_ge(step_done, done[0])

            dve.wait_ge(weighted, made(steps - 1))
            wv = w_all[:].rearrange("p (b t) -> p b t", b=batches)
            chained(nc.vector.tensor_scalar(fl[:].bitcast(mybir.dt.int32), wv.bitcast(mybir.dt.int32), 31, -2 ** 31,
                                            ALU.arith_shift_right, ALU.bitwise_or))
            chained(nc.vector.tensor_tensor(ke[:], wv.bitcast(U32), fl[:], ALU.bitwise_xor))
            nc.vector.tensor_scalar(hb[:], ke[:], 16, None, ALU.logical_shift_right)
            chained(nc.vector.tensor_scalar(lb[:], ke[:], 65535, None, ALU.bitwise_and))
            nc.vector.tensor_copy(hi[:], hb[:])
            nc.vector.tensor_copy(lo[:], lb[:])
            nc.vector.memset(want[:, 0], float(keep))
            nc.vector.memset(unit[:], 4.0 ** (DIGITS - 1))
            for j in range(3):
                nc.vector.memset(digit[:, j], j + 1.0)
            nc.vector.memset(cnt[:], 0.0)
            nc.vector.memset(scan, 0.0)
            chained(nc.vector.memset(cur[:], 0.0))

            def count(key, op, least, j=0):
                for b in range(batches):
                    ins = nc.vector.tensor_scalar(passes[j][:, b], key[:, b], least[:, b:b + 1], 0.0, op, ALU.add,
                                                  accum_out=cnt[:, j, b:b + 1])
                return ins

            def largest(key, half, first):
                start = done[0]
                value = cur[:, half].rearrange("p (o b) -> p o b", o=1).to_broadcast([P, 3, batches])
                goal = want[:, half].rearrange("p (o b) -> p o b", o=1).to_broadcast([P, 3, batches])
                with dve.Fori(0, DIGITS) as n:
                    base = start + 4 * n
                    nc.vector.scalar_tensor_tensor(out=cand[:], in0=digit[:], scalar=unit[:, half:half + 1], in1=value,
                                                   op0=ALU.mult, op1=ALU.add).then_inc(step_done, 1)
                    dve.wait_ge(step_done, base + 1)
                    for j in range(3):
                        ins = count(key, ALU.is_ge, cand[:, j], j)
                    ins.then_inc(counted, 1)
                    dve.wait_ge(chosen, first + n + 1)
                    totals = t_ps[:, 0, 0:3 * batches].rearrange("p (j b) -> p j b", j=3)
                    nc.vector.tensor_tensor(inc[:], totals, goal, ALU.is_ge).then_inc(step_done, 1)
                    dve.wait_ge(step_done, base + 2)
                    nc.vector.tensor_reduce(steps_up[:], inc[:].rearrange("p j b -> p b j"), AX_X, ALU.add
                                            ).then_inc(step_done, 1)
                    dve.wait_ge(step_done, base + 3)
                    nc.vector.scalar_tensor_tensor(out=cur[:, half], in0=steps_up[:], scalar=unit[:, half:half + 1],
                                                   in1=cur[:, half], op0=ALU.mult, op1=ALU.add)
                    nc.vector.tensor_scalar(unit[:, half:half + 1], unit[:, half:half + 1], 0.25, None, ALU.mult
                                            ).then_inc(step_done, 1)
                    dve.wait_ge(step_done, base + 4)
                done[0] += 4 * DIGITS

            largest(hi, 0, 0)
            count(hi, ALU.is_gt, cur[:, 0]).then_inc(counted, 1)
            for b in range(batches):
                nc.vector.tensor_scalar(over[:, b], hi[:, b], cur[:, 0, b:b + 1], None, ALU.is_gt)
                op = nc.vector.tensor_scalar(tie[:, b], hi[:, b], cur[:, 0, b:b + 1], None, ALU.is_equal)
            chained(op)
            chained(nc.vector.scalar_tensor_tensor(out=low_key[:], in0=lo[:], scalar=1.0, in1=tie[:],
                                                   op0=ALU.add, op1=ALU.mult))
            chained(nc.vector.tensor_scalar(low_key[:], low_key[:], -1.0, None, ALU.add))
            dve.wait_ge(chosen, DIGITS + 1)
            chained(nc.vector.tensor_tensor(want[:, 1], want[:, 0], t_ps[:, 0, 0:batches], ALU.subtract))
            largest(low_key, 1, DIGITS + 1)
            for b in range(batches):
                nc.vector.tensor_scalar(tie[:, b], low_key[:, b], cur[:, 1, b:b + 1], None, ALU.is_equal)
            count(low_key, ALU.is_gt, cur[:, 1]).then_inc(counted, 1)
            dve.wait_ge(counted, 2 * DIGITS + 2)
            chained(nc.vector.tensor_tensor(over[:], over[:], cmp_[:], ALU.add))
            dve.wait_ge(chosen, 2 * DIGITS + 3)
            chained(nc.vector.tensor_tensor(want[:, 2], want[:, 1], t_ps[:, 0, 0:batches], ALU.subtract))
            tot = p_ps[:, 0, 0:tiles].rearrange("p (b t) -> p b t", b=batches)
            chained(nc.vector.tensor_copy(scan[:, 0, :, pad:], tot))
            side, d = 0, 1
            while d < bt:
                chained(nc.vector.tensor_tensor(scan[:, 1 - side, :, pad:], scan[:, side, :, pad:],
                                                scan[:, side, :, pad - d:pad + bt - d], ALU.add))
                side, d = 1 - side, 2 * d
            rank = low_key
            chained(nc.vector.tensor_tensor(rank[:], scan[:, side, :, pad:], tot, ALU.subtract))
            chained(nc.vector.tensor_tensor(rank[:], rank[:], t_ps[:, 1, 0:tiles].rearrange(
                "p (b t) -> p b t", b=batches), ALU.add))
            for b in range(batches):
                op = nc.vector.tensor_scalar(cmp_[:, b], rank[:, b], want[:, 2, b:b + 1], None, ALU.is_le)
            chained(op)
            chained(nc.vector.tensor_tensor(tie[:], tie[:], cmp_[:], ALU.mult))
            chained(nc.vector.tensor_tensor(over[:], over[:], tie[:], ALU.add))
            chained(nc.vector.tensor_tensor(fac[:].rearrange("p (b t) -> p b t", b=batches), over[:], wv, ALU.mult))
            dve.wait_ge(z0_made, made(steps - 1))
            dve.wait_ge(z1_made, made(steps - 1))
            with dve.Fori(0, steps) as t:
                for k in range(SUB):
                    tile = ds(t * (SUB * C) + k * C, C)
                    op = nc.vector.scalar_tensor_tensor(out=z0[:, tile], in0=z1[:, tile],
                                                        scalar=fac[:, ds(t * SUB + k, 1)], in1=z0[:, tile],
                                                        op0=ALU.mult, op1=ALU.add)
                op.then_inc(out_made, 1)


def flash_phase(nc, seq, heads, q_tab, q_past, k_tab, v_tab, pe_sb, pe_in, diag_masks, identity, ctx_out):
    tiles = seq // P
    blocks = seq // 512
    spi = seq // 1024
    n_tiles = heads * tiles
    dim = 256
    sc = 1.0 / (math.sqrt(dim) * SCORE_SCALE)

    with ExitStack() as ctx:
        def sb(name, shape, dt):
            return ctx.enter_context(nc.sbuf_tensor(name, shape, dt))

        def psum(name, shape):
            return ctx.enter_context(nc.psum_tensor(name, shape, F32))

        sems = []

        def sem(name):
            sems.append(nc.alloc_semaphore(name=name))
            return sems[-1]

        def clear_semaphores():
            nc.clear_and_free_semaphores(sems)
            nc.all_engine_barrier()

        k_sb = sb("k_sb", [P, 2 * 2 * seq], F16)
        v_sb = sb("v_sb", [P, 2 * tiles * P], F16)
        q_sb = sb("q_sb", [P, 2, 9 * P], F16)
        mask_sb = sb("mask_sb", [P, 2 * 256], F32)
        id_sb = sb("fid_sb", [P, P], F32)
        p_sb = sb("p_sb", [P, 2, 1024], F32)
        hi_sb = sb("hi_sb", [P, 2, 8, P], F16)
        lo_sb = sb("lo_sb", [P, 2, 8, P], F16)
        dmask = sb("dmask", [P, 256], F32)
        dsum = sb("dsum", [P, P], F32)
        NS = 2 * spi
        blk_max = sb("blk_max", [P, NS], F32)
        run_max = sb("run_max", [P, NS], F32)
        max_step = sb("max_step", [P, NS], F32)
        neg_max = sb("neg_max", [P, NS], F32)
        corr = sb("corr", [P, NS], F32)
        row_sum = sb("row_sum", [P, NS], F32)
        tot = sb("tot", [P, NS], F32)
        o_acc = sb("o_acc", [P, NS, P], F32)
        o_sum = sb("o_sum", [P, 64], F32)
        r_tot = sb("r_tot", [P, 1], F32)
        o_out = sb("o_out", [P, 2, 64], F32)

        s_ps = psum("s_ps", [P, 2, 1024])
        t_ps = psum("t_ps", [P, 8, P])
        o_ps = psum("o_ps", [P, 512])
        d_ps = psum("d_ps", [P, 512])

        const_in = sem("f_const_in")
        q_in = [sem(f"f_q_in{p}") for p in range(2)]
        k_in, v_in = sem("f_k_in"), sem("f_v_in")
        scored = sem("f_scored")
        exped = sem("f_exped")
        turned = sem("f_turned")
        hi_made = sem("f_hi_made")
        lo_made = sem("f_lo_made")
        pv_made = sem("f_pv_made")
        maxed = sem("f_maxed")
        o_added = sem("f_o_added")
        diag_read = sem("f_diag_read")
        ctx_made = sem("f_ctx_made")
        stored = sem("f_stored")
        out_free = sem("f_out_free")
        dve_step = sem("f_dve_step")
        fin_step = sem("f_fin_step")

        def head_of(g):
            return g // tiles

        def over_tiles(eng, query_tile):
            with eng.Fori(0, n_tiles // 4 - 1) as q4:
                for r in range(4):
                    query_tile(4 * q4 + r, r)
            for r in range(4):
                query_tile(n_tiles - 4 + r, r, last=r == 3)

        ctx.callback(clear_semaphores)
        block = ctx.enter_context(nc.Block())

        @block.sync
        def _(sp):
            sp.dma_start(mask_sb[:], diag_masks).then_inc(const_in, 16)
            sp.dma_start(id_sb[:], identity).then_inc(const_in, 16)

            def load_kv(h):
                par = h % 2
                sp.dma_start(k_sb[:, ds(par * (2 * seq), 2 * seq)],
                             k_tab[ds(h, 1)].rearrange("o p a s -> p (o a s)")).then_inc(k_in, 16)
                sp.dma_start(v_sb[:, ds(par * (tiles * P), tiles * P)],
                             v_tab[ds(h, 1)].rearrange("o p t d -> p (o t d)")).then_inc(v_in, 16)

            def load_q(g, par, first=False):
                sp.wait_ge(scored, spi * g + PRIME)
                h, i = g // tiles, g % tiles
                q = q_sb[:, par, :].rearrange("p (n c) -> p n c", c=P)
                src = q_tab[ds(h, 1)].rearrange("o p n c -> p (o n) c")
                if first:
                    sp.dma_start(q[:, 0:4, 1:P], src[:, 0:4, 2:P + 1]).then_inc(q_in[par], 16)
                    sp.dma_start(q[:, 0:4, 0:1], q_past[ds(h, 1)].rearrange("o p n c -> p (o n) c"),
                                 allow_slow_non_contiguous=True).then_inc(q_in[par], 16)
                    sp.dma_start(q[:, 4:9, :], src[:, :, 0:P]).then_inc(q_in[par], 16)
                else:
                    sp.dma_start(q[:, 0:4, :], src[:, 0:4, ds(i * P + 1, P)]).then_inc(q_in[par], 16)
                    sp.dma_start(q[:, 4:8, :], src[:, 0:4, ds(i * P, P)]).then_inc(q_in[par], 16)
                    sp.dma_start(q[:, 8:9, :], src[:, 4:5, ds(i * P, P)]).then_inc(q_in[par], 16)

            load_q(0, 0, first=True)
            load_q(1, 1)
            load_kv(0)
            with sp.Fori(0, heads - 1) as h:
                g0 = h * tiles
                load_q(g0 + 2, 0)
                load_q(g0 + 3, 1)
                sp.wait_ge(pv_made, spi * g0 + PRIME)
                sp.wait_ge(k_in, 16 * (h + 1))
                sp.wait_ge(v_in, 16 * (h + 1))
                load_kv(h + 1)
                with sp.Fori(2, tiles // 2) as i2:
                    load_q(g0 + 2 * i2, 0)
                    load_q(g0 + 2 * i2 + 1, 1)
                load_q(g0 + tiles, 0, first=True)
                load_q(g0 + tiles + 1, 1)
            with sp.Fori(1, tiles // 2) as i2:
                load_q((heads - 1) * tiles + 2 * i2, 0)
                load_q((heads - 1) * tiles + 2 * i2 + 1, 1)

        @block.tensor
        def _(pe):
            pe.sem_inc(scored, PRIME + spi)
            pe.sem_inc(turned, PRIME)
            pe.sem_inc(pv_made, PRIME)
            pe.wait_ge(const_in, 32)
            pe.wait_ge(pe_in, 64)

            def scores(g, r, s, half):
                h = head_of(g)
                par = r % 2
                i4 = (g % tiles) // 4
                kb = (h % 2) * (2 * seq)
                j = 2 * s + half
                out = s_ps[:, s % 2, half * 512:(half + 1) * 512]
                q = q_sb[:, par, :]
                content = q[:, 8 * P:9 * P]

                def part(sel, n):
                    if isinstance(sel, int):
                        return q[:, sel * 512 + n * P:sel * 512 + (n + 1) * P]
                    return q_sb[:, par, ds(sel * 512 + n * P, P)]

                def position(to, sel, first, n_keys, start=False):
                    for a in range(2):
                        for n, b in ((0, 0), (1, 0), (0, 1)):
                            mm = nc.tensor.matmul(to, part(sel, 2 * a + n), pe_sb[:, a, b, ds(first, n_keys)],
                                                  start=start and a + n + b == 0, stop=a == 1 and b == 1,
                                                  skip_group_check=True)
                    return mm

                if s == 0 and half == 0:
                    pe.wait_ge(q_in[par], 48 * (g // 2 + 1))
                    pe.wait_ge(k_in, 16 * (h + 1))
                    col = i4 * 512
                    for a in range(2):
                        nc.tensor.matmul(out, content, k_sb[:, ds(kb + a * seq + col, 512)],
                                         start=(a == 0), stop=(a == 1), skip_group_check=True)
                    if r < 3:
                        position(out[:, (r + 1) * P:512], 0, col + (r + 1) * P, (3 - r) * P)
                    if r > 0:
                        position(out[:, 0:r * P], 1, col + seq, r * P)
                    pe.wait_ge(diag_read, made_before(g, 1))
                    for sel in (1, 0):
                        position(d_ps[:, (1 - sel) * P:(2 - sel) * P], sel, col + r * P + sel * seq, P, start=True)
                    return None
                col = ((i4 + j) % blocks) * 512
                past = (i4 + j) >= blocks
                for a in range(2):
                    nc.tensor.matmul(out, content, k_sb[:, ds(kb + a * seq + col, 512)],
                                     start=(a == 0), stop=False, skip_group_check=True)
                mm = position(out, past, (i4 + j) * 512, 512)
                return mm

            def turn(n, s):
                pe.wait_ge(exped, made(n))
                pe.wait_ge(lo_made, made_before(n, 1))
                for k in range(8):
                    tr = nc.tensor.transpose(t_ps[:, k, :], p_sb[:, s % 2, k * P:(k + 1) * P], id_sb[:])
                tr.then_inc(turned, 1)

            def weigh(g, n, s):
                h = head_of(g)
                i4 = (g % tiles) // 4
                vb = (h % 2) * (tiles * P)
                if s == 0:
                    pe.wait_ge(v_in, 16 * (h + 1))
                pe.wait_ge(hi_made, made(n))
                pe.wait_ge(o_added, made_before(n, 1))

                def tile_of(k):
                    return ((i4 + 2 * s + k // 4) % blocks) * 4 + k % 4

                for k in range(8):
                    nc.tensor.matmul(o_ps[:, 0:P], hi_sb[:, s % 2, k, :], v_sb[:, ds(vb + tile_of(k) * P, P)],
                                     start=(k == 0), stop=False, skip_group_check=True)
                pe.wait_ge(lo_made, made(n))
                for k in range(8):
                    mm = nc.tensor.matmul(o_ps[:, 0:64], lo_sb[:, s % 2, k, :], v_sb[:, ds(vb + tile_of(k) * P, 64)],
                                          start=False, stop=(k == 7), skip_group_check=True)
                mm.then_inc(pv_made, 1)

            def query_tile(g, r, last=False):
                for s in range(spi):
                    n = spi * g + s
                    turn(n, s)
                    ahead, s2 = (s + 2) // spi, (s + 2) % spi
                    if not (last and ahead):
                        scores(g + ahead, (r + ahead) % 4, s2, 0)
                        scores(g + ahead, (r + ahead) % 4, s2, 1).then_inc(scored, 1)
                    weigh(g, n, s)

            for s in range(2):
                scores(s // spi, s // spi, s % spi, 0)
                scores(s // spi, s // spi, s % spi, 1).then_inc(scored, 1)
            over_tiles(pe, query_tile)

        @block.vector
        def _(dve):
            for s_ in (lo_made, maxed, o_added, diag_read, ctx_made):
                dve.sem_inc(s_, PRIME)
            dve.wait_ge(const_in, 32)

            CHAIN = 3 + 2 * (spi - 1)

            def row_max(g, r, s):
                par = r % 2
                n = spi * g + s
                x = par * spi + s
                base = CHAIN * g
                dve.wait_ge(scored, n + 1 + PRIME + spi)
                if s == 0:
                    variant = (g % tiles) < 1
                    nc.vector.tensor_tensor(dmask[:], d_ps[:, 0:256], mask_sb[:, ds(variant * 256, 256)],
                                            ALU.mult).then_inc(diag_read, 1)
                    dve.wait_ge(diag_read, made(g))
                    nc.vector.tensor_tensor(dsum[:], dmask[:, 0:P], dmask[:, P:2 * P],
                                            ALU.add).then_inc(dve_step, 1)
                    dve.wait_ge(dve_step, base + 1)
                    nc.vector.tensor_tensor(s_ps[:, 0, r * P:(r + 1) * P], s_ps[:, 0, r * P:(r + 1) * P], dsum[:],
                                            ALU.add).then_inc(dve_step, 1)
                    dve.wait_ge(dve_step, base + 2)
                    nc.vector.tensor_reduce(run_max[:, x:x + 1], s_ps[:, s % 2, :], AX_X, ALU.max).then_inc(dve_step, 1)
                    dve.wait_ge(dve_step, base + 3)
                else:
                    nc.vector.tensor_reduce(blk_max[:, x:x + 1], s_ps[:, s % 2, :], AX_X, ALU.max).then_inc(dve_step, 1)
                    dve.wait_ge(dve_step, base + 3 + 2 * s - 1)
                    nc.vector.tensor_tensor(run_max[:, x:x + 1], blk_max[:, x:x + 1], run_max[:, x - 1:x],
                                            ALU.max).then_inc(dve_step, 1)
                    dve.wait_ge(dve_step, base + 3 + 2 * s)
                if s:
                    nc.vector.tensor_tensor(max_step[:, x:x + 1], run_max[:, x - 1:x], run_max[:, x:x + 1],
                                            ALU.subtract)
                nc.vector.tensor_scalar(neg_max[:, x:x + 1], run_max[:, x:x + 1], -sc, math.log(P_SCALE),
                                        ALU.mult, ALU.add).then_inc(maxed, 1)

            def low_part(n, s):
                dve.wait_ge(hi_made, made(n))
                dve.wait_ge(pv_made, made_before(n, 2))
                nc.vector.tensor_tensor(lo_sb[:, s % 2, :, :], t_ps[:], hi_sb[:, s % 2, :, :],
                                        ALU.subtract).then_inc(lo_made, 1)

            def add_output(g, par, s):
                n = spi * g + s
                x = par * spi + s
                dve.wait_ge(exped, made(n))
                dve.wait_ge(pv_made, made(n))
                if s:
                    dve.wait_ge(o_added, made_before(n, 1))
                    nc.vector.scalar_tensor_tensor(out=tot[:, x:x + 1], in0=tot[:, x - 1:x], scalar=corr[:, x:x + 1],
                                                   in1=row_sum[:, x:x + 1], op0=ALU.mult, op1=ALU.add)
                    nc.vector.scalar_tensor_tensor(out=o_acc[:, x, :], in0=o_acc[:, x - 1, :], scalar=corr[:, x:x + 1],
                                                   in1=o_ps[:, 0:P], op0=ALU.mult, op1=ALU.add).then_inc(o_added, 1)
                else:
                    nc.vector.tensor_copy(tot[:, x:x + 1], row_sum[:, x:x + 1])
                    nc.vector.tensor_copy(o_acc[:, x, :], o_ps[:, 0:P]).then_inc(o_added, 1)

            def finish(g, par):
                x = par * spi + spi - 1
                dve.wait_ge(o_added, made(spi * g + spi - 1))
                nc.vector.reciprocal(r_tot[:], tot[:, x:x + 1]).then_inc(fin_step, 1)
                nc.vector.tensor_tensor(o_sum[:], o_acc[:, x, 0:64], o_acc[:, x, 64:128], ALU.add).then_inc(fin_step, 1)
                dve.wait_ge(fin_step, 2 * g + 2)
                dve.wait_ge(out_free, made_before(g, 2))
                nc.vector.tensor_scalar(o_out[:, par, :], o_sum[:], r_tot[:, 0:1], 1.0 / V_SCALE,
                                        ALU.mult, ALU.mult).then_inc(ctx_made, 1)

            def query_tile(g, r, last=False):
                par = r % 2
                for s in range(spi):
                    ahead, s2 = (s + 1) // spi, (s + 1) % spi
                    if not (last and ahead):
                        row_max(g + ahead, (r + ahead) % 4, s2)
                    low_part(spi * g + s, s)
                    add_output(g, par, s)
                finish(g, par)

            row_max(0, 0, 0)
            over_tiles(dve, query_tile)

        @block.scalar
        def _(act):
            act.sem_inc(exped, PRIME)
            act.sem_inc(hi_made, PRIME)

            def exponentials(g, par, s):
                n = spi * g + s
                x = par * spi + s
                act.wait_ge(maxed, made(n))
                act.wait_ge(turned, made_before(n, 2))
                if s:
                    nc.scalar.activation(corr[:, x:x + 1], max_step[:, x:x + 1], ACT.Exp, scale=sc)
                nc.scalar.activation(p_sb[:, s % 2, :], s_ps[:, s % 2, :], ACT.Exp, bias=neg_max[:, x:x + 1],
                                     scale=sc, accum_out=row_sum[:, x:x + 1]).then_inc(exped, 1)

            def high_part(n, s):
                act.wait_ge(turned, made(n))
                act.wait_ge(pv_made, made_before(n, 2))
                nc.scalar.activation(hi_sb[:, s % 2, :, :], t_ps[:], ACT.Copy).then_inc(hi_made, 1)

            def query_tile(g, r, last=False):
                for s in range(spi):
                    high_part(spi * g + s, s)
                    ahead, s2 = (s + 1) // spi, (s + 1) % spi
                    if not (last and ahead):
                        exponentials(g + ahead, (r + ahead) % 2, s2)

            exponentials(0, 0, 0)
            over_tiles(act, query_tile)

        @block.gpsimd
        def _(pool):
            pool.sem_inc(out_free, PRIME)
            with pool.Fori(0, n_tiles // 2) as g2:
                for par in range(2):
                    g = 2 * g2 + par
                    pool.wait_ge(ctx_made, made(g))
                    pool.dma_start(ctx_out(g), o_out[:, par, :]).then_inc(stored, 16)
                    pool.wait_ge(stored, 16 * (g + 1))
                    pool.sem_inc(out_free, 1)


def two_layers(nc, x, norm1_w, norm2_w, w_qkv, w_proj, b_proj, l0_ff1_w, l0_ff1_b, l0_ff2_w, l0_ff2_b, gamma, beta,
               wq, bq, wk, bk, wv, bv, wpos_t, u_bias, v_bias, w_out, b_out, wr, br, ff1_w, ff1_b, ff2_w, ff2_b,
               rope, win_mask, turn_tab, pe_tab, diag_mask, identity, prefix, out):
    batches, height, width, c = x.shape
    seq = height * width
    n = batches * seq
    heads = batches * NH
    tiles = seq // P

    def scratch(name, shape, dt=F32):
        return nc.dram_tensor(name, shape, dt).ap()

    x = x.rearrange("b h w c -> (b h w) c")
    out = out.rearrange("b h w c -> (b h w) c")
    qk_t = scratch("qk_t", (2, 2 * c, n), F16)
    v_rows = scratch("v_rows", (n, 2 * c), F16)
    ctx0 = scratch("ctx0", (n, c))
    x1 = scratch("x1", (n, c))
    q_tab = scratch("q_tab", (heads, P, 5, 1 + seq), F16)
    q_past = scratch("q_past", (heads, P, 4, 1), F16)
    k_tab = scratch("k_tab", (heads, P, 2, seq), F16)
    v_tab = scratch("v_tab", (heads, P, tiles, P), F16)
    ctx1 = scratch("ctx1", (batches, 1 + seq, c))
    ctx1_rows = ctx1.rearrange("b r c -> (b r) c")

    def ctx_out(g):
        b, h, i = g // (NH * tiles), (g // tiles) % NH, g % tiles
        return ctx1_rows[ds(b * (seq + 1) + i * P, P), ds(h * HD, HD)]

    qkv_phase(nc, n, seq, x, norm1_w, w_qkv, rope, identity, qk_t, v_rows)
    window_phase(nc, batches, height, width, qk_t, v_rows, win_mask, identity, ctx0)
    layer0_mlp_phase(nc, n, x, ctx0, w_proj, b_proj, norm2_w, l0_ff1_w, l0_ff1_b, l0_ff2_w, l0_ff2_b, identity, x1)
    with nc.sbuf_tensor("pe_sb", [P, 2, 2, 2 * seq], F16) as pe_sb, nc.semaphore("pe_in") as pe_in:
        tables_phase(nc, batches, seq, x1, gamma, beta, wq, bq, wk, bk, wv, bv, wpos_t, u_bias, v_bias, turn_tab,
                     identity, q_tab, q_past, k_tab, v_tab, pe_sb, pe_tab, pe_in)
        flash_phase(nc, seq, heads, q_tab, q_past, k_tab, v_tab, pe_sb, pe_in, diag_mask, identity, ctx_out)
    ffn_phase(nc, batches, seq, x1, ctx1, w_out, b_out, wr, br, ff1_w, ff1_b, ff2_w, ff2_b, identity, prefix, out)


def rope_table(height, width, pairs):
    q = pairs // 2
    inv = (1.0 / 10000.0 ** (np.arange(q, dtype=np.float32) / q)).astype(np.float32)
    by_row = np.arange(height, dtype=np.float32)[:, None] * inv
    by_col = np.arange(width, dtype=np.float32)[:, None] * inv
    angle = np.concatenate([np.broadcast_to(by_row[:, None], (height, width, q)),
                            np.broadcast_to(by_col[None], (height, width, q))], -1).reshape(height * width, pairs)
    return np.stack([np.cos(angle), np.sin(angle)]).astype(np.float32)


def window_masks(height, width, span=8, ks=7):
    mask = np.full((3, 2, width, span, width), -1e30, np.float32)
    left = np.clip(np.arange(width) - ks // 2, 0, width - ks)
    for kind, (y, first) in enumerate(((0, 0), (2, 4 - ks // 2), (height // 2 - 1, height - span))):
        for a in range(2):
            top = min(max(2 * y + a - ks // 2, 0), height - ks) - first
            for c in range(width):
                mask[kind, a, c, top:top + ks, left[c]:left[c] + ks] = 0
    return np.ascontiguousarray(mask.reshape(3, P, span * width).transpose(1, 0, 2).reshape(P, -1))


def frequencies(dim):
    return np.exp(np.arange(0, dim, 2, dtype=np.float32) * np.float32(-np.log(10000.0) / dim)).astype(np.float64)


def turn_table(seq, dim):
    angle = frequencies(dim)[:, None] * (np.arange(seq) + 1)[None]
    return (np.stack([np.cos(angle), np.sin(angle)], 1) * B_SCALE).astype(np.float32)


def pe_table(seq, dim):
    angle = frequencies(dim)[:, None] * np.arange(2 * seq)[None]
    value = np.stack([np.sin(angle), np.cos(angle)], 1) * PE_SCALE
    high = value.astype(np.float16)
    return np.stack([high, (value - high).astype(np.float16)], 2)


def diagonal_masks():
    r, c = np.arange(P)[:, None], np.arange(P)[None]
    below, above = (c < r).astype(np.float32), (c > r).astype(np.float32)
    above_first = above.copy()
    above_first[0, 0] = 1
    return np.ascontiguousarray(np.concatenate([below, above, below, above_first], 1))


_INS = ["x", "L0_conv_norm1_w", "L0_conv_norm2_w", "L0_conv_w_qkv", "L0_conv_w_proj", "L0_conv_b_proj",
        "L0_conv_ff1_w", "L0_conv_ff1_b", "L0_conv_ff2_w", "L0_conv_ff2_b", "L1_attn_ln_gamma", "L1_attn_ln_beta",
        "L1_attn_Wq", "L1_attn_bq", "L1_attn_Wk", "L1_attn_bk", "L1_attn_Wv", "L1_attn_bv", "L1_attn_Wpos",
        "L1_attn_u_bias", "L1_attn_v_bias", "L1_attn_Wout", "L1_attn_bout", "L1_ffn_wr", "L1_ffn_br", "L1_ffn_w1",
        "L1_ffn_b1", "L1_ffn_w2", "L1_ffn_b2"]


def kernel(**inputs):
    import numpy as _np
    import concourse.bacc as _bacc
    from concourse import mybir as _mybir
    from concourse.bass_utils import run_bass_kernel_spmd as _run

    data = {name: _np.asarray(inputs[name]) for name in _INS}
    height, width, dim = data["x"].shape[1:]
    data["L1_attn_Wpos"] = data["L1_attn_Wpos"].reshape(dim // 2, 2, NH, HD).transpose(3, 2, 1, 0)
    data["L1_ffn_wr"] = data["L1_ffn_wr"].reshape(-1)
    tri = _np.triu(_np.ones((P, P), _np.float32))
    data.update(rope=rope_table(height, width, dim // 2), win_mask=window_masks(height, width),
                turn_tab=turn_table(height * width, dim), pe_tab=pe_table(height * width, dim),
                diag_mask=diagonal_masks(), identity=_np.eye(P, dtype=_np.float32),
                prefix=_np.concatenate([tri, _np.ones((P, P), _np.float32)], 1))

    nc = _bacc.Bacc("TRN2", target_bir_lowering=False, num_devices=1)
    arrays, args = {}, []
    for name, a in data.items():
        a = _np.ascontiguousarray(a)
        arrays[f"in_{name}_dram"] = a
        args.append(nc.dram_tensor(f"in_{name}_dram", a.shape, _mybir.dt.from_np(a.dtype), kind="ExternalInput").ap())
    args.append(nc.dram_tensor("out_0_dram", data["x"].shape, _mybir.dt.float32, kind="ExternalOutput").ap())
    two_layers(nc, *args)
    r = _run(nc, [arrays], core_ids=[0])
    return r.results[0]["out_0_dram"]
```
